# Optimizing a Trainium2 kernel written in Bass

```python
import numpy as np
import jax
import jax.numpy as jnp

def _softmax(x, axis=-1):
    return jax.nn.softmax(x, axis=axis)

def _gelu(x):
    return jax.nn.gelu(x, approximate=True)

def _silu(x):
    return jax.nn.silu(x)

def _sigmoid(x):
    return jax.nn.sigmoid(x)

def _layernorm(x, axis=-1, eps=1e-05):
    m = jnp.mean(x, axis=axis, keepdims=True)
    v = jnp.var(x, axis=axis, keepdims=True)
    return (x - m) / jnp.sqrt(v + eps)

def _scatter_add(tgt, idx, src, axis=0):
    return tgt.at[idx].add(src)

def _segment_sum(src, seg, n):
    return jax.ops.segment_sum(src, seg, n)
kernel_name = 'mk_gnn_preln_d4_gnn_r8_485110'

def setup_inputs(seed: int=0):
    np.random.seed(seed)
    _w = jnp.asarray

    def _rec_inputs():
        import jax
        import jax.numpy as jnp
        _gk = jax.random.key(seed)
        x = -8.776e-05 + 1 * jax.random.normal(jax.random.fold_in(_gk, 1), (6250, 128), jnp.float32)
        src = jax.random.randint(jax.random.fold_in(_gk, 2), (100000,), 0, 6250, jnp.int32)
        dst = jnp.minimum((6250 * jax.random.uniform(jax.random.fold_in(_gk, 3), (100000,)) ** 2.0).astype(jnp.int32), 49999)
        _o = jnp.argsort(dst, stable=True)
        src = src[_o]
        dst = dst[_o]
        return (x, src, dst)
    x, src, dst = _rec_inputs()

    def _L0_gnn_setup():
        import jax, jax.numpy as jnp
        import numpy as np
        N = 5000
        E = 80000
        IN = 128
        H = 8
        F = 16
        NEG_SLOPE = 0.2
        BN_EPS = 1e-05
        SOFTMAX_EPS = 1e-16

        def _gat_layer(x, src, dst, W, att_src, att_dst, bias, bn_gamma, bn_beta):
            n = x.shape[0]
            xp = (x @ W).reshape(n, H, F)
            a_s = jnp.einsum('nhf,hf->nh', xp, att_src)
            a_d = jnp.einsum('nhf,hf->nh', xp, att_dst)
            e = jax.nn.leaky_relu(a_s[src] + a_d[dst], NEG_SLOPE)
            m = jax.ops.segment_max(e, dst, num_segments=n)
            m = jnp.where(jnp.isfinite(m), m, 0.0)
            p = jnp.exp(e - m[dst])
            s = jax.ops.segment_sum(p, dst, num_segments=n)
            alpha = p / (s[dst] + SOFTMAX_EPS)
            msg = alpha[:, :, None] * xp[src]
            out = jax.ops.segment_sum(msg, dst, num_segments=n)
            h = out.reshape(n, H * F) + bias
            mean = h.mean(axis=0)
            var = h.var(axis=0)
            h = (h - mean) * jax.lax.rsqrt(var + BN_EPS) * bn_gamma + bn_beta
            h = jax.nn.relu(h)
            return h + x
        key = jax.random.key(seed)
        ks = jax.random.split(key, 7)
        x = jax.random.normal(ks[0], (N, IN), dtype=jnp.float32)
        edge_index = jax.random.randint(ks[1], (2, E), 0, N, dtype=jnp.int32)
        W = jax.random.normal(ks[2], (IN, H * F), dtype=jnp.float32) * (1.0 / np.sqrt(IN))
        att_src = jax.random.normal(ks[3], (H, F), dtype=jnp.float32) * (1.0 / np.sqrt(F))
        att_dst = jax.random.normal(ks[4], (H, F), dtype=jnp.float32) * (1.0 / np.sqrt(F))
        bias = jnp.zeros((H * F,), dtype=jnp.float32)
        bn_gamma = jnp.ones((H * F,), dtype=jnp.float32)
        bn_beta = jnp.zeros((H * F,), dtype=jnp.float32)
        return {'x': x, 'edge_index': edge_index, 'W': W, 'att_src': att_src, 'att_dst': att_dst, 'bias': bias, 'bn_gamma': bn_gamma, 'bn_beta': bn_beta}
    _L0_gnn_all = _L0_gnn_setup()
    _L0_gnn_in = {k: v for k, v in _L0_gnn_all.items() if k in ('W', 'att_src', 'att_dst', 'bias', 'bn_gamma', 'bn_beta')}
    del _L0_gnn_all

    def _L1_gnn_setup():
        import jax, jax.numpy as jnp
        import numpy as np
        N_NODES = 12500
        N_EDGES = 200000
        D = 128
        BN_EPS = 1e-05
        key = jax.random.key(seed)
        k1, k2, k3, k4, k5 = jax.random.split(key, 5)
        feature = jax.random.normal(k1, (N_NODES, D), dtype=jnp.float32)
        src = jax.random.randint(k2, (N_EDGES,), 0, N_NODES, dtype=jnp.int32)
        dst = jax.random.randint(k3, (N_EDGES,), 0, N_NODES, dtype=jnp.int32)
        lim = 1.0 / np.sqrt(D)
        W = jax.random.uniform(k4, (D, D), dtype=jnp.float32, minval=-lim, maxval=lim)
        b = jax.random.uniform(k5, (D,), dtype=jnp.float32, minval=-lim, maxval=lim)
        gamma = jnp.ones((D,), dtype=jnp.float32)
        beta = jnp.zeros((D,), dtype=jnp.float32)
        return {'feature': feature, 'W': W, 'b': b, 'gamma': gamma, 'beta': beta, 'src': src, 'dst': dst}
    _L1_gnn_all = _L1_gnn_setup()
    _L1_gnn_in = {k: v for k, v in _L1_gnn_all.items() if k in ('W', 'b', 'gamma', 'beta')}
    del _L1_gnn_all

    def _L2_gnn_setup():
        import jax, jax.numpy as jnp
        import numpy as np
        N = 6250
        E = 100000
        F = 128
        AVG_LOG = float(np.log(17.0))
        BN_EPS = 1e-05
        STD_EPS = 1e-05
        key = jax.random.key(seed)
        ks = jax.random.split(key, 10)
        h = jax.random.normal(ks[0], (N, F), dtype=jnp.float32)
        edge_index = jax.random.randint(ks[1], (2, E), 0, N, dtype=jnp.int64)

        def lin_w(k, fan_in, fan_out):
            return jax.random.normal(k, (fan_in, fan_out), dtype=jnp.float32) / np.sqrt(fan_in)
        return {'h': h, 'edge_index': edge_index, 'W_pre': lin_w(ks[2], 2 * F, F), 'b_pre': jnp.zeros((F,), jnp.float32), 'W_post': lin_w(ks[3], 13 * F, F), 'b_post': jnp.zeros((F,), jnp.float32), 'W_lin': lin_w(ks[4], F, F), 'b_lin': jnp.zeros((F,), jnp.float32), 'gamma': jnp.ones((F,), jnp.float32), 'beta': jnp.zeros((F,), jnp.float32)}
    _L2_gnn_all = _L2_gnn_setup()
    _L2_gnn_in = {k: v for k, v in _L2_gnn_all.items() if k in ('W_pre', 'b_pre', 'W_post', 'b_post', 'W_lin', 'b_lin', 'gamma', 'beta')}
    del _L2_gnn_all

    def _L3_gnn_setup():
        import jax, jax.numpy as jnp
        import numpy as np
        N_NODES = 12500
        N_EDGES = 200000
        DIM = 128
        NEG_SLOPE = 0.2
        key = jax.random.key(seed)
        ks = jax.random.split(key, 8)
        x = jax.random.normal(ks[0], (N_NODES, DIM), dtype=jnp.float32)
        edge_index = jax.random.randint(ks[1], (2, N_EDGES), 0, N_NODES, dtype=jnp.int64)
        scale = 1.0 / np.sqrt(DIM)
        W_l = jax.random.normal(ks[2], (DIM, DIM), dtype=jnp.float32) * scale
        b_l = jax.random.normal(ks[3], (DIM,), dtype=jnp.float32) * 0.02
        W_r = jax.random.normal(ks[4], (DIM, DIM), dtype=jnp.float32) * scale
        b_r = jax.random.normal(ks[5], (DIM,), dtype=jnp.float32) * 0.02
        att = jax.random.normal(ks[6], (DIM,), dtype=jnp.float32) * scale
        bias = jax.random.normal(ks[7], (DIM,), dtype=jnp.float32) * 0.02
        return {'x': x, 'edge_index': edge_index, 'W_l': W_l, 'b_l': b_l, 'W_r': W_r, 'b_r': b_r, 'att': att, 'bias': bias}
    _L3_gnn_all = _L3_gnn_setup()
    _L3_gnn_in = {k: v for k, v in _L3_gnn_all.items() if k in ('W_l', 'b_l', 'W_r', 'b_r', 'att', 'bias')}
    del _L3_gnn_all
    return {'x': x, 'src': src, 'dst': dst, 'L0_gnn_W': _L0_gnn_in['W'], 'L0_gnn_att_src': _L0_gnn_in['att_src'], 'L0_gnn_att_dst': _L0_gnn_in['att_dst'], 'L0_gnn_bias': _L0_gnn_in['bias'], 'L0_gnn_bn_gamma': _L0_gnn_in['bn_gamma'], 'L0_gnn_bn_beta': _L0_gnn_in['bn_beta'], 'L1_gnn_W': _L1_gnn_in['W'], 'L1_gnn_b': _L1_gnn_in['b'], 'L1_gnn_gamma': _L1_gnn_in['gamma'], 'L1_gnn_beta': _L1_gnn_in['beta'], 'L2_gnn_W_pre': _L2_gnn_in['W_pre'], 'L2_gnn_b_pre': _L2_gnn_in['b_pre'], 'L2_gnn_W_post': _L2_gnn_in['W_post'], 'L2_gnn_b_post': _L2_gnn_in['b_post'], 'L2_gnn_W_lin': _L2_gnn_in['W_lin'], 'L2_gnn_b_lin': _L2_gnn_in['b_lin'], 'L2_gnn_gamma': _L2_gnn_in['gamma'], 'L2_gnn_beta': _L2_gnn_in['beta'], 'L3_gnn_W_l': _L3_gnn_in['W_l'], 'L3_gnn_b_l': _L3_gnn_in['b_l'], 'L3_gnn_W_r': _L3_gnn_in['W_r'], 'L3_gnn_b_r': _L3_gnn_in['b_r'], 'L3_gnn_att': _L3_gnn_in['att'], 'L3_gnn_bias': _L3_gnn_in['bias']}

def reference(x, src, dst, L0_gnn_W, L0_gnn_att_src, L0_gnn_att_dst, L0_gnn_bias, L0_gnn_bn_gamma, L0_gnn_bn_beta, L1_gnn_W, L1_gnn_b, L1_gnn_gamma, L1_gnn_beta, L2_gnn_W_pre, L2_gnn_b_pre, L2_gnn_W_post, L2_gnn_b_post, L2_gnn_W_lin, L2_gnn_b_lin, L2_gnn_gamma, L2_gnn_beta, L3_gnn_W_l, L3_gnn_b_l, L3_gnn_W_r, L3_gnn_b_r, L3_gnn_att, L3_gnn_bias):
    import jax
    import jax.numpy as jnp

    def _L0_gnn_ref(x, edge_index, W, att_src, att_dst, bias, bn_gamma, bn_beta):
        import jax, jax.numpy as jnp
        import numpy as np
        N = 5000
        E = 80000
        IN = 128
        H = 8
        F = 16
        NEG_SLOPE = 0.2
        BN_EPS = 1e-05
        SOFTMAX_EPS = 1e-16

        def _gat_layer(x, src, dst, W, att_src, att_dst, bias, bn_gamma, bn_beta):
            n = x.shape[0]
            xp = (x @ W).reshape(n, H, F)
            a_s = jnp.einsum('nhf,hf->nh', xp, att_src)
            a_d = jnp.einsum('nhf,hf->nh', xp, att_dst)
            e = jax.nn.leaky_relu(a_s[src] + a_d[dst], NEG_SLOPE)
            m = jax.ops.segment_max(e, dst, num_segments=n)
            m = jnp.where(jnp.isfinite(m), m, 0.0)
            p = jnp.exp(e - m[dst])
            s = jax.ops.segment_sum(p, dst, num_segments=n)
            alpha = p / (s[dst] + SOFTMAX_EPS)
            msg = alpha[:, :, None] * xp[src]
            out = jax.ops.segment_sum(msg, dst, num_segments=n)
            h = out.reshape(n, H * F) + bias
            mean = h.mean(axis=0)
            var = h.var(axis=0)
            h = (h - mean) * jax.lax.rsqrt(var + BN_EPS) * bn_gamma + bn_beta
            h = jax.nn.relu(h)
            return h + x
        n = x.shape[0]
        loops = jnp.arange(n, dtype=edge_index.dtype)
        src = jnp.concatenate([edge_index[0], loops])
        dst = jnp.concatenate([edge_index[1], loops])
        return _gat_layer(x, src, dst, W, att_src, att_dst, bias, bn_gamma, bn_beta)

    def _L1_gnn_ref(feature, W, b, gamma, beta, src, dst):
        import jax, jax.numpy as jnp
        import numpy as np
        N_NODES = 12500
        N_EDGES = 200000
        D = 128
        BN_EPS = 1e-05
        N = feature.shape[0]
        ones_e = jnp.ones(src.shape[0], dtype=feature.dtype)
        deg_out = jnp.maximum(jax.ops.segment_sum(ones_e, src, num_segments=N), 1.0)
        deg_in = jnp.maximum(jax.ops.segment_sum(ones_e, dst, num_segments=N), 1.0)
        x = feature * jax.lax.rsqrt(deg_out)[:, None]
        agg = jax.ops.segment_sum(x[src], dst, num_segments=N)
        agg = agg * jax.lax.rsqrt(deg_in)[:, None]
        h = agg @ W + b
        mu = jnp.mean(h, axis=0)
        var = jnp.mean((h - mu) ** 2, axis=0)
        h = (h - mu) * jax.lax.rsqrt(var + BN_EPS) * gamma + beta
        h = jax.nn.relu(h)
        h = feature + h
        return h

    def _L2_gnn_ref(h, edge_index, W_pre, b_pre, W_post, b_post, W_lin, b_lin, gamma, beta):
        import jax, jax.numpy as jnp
        import numpy as np
        N = 6250
        E = 100000
        F = 128
        AVG_LOG = float(np.log(17.0))
        BN_EPS = 1e-05
        STD_EPS = 1e-05
        src = edge_index[0]
        dst = edge_index[1]
        n = h.shape[0]
        m = jnp.concatenate([h[dst], h[src]], axis=-1) @ W_pre + b_pre
        cnt = jax.ops.segment_sum(jnp.ones((m.shape[0],), m.dtype), dst, num_segments=n)
        deg = jnp.maximum(cnt, 1.0)[:, None]
        mean = jax.ops.segment_sum(m, dst, num_segments=n) / deg
        mean_sq = jax.ops.segment_sum(m * m, dst, num_segments=n) / deg
        std = jnp.sqrt(jax.nn.relu(mean_sq - mean * mean) + STD_EPS)
        has = (cnt > 0)[:, None]
        mn = jnp.where(has, jax.ops.segment_min(m, dst, num_segments=n), 0.0)
        mx = jnp.where(has, jax.ops.segment_max(m, dst, num_segments=n), 0.0)
        aggr = jnp.concatenate([mean, mn, mx, std], axis=-1)
        logd = jnp.log(deg + 1.0)
        out = jnp.concatenate([aggr, aggr * (logd / AVG_LOG), aggr * (AVG_LOG / logd)], axis=-1)
        out = jnp.concatenate([h, out], axis=-1) @ W_post + b_post
        out = out @ W_lin + b_lin
        mu = out.mean(axis=0)
        var = out.var(axis=0)
        out = (out - mu) / jnp.sqrt(var + BN_EPS) * gamma + beta
        out = jax.nn.relu(out)
        return out + h

    def _L3_gnn_ref(x, edge_index, W_l, b_l, W_r, b_r, att, bias):
        import jax, jax.numpy as jnp
        import numpy as np
        N_NODES = 12500
        N_EDGES = 200000
        DIM = 128
        NEG_SLOPE = 0.2
        src = edge_index[0]
        dst = edge_index[1]
        n = x.shape[0]
        x_l = x @ W_l + b_l
        x_r = x @ W_r + b_r
        h = x_l[src] + x_r[dst]
        h = jnp.where(h >= 0, h, NEG_SLOPE * h)
        e = h @ att
        e_max = jax.ops.segment_max(e, dst, num_segments=n)
        e_max = jnp.where(jnp.isfinite(e_max), e_max, 0.0)
        alpha = jnp.exp(e - e_max[dst])
        denom = jax.ops.segment_sum(alpha, dst, num_segments=n)
        alpha = alpha / (denom[dst] + 1e-16)
        out = jax.ops.segment_sum(alpha[:, None] * x_l[src], dst, num_segments=n)
        out = out + bias
        return jax.nn.relu(out)
    edge_index = jnp.stack([src, dst])
    h = jnp.maximum(_layernorm(x, axis=-1), 0.0)
    x = x + _L0_gnn_ref(h, edge_index, L0_gnn_W, L0_gnn_att_src, L0_gnn_att_dst, L0_gnn_bias, L0_gnn_bn_gamma, L0_gnn_bn_beta)
    h = jnp.maximum(_layernorm(x, axis=-1), 0.0)
    x = x + _L1_gnn_ref(h, L1_gnn_W, L1_gnn_b, L1_gnn_gamma, L1_gnn_beta, src, dst)
    h = jnp.maximum(_layernorm(x, axis=-1), 0.0)
    x = x + _L2_gnn_ref(h, edge_index, L2_gnn_W_pre, L2_gnn_b_pre, L2_gnn_W_post, L2_gnn_b_post, L2_gnn_W_lin, L2_gnn_b_lin, L2_gnn_gamma, L2_gnn_beta)
    h = jnp.maximum(_layernorm(x, axis=-1), 0.0)
    x = x + _L3_gnn_ref(h, edge_index, L3_gnn_W_l, L3_gnn_b_l, L3_gnn_W_r, L3_gnn_b_r, L3_gnn_att, L3_gnn_bias)
    return x

_drawn_inputs = setup_inputs


def setup_inputs(seed=0):
    import zlib

    import numpy as np

    out = dict(_drawn_inputs(seed))
    spreads = {'L0_gnn_bias': (0.0, 2.0),
     'L0_gnn_bn_gamma': (1.0, 0.2),
     'L0_gnn_bn_beta': (0.0, 0.1),
     'L1_gnn_gamma': (1.0, 0.2),
     'L1_gnn_beta': (0.0, 0.342),
     'L2_gnn_b_pre': (0.0, 0.8),
     'L2_gnn_b_post': (0.0, 2.0),
     'L2_gnn_b_lin': (0.0, 2.0),
     'L2_gnn_gamma': (1.0, 0.2),
     'L2_gnn_beta': (0.0, 0.451)}
    factors = {'L1_gnn_b': 200.0,
     'L3_gnn_b_l': 8.0,
     'L3_gnn_W_r': 7.062,
     'L3_gnn_b_r': 200.0,
     'L3_gnn_att': 2.694,
     'L3_gnn_bias': 8.0}
    for name, (base, spread) in spreads.items():
        noise = np.random.default_rng([zlib.crc32(name.encode()), seed]).standard_normal(out[name].shape)
        drawn = base * np.exp(spread * noise) if base else spread * noise
        out[name] = jnp.asarray(drawn.astype(out[name].dtype))
    for name, factor in factors.items():
        out[name] = (out[name] * factor).astype(out[name].dtype)
    return out
```

```python
import concourse.bass as bass
from concourse import mybir
from contextlib import ExitStack
import math

F32, I32, BF16 = mybir.dt.float32, mybir.dt.int32, mybir.dt.bfloat16
ALU, ACT, AX = mybir.AluOpType, mybir.ActivationFunctionType, mybir.AxisListType

P = 128
D = 128
N = 6250
E = 100000
TILES = -(-N // P)
LAST = N - (TILES - 1) * P
CHUNKS = -(-E // P)
FULL = E // P
TAIL = E - FULL * P
GROUP = 8
GROUPS = -(-(CHUNKS + TILES - 1) // GROUP)
STEPS = GROUPS * GROUP
IT = -(-(STEPS + GROUP) // P)
SPAD = IT * P
SLOTS = GROUP * P
BIG = 1e38
HEADS, HF = 8, 16
LN_EPS = BN_EPS = STD_EPS = 1e-5
SOFTMAX_EPS = 1e-16
SLOPE = 0.2
AVG_LOG = math.log(17.0)
TG = 7
NG = TILES // TG


def whole_program_tensors(nc, ctx):
    g = {}

    def sb(name, shape, dt):
        g[name] = ctx.enter_context(nc.sbuf_tensor(name, shape, dt))

    g["gathered"] = [ctx.enter_context(nc.semaphore(f"gathered{b}")) for b in range(4)]
    g["rows_gathered"] = [16 * IT, 0, 0, 0]
    sb("eye", [P, P], F32)
    sb("iota_row", [P, P], F32)
    sb("iota_col", [P, 1], F32)
    sb("ones", [P, P], F32)
    sb("mhalf", [P, P], F32)
    sb("loc", [P, SPAD], F32)
    sb("loc_end", [P, SPAD], F32)
    sb("src_idx", [P, SPAD], I32)
    sb("tile_row", [1, SPAD], I32)
    sb("rs_out", [P, TILES], F32)
    sb("cnt", [P, TILES], F32)
    sb("X", [P, TILES, D], F32)
    for name, shape, dt in (
        ("step_rows", (CHUNKS + 2, 2 * P), I32),
        ("keys", (P + SPAD * P + P,), F32),
        ("row_loc", (SPAD * P,), BF16),
        ("row_start", (SPAD * P,), BF16),
        ("row_end", (SPAD * P,), BF16),
        ("tab0", (TILES * P, D + HEADS), F32),
        ("tab1", (TILES * P, D), F32),
        ("tab2", (TILES * P, D), F32),
        ("tab3", (TILES * P, D), F32),
        ("h2", (TILES * P, D), F32),
    ):
        g[name] = nc.dram_tensor("dr_" + name, shape, dt, kind="Internal").ap()
    return g


def wait(eng, sem, value):
    if isinstance(value, int) and value <= 0:
        return
    eng.wait_ge(sem, value)


def wait_alone(eng, sem, value, stood):
    if isinstance(value, int) and value <= 0:
        return
    eng.wait_ge(sem, value)
    if not isinstance(value, int):
        eng.sem_inc(stood, 1)


def in_groups_of_two(eng, body):
    body(0, 0, 0)
    body(1, 0, 1)
    with eng.Fori(1, GROUPS // 2) as i:
        body(2 * i, i, 0)
        body(2 * i + 1, i, 1)


def load_tiles(nc, engine, row, lo, n, top=TILES - 1):
    _, vals = nc.values_load_multi_w_load_instructions(
        row[0:1, bass.ds(lo, n)], engines=[engine], min_val=0, max_val=top,
        skip_runtime_bounds_check_because="the row is clamped to the last tile when it is built")
    return vals


class Semaphores:

    def __init__(self, nc, ctx, prefix):
        self.nc, self.ctx, self.prefix, self.all = nc, ctx, prefix, []

    def __call__(self, name):
        self.all.append(self.ctx.enter_context(self.nc.semaphore(self.prefix + name)))
        return self.all[-1]

    def clear(self):
        with self.nc.Block() as block:
            @block.sync
            def _(sp):
                for s in self.all:
                    sp.sem_clear(s)


def build_steps(nc, g, src, dst):
    with ExitStack() as ctx:
        def sb(name, shape, dt):
            return ctx.enter_context(nc.sbuf_tensor(name, shape, dt))

        sem = Semaphores(nc, ctx, "")

        last_dst = sb("last_dst", [P, IT], I32)
        tail = sb("tail", [3, 2 * P], I32)
        fin = sb("fin", [P, IT], F32)
        big = sb("big", [P, IT], F32)
        itmp = sb("itmp", [P, IT], I32)
        iota_p = sb("iota_p", [P, IT], F32)
        iota_s = sb("iota_s", [P, SPAD], F32)
        ints = sb("ints", [P, SPAD], I32)
        intp = sb("intp", [P, IT], I32)
        before = sb("before", [P, IT, SPAD], BF16)
        ones_bf = sb("ones_bf", [P, P], BF16)
        crep = sb("crep", [P, SPAD], F32)
        chunk_f = sb("chunk_f", [P, IT], F32)
        chunk_i = sb("chunk_i", [P, IT], I32)
        tile_c = sb("tile_c", [P, IT], F32)
        edges = sb("edges", [P, IT, 2 * P], I32)
        ef = sb("ef", [P, IT, 2 * P], F32)
        locp = sb("locp", [P, IT, P], F32)
        v = sb("v", [P, IT, P], F32)
        v2 = sb("v2", [P, IT, P], F32)
        key = sb("key", [P, IT, P], F32)
        kprev = sb("kprev", [P, IT, P], F32)
        knext = sb("knext", [P, IT, P], F32)
        padrow = sb("padrow", [1, P], F32)
        b_loc = sb("b_loc", [P, IT, P], BF16)
        b_start = sb("b_start", [P, IT, P], BF16)
        b_end = sb("b_end", [P, IT, P], BF16)
        lo_i = sb("lo_i", [P, SPAD], I32)
        hi_i = sb("hi_i", [P, SPAD], I32)
        lo_f = sb("lo_f", [P, SPAD], F32)
        hi_f = sb("hi_f", [P, SPAD], F32)
        eq_lo = sb("eq_lo", [P, 2, 16, P], BF16)
        eq_hi = sb("eq_hi", [P, 2, 16, TILES], BF16)
        deg = sb("deg", [P, TILES], F32)
        ps_c = ctx.enter_context(nc.psum_tensor("ps_c", [P, 2, 512], F32))
        ps_p = ctx.enter_context(nc.psum_tensor("ps_p", [P, 512], F32))
        ps_t = ctx.enter_context(nc.psum_tensor("ps_t", [P, 3, 512], F32))
        ps_h = ctx.enter_context(nc.psum_tensor("ps_h", [P, 2, 512], F32))
        HALF = SPAD // 2

        consts = sem("consts")
        setup = sem("setup")
        copied = sem("copied")
        tail_in = sem("tail_in")
        last_in = sem("last_in")
        v_done = sem("v_done")
        counted = sem("counted")
        gathered = g["gathered"][0]
        keys_out = sem("keys_out")
        near_in = sem("near_in")
        rows_out = sem("rows_out")
        turned = sem("turned")
        hist = sem("hist")
        added = sem("added")
        onehots = sem("onehots")

        with nc.Block() as block:
            @block.gpsimd
            def _(pool):
                pool.memset(g["eye"][:], 0.0).then_inc(setup, 1)
                pool.memset(g["ones"][:], 1.0).then_inc(setup, 1)
                pool.memset(ones_bf[:], 1.0).then_inc(setup, 1)
                pool.memset(g["mhalf"][:], -0.5).then_inc(setup, 1)
                pool.memset(tail[:, 0:P], 0).then_inc(setup, 1)
                pool.memset(tail[:, P:2 * P], -1).then_inc(setup, 1)
                pool.memset(last_dst[:], 0).then_inc(setup, 1)
                pool.memset(padrow[:], -1.0).then_inc(setup, 1)
                pool.iota(ints[:], pattern=[[1, SPAD]], base=0, channel_multiplier=0).then_inc(setup, 1)
                pool.iota(intp[:], pattern=[[P, IT]], base=0, channel_multiplier=1).then_inc(setup, 1)
                pool.wait_ge(setup, 10)
                pool.affine_select(out=g["eye"][:], in_=g["eye"][:], compare_op=ALU.not_equal, fill=1.0,
                                   base=0, pattern=[[-1, P]], channel_multiplier=1).then_inc(consts, 1)
                pool.wait_ge(copied, 16 * 3)
                pool.wait_ge(v_done, 7)
                for k in range(IT):
                    pool.indirect_dma_start(
                        out=edges[:, k, :], out_offset=None, in_=g["step_rows"][:, :],
                        in_offset=bass.IndirectOffsetOnAxis(ap=chunk_i[:, k:k + 1], axis=0)).then_inc(gathered, 16)

                pool.wait_ge(added, STEPS // 16 + 2)
                pool.tensor_tensor(g["rs_out"][:], deg[:], g["mhalf"][:, 0:TILES], ALU.pow).then_inc(added, 1)
                pool.wait_ge(added, STEPS // 16 + 3)

            @block.sync
            def _(sp):
                sp.dma_start(g["step_rows"][0:FULL, 0:P],
                             src[0:FULL * P].rearrange("(c e) -> c e", e=P)).then_inc(copied, 16)
                sp.dma_start(g["step_rows"][0:FULL, P:2 * P],
                             dst[0:FULL * P].rearrange("(c e) -> c e", e=P)).then_inc(copied, 16)
                sp.wait_ge(setup, 10)
                sp.dma_start(tail[0:1, 0:TAIL], src[FULL * P:E].unsqueeze(0)).then_inc(tail_in, 16)
                sp.dma_start(tail[0:1, P:P + TAIL], dst[FULL * P:E].unsqueeze(0)).then_inc(tail_in, 16)
                lasts = dst[0:FULL * P].rearrange("(c e) -> c e", e=P)[:, P - 1:P]
                whole = FULL // P
                sp.dma_start(last_dst[:, 0:whole],
                             lasts[0:whole * P, :].rearrange("(k p) o -> p (k o)", p=P),
                             allow_slow_non_contiguous=True).then_inc(last_in, 16)
                sp.dma_start(last_dst[0:FULL - whole * P, whole:whole + 1],
                             lasts[whole * P:FULL, :], allow_slow_non_contiguous=True).then_inc(last_in, 16)
                sp.dma_start(last_dst[FULL - whole * P:CHUNKS - whole * P, whole:whole + 1],
                             dst[E - 1:E].unsqueeze(0)).then_inc(last_in, 16)
                sp.wait_ge(tail_in, 32)
                sp.dma_start(g["step_rows"][FULL:FULL + 3, :], tail[:]).then_inc(copied, 16)
                body = g["keys"][P:P + SPAD * P].rearrange("(k p e) -> p k e", p=P, e=P)
                sp.wait_ge(v_done, 14)
                sp.dma_start(body, key[:]).then_inc(keys_out, 16)
                sp.dma_start(g["keys"][0:P].unsqueeze(0), padrow[:]).then_inc(keys_out, 16)
                sp.dma_start(g["keys"][P + SPAD * P:2 * P + SPAD * P].unsqueeze(0), padrow[:]).then_inc(keys_out, 16)
                sp.wait_ge(keys_out, 48)
                sp.dma_start(kprev[:], g["keys"][P - 1:P - 1 + SPAD * P].rearrange("(k p e) -> p k e", p=P, e=P)).then_inc(near_in, 16)
                sp.dma_start(knext[:], g["keys"][P + 1:P + 1 + SPAD * P].rearrange("(k p e) -> p k e", p=P, e=P)).then_inc(near_in, 16)
                sp.wait_ge(v_done, 20)
                for row, tile in (("row_loc", b_loc), ("row_start", b_start), ("row_end", b_end)):
                    sp.dma_start(g[row].rearrange("(k p e) -> p k e", p=P, e=P), tile[:]).then_inc(rows_out, 16)
                sp.wait_ge(rows_out, 48)

            @block.vector
            def _(dve):
                V = nc.vector
                n = [0]

                def step(ins):
                    n[0] += 1
                    ins.then_inc(v_done, 1)

                def then(ins):
                    step(ins)
                    dve.wait_ge(v_done, n[0])

                dve.wait_ge(setup, 10)
                V.tensor_copy(g["iota_row"][:], ints[:, 0:P]).then_inc(consts, 1)
                V.tensor_copy(iota_s[:], ints[:]).then_inc(consts, 1)
                V.tensor_copy(iota_p[:], intp[:]).then_inc(consts, 1)
                V.tensor_copy(g["iota_col"][:], intp[:, 0:1]).then_inc(consts, 1)
                dve.wait_ge(consts, 5)
                dve.wait_ge(last_in, 48)
                then(V.tensor_single_scalar(itmp[:], last_dst[:], 7, op=ALU.logical_shift_right))
                then(V.tensor_tensor(fin[:], itmp[:], iota_p[:], ALU.add))
                then(V.tensor_scalar(big[:], iota_p[:], float(CHUNKS), 1e6, ALU.is_ge, ALU.mult))
                then(V.tensor_tensor(fin[:], fin[:], big[:], ALU.max))
                for k in range(IT):
                    ins = V.tensor_scalar(before[:, k, :], iota_s[:], fin[:, k:k + 1], None, ALU.is_gt)
                step(ins)
                dve.wait_ge(counted, 1)
                then(V.tensor_copy(chunk_f[:], ps_p[:, 0:IT]))
                then(V.tensor_copy(chunk_i[:], chunk_f[:]))
                then(V.tensor_tensor(tile_c[:], iota_p[:], chunk_f[:], ALU.subtract))
                then(V.tensor_scalar(tile_c[:], tile_c[:], float(TILES - 1), float(P), ALU.min, ALU.mult))
                for h in range(2):
                    ins = V.tensor_copy(crep[:, h * HALF:(h + 1) * HALF], ps_c[:, h, 0:HALF])
                then(ins)
                then(V.tensor_tensor(crep[:], iota_s[:], crep[:], ALU.subtract))
                V.tensor_scalar(g["tile_row"][:], crep[0:1, :], float(TILES - 1), None, ALU.min).then_inc(consts, 1)
                dve.wait_ge(gathered, 16 * IT)
                then(V.tensor_copy(ef[:], edges[:]))
                V_tile = tile_c[:].unsqueeze(2).to_broadcast([P, IT, P])
                V.tensor_tensor(locp[:], ef[:, :, P:2 * P], V_tile, ALU.subtract).then_inc(turned, 1)
                dve.wait_ge(turned, 1)
                V.tensor_scalar(v[:], locp[:], 0.0, None, ALU.is_ge).then_inc(turned, 1)
                dve.wait_ge(turned, 2)
                V.scalar_tensor_tensor(v2[:], locp[:], float(P), v[:], ALU.is_lt, ALU.mult).then_inc(turned, 1)
                dve.wait_ge(turned, 3)
                then(V.scalar_tensor_tensor(locp[:], locp[:], 1.0, v2[:], ALU.add, ALU.mult))
                step(V.scalar_tensor_tensor(key[:], ef[:, :, P:2 * P], 1.0, v2[:], ALU.add, ALU.mult))
                step(V.tensor_scalar(b_loc[:], locp[:], -1.0, None, ALU.add))
                dve.wait_ge(near_in, 32)
                then(V.tensor_tensor(v[:], key[:], kprev[:], ALU.not_equal))
                step(V.tensor_scalar(b_start[:], v[:], -BIG, None, ALU.mult))
                then(V.tensor_tensor(v2[:], key[:], knext[:], ALU.not_equal))
                step(V.tensor_scalar(b_end[:], v2[:], -BIG, None, ALU.mult))
                then(V.tensor_tensor(key[:], locp[:], v2[:], ALU.mult))
                for k in range(IT):
                    dve.wait_ge(counted, 2 + k)
                    cols = slice(k * P, (k + 1) * P)
                    V.tensor_scalar(g["loc"][:, cols], ps_t[:, 0, 0:P], -1.0, None, ALU.add)
                    V.tensor_scalar(g["loc_end"][:, cols], ps_t[:, 1, 0:P], -1.0, None, ALU.add)
                    ins = V.tensor_copy(g["src_idx"][:, cols], ps_t[:, 2, 0:P])
                    then(ins)
                then(V.tensor_single_scalar(lo_i[:], g["src_idx"][:], P - 1, op=ALU.bitwise_and))
                then(V.tensor_single_scalar(hi_i[:], g["src_idx"][:], 7, op=ALU.logical_shift_right))
                then(V.tensor_copy(lo_f[:], lo_i[:]))
                then(V.tensor_copy(hi_f[:], hi_i[:]))
                then(V.tensor_scalar(crep[:], g["loc"][:], 0.0, None, ALU.is_ge))
                then(V.scalar_tensor_tensor(hi_f[:], hi_f[:], 1.0, crep[:], ALU.add, ALU.mult))
                then(V.tensor_scalar(hi_f[:], hi_f[:], -1.0, None, ALU.add))
                V.memset(deg[:], 0.0).then_inc(added, 1)

                def onehot(i, b):
                    a = iota_bc(16, P)
                    V.tensor_tensor(eq_lo[:, b], a, lo_f[:, bass.ds(i * 16, 16)].unsqueeze(2).to_broadcast([P, 16, P]),
                                    ALU.is_equal).then_inc(onehots, 1)
                    V.tensor_tensor(eq_hi[:, b], iota_bc(16, TILES),
                                    hi_f[:, bass.ds(i * 16, 16)].unsqueeze(2).to_broadcast([P, 16, TILES]),
                                    ALU.is_equal).then_inc(onehots, 1)

                def iota_bc(m, w):
                    return g["iota_row"][:, 0:w].unsqueeze(1).to_broadcast([P, m, w])

                onehot(0, 0)
                onehot(1, 1)
                with dve.Fori(1, STEPS // 32) as i:
                    for b in range(2):
                        dve.wait_ge(hist, 2 * i + b - 1)
                        dve.wait_ge(added, 2 * i + b - 1)
                        V.tensor_tensor(deg[:], deg[:], ps_h[:, b, 0:TILES], ALU.add).then_inc(added, 1)
                        onehot(2 * i + b, b)
                for b in range(2):
                    dve.wait_ge(hist, STEPS // 16 - 1 + b)
                    dve.wait_ge(added, STEPS // 16 - 1 + b)
                    V.tensor_tensor(deg[:], deg[:], ps_h[:, b, 0:TILES], ALU.add).then_inc(added, 1)
                dve.wait_ge(added, STEPS // 16 + 1)
                V.tensor_scalar(deg[:], deg[:], 1.0, None, ALU.max).then_inc(added, 1)

            @block.tensor
            def _(pe):
                pe.wait_ge(v_done, 5)
                for h in range(2):
                    for k in range(IT):
                        nc.tensor.matmul(ps_c[:, h, 0:HALF], ones_bf[:], before[:, k, h * HALF:(h + 1) * HALF],
                                         start=(k == 0), stop=(k == IT - 1))
                for s in range(IT):
                    for k in range(IT):
                        ins = nc.tensor.matmul(ps_p[:, s:s + 1], before[:, k, s * P:(s + 1) * P], ones_bf[:, 0:1],
                                               start=(k == 0), stop=(k == IT - 1))
                ins.then_inc(counted, 1)
                pe.wait_ge(consts, 1)
                pe.wait_ge(v_done, 20)
                for k in range(IT):
                    if k:
                        pe.wait_ge(v_done, 20 + k)
                    for j, m in enumerate((locp[:, k, :], key[:, k, :], ef[:, k, 0:P])):
                        ins = nc.tensor.transpose(ps_t[:, j, 0:P], m, g["eye"][:])
                    ins.then_inc(counted, 1)

                def count(i, b, waits):
                    pe.wait_ge(onehots, waits)
                    for s in range(16):
                        ins = nc.tensor.matmul(ps_h[:, b, 0:TILES], eq_lo[:, b, s, :], eq_hi[:, b, s, :],
                                               start=(s == 0), stop=(s == 15))
                    ins.then_inc(hist, 1)

                count(0, 0, 2)
                count(1, 1, 4)
                with pe.Fori(1, STEPS // 32) as i:
                    for b in range(2):
                        count(i, b, 2 * (2 * i + b + 1))
        sem.clear()


def per_tile(v):
    return v.unsqueeze(2).to_broadcast([P, TILES, D])


def per_feature(v, tiles=TILES):
    return v.unsqueeze(1).to_broadcast([P, tiles, v.shape[1]])


def layer_norm_relu(nc, g, name, H):
    with ExitStack() as ctx:
        sem = Semaphores(nc, ctx, name)
        SQ = ctx.enter_context(nc.sbuf_tensor(name + "_sq", [P, TILES, D], F32))
        mean = ctx.enter_context(nc.sbuf_tensor(name + "_mean", [P, TILES], F32))
        var = ctx.enter_context(nc.sbuf_tensor(name + "_var", [P, TILES], F32))
        centred = sem("_centred")
        squared = sem("_squared")
        stat = sem("_stat")
        with nc.Block() as block:
            @block.vector
            def _(dve):
                V = nc.vector
                V.tensor_reduce(mean[:], g["X"][:], AX.X, ALU.add).then_inc(stat, 1)
                dve.wait_ge(stat, 1)
                V.tensor_scalar(mean[:], mean[:], 1.0 / D, None, ALU.mult).then_inc(stat, 1)
                dve.wait_ge(stat, 2)
                V.tensor_tensor(H[:], g["X"][:], per_tile(mean[:]), ALU.subtract).then_inc(centred, 1)
                dve.wait_ge(squared, 1)
                V.tensor_reduce(var[:], SQ[:], AX.X, ALU.add).then_inc(stat, 1)
                dve.wait_ge(stat, 3)
                V.tensor_scalar(var[:], var[:], 1.0 / D, LN_EPS, ALU.mult, ALU.add).then_inc(stat, 1)
                dve.wait_ge(stat, 4)
                dve.wait_ge(stat, 5)
                dve.wait_ge(centred, 1)
                V.scalar_tensor_tensor(H[:], H[:], 0.0, per_tile(var[:]), ALU.max, ALU.mult).then_inc(stat, 1)
                dve.wait_ge(stat, 6)

            @block.scalar
            def _(act):
                act.wait_ge(centred, 1)
                nc.scalar.activation(SQ[:], H[:], ACT.Square).then_inc(squared, 1)

            @block.gpsimd
            def _(pool):
                pool.wait_ge(stat, 4)
                pool.tensor_tensor(var[:], var[:], g["mhalf"][:, 0:TILES], ALU.pow).then_inc(stat, 1)
        sem.clear()


def node_matmul(nc, g, name, SRC, W, NC, evacuate, loads=()):
    per = 512 // NC
    banks = [(u, min(per, TG - u)) for u in range(0, TG, per)]
    with ExitStack() as ctx:
        sem = Semaphores(nc, ctx, name)
        STG = ctx.enter_context(nc.sbuf_tensor(name + "_stage", [P, TG, D], F32))
        HT = ctx.enter_context(nc.sbuf_tensor(name + "_ht", [P, TG, P], F32))
        TP = ctx.enter_context(nc.psum_tensor(name + "_tp", [P, 2, 512], F32))
        OP = ctx.enter_context(nc.psum_tensor(name + "_op", [P, len(banks), 512], F32))
        loaded = sem("_loaded")
        staged = sem("_staged")
        stood = sem("_stood")
        turned = sem("_turned")
        ht_in = sem("_ht_in")
        product = sem("_product")
        taken = sem("_taken")

        def groups(eng, body):
            body(0)
            with eng.Fori(1, NG) as i:
                body(i)

        with nc.Block() as block:
            @block.sync
            def _(sp):
                for o, i in loads:
                    sp.dma_start(o, i).then_inc(loaded, 16)

            @block.gpsimd
            def _(pool):
                def body(i):
                    wait_alone(pool, turned, i, stood)
                    pool.tensor_copy(STG[:], SRC[:, bass.ds(i * TG, TG), :]).then_inc(staged, 1)
                groups(pool, body)

            @block.tensor
            def _(pe):
                if loads:
                    pe.wait_ge(loaded, 16 * len(loads))

                def body(i):
                    pe.wait_ge(staged, i + 1)
                    for u in range(TG):
                        ins = nc.tensor.transpose(TP[:, u // 4, (u % 4) * P:(u % 4 + 1) * P], STG[:, u, :], g["eye"][:])
                    ins.then_inc(turned, 1)
                    wait(pe, taken, i)
                    pe.wait_ge(ht_in, i + 1)
                    for u in range(TG):
                        ins = nc.tensor.matmul(OP[:, u // per, (u % per) * NC:(u % per + 1) * NC], HT[:, u, :], W,
                                               start=True, stop=True)
                    ins.then_inc(product, 1)
                groups(pe, body)

            @block.scalar
            def _(act):
                def body(i):
                    wait_alone(act, turned, i + 1, stood)
                    nc.scalar.copy(HT[:, 0:4, :], TP[:, 0, :].rearrange("p (u n) -> p u n", n=P))
                    nc.scalar.copy(HT[:, 4:TG, :], TP[:, 1, 0:(TG - 4) * P].rearrange("p (u n) -> p u n", n=P)).then_inc(ht_in, 1)
                groups(act, body)

            @block.vector
            def _(dve):
                if loads:
                    dve.wait_ge(loaded, 16 * len(loads))

                def body(i):
                    wait(dve, taken, i)
                    dve.wait_ge(product, i + 1)
                    for k, (u, m) in enumerate(banks):
                        ins = evacuate(dve, i * TG + u, m, OP[:, k, 0:m * NC].rearrange("p (u n) -> p u n", n=NC),
                                       i, k)
                    ins.then_inc(taken, 1)
                groups(dve, body)
                dve.wait_ge(taken, NG)
        sem.clear()


def batch_norm(nc, g, name, U, H, gamma, beta):
    with ExitStack() as ctx:
        sem = Semaphores(nc, ctx, name)
        SQ = ctx.enter_context(nc.sbuf_tensor(name + "_sq", [P, TILES, D], F32))
        gam = ctx.enter_context(nc.sbuf_tensor(name + "_gam", [P, D], F32))
        bet = ctx.enter_context(nc.sbuf_tensor(name + "_bet", [P, D], F32))
        mean = ctx.enter_context(nc.sbuf_tensor(name + "_mean", [P, D], F32))
        scl = ctx.enter_context(nc.sbuf_tensor(name + "_scl", [P, D], F32))
        PM = ctx.enter_context(nc.psum_tensor(name + "_pm", [P, 512], F32))
        PV = ctx.enter_context(nc.psum_tensor(name + "_pv", [P, 512], F32))
        loaded = sem("_loaded")
        summed = sem("_summed")
        centred = sem("_centred")
        squared = sem("_squared")
        stat = sem("_stat")
        root = sem("_root")

        with nc.Block() as block:
            @block.gpsimd
            def _(pool):
                pool.wait_ge(stat, 2)
                pool.tensor_tensor(scl[:], scl[:], g["mhalf"][:], ALU.pow).then_inc(root, 1)

            @block.sync
            def _(sp):
                sp.dma_start(gam[:], gamma.partition_broadcast(P)).then_inc(loaded, 16)
                sp.dma_start(bet[:], beta.partition_broadcast(P)).then_inc(loaded, 16)

            @block.tensor
            def _(pe):
                def column_sums(out, A):
                    nc.tensor.matmul(out, g["ones"][:], A[:, 0, :], start=True, stop=False)
                    with pe.Fori(1, TILES - 1) as t:
                        nc.tensor.matmul(out, g["ones"][:], A[:, bass.ds(t, 1), :].rearrange("p o d -> p (o d)"), start=False, stop=False)
                    nc.tensor.matmul(out, g["ones"][0:LAST, :], A[0:LAST, TILES - 1, :],
                                     start=False, stop=True).then_inc(summed, 1)
                column_sums(PM[:, 0:D], U)
                pe.wait_ge(squared, 1)
                column_sums(PV[:, 0:D], SQ)

            @block.scalar
            def _(act):
                act.wait_ge(centred, 1)
                nc.scalar.activation(SQ[:], U[:], ACT.Square).then_inc(squared, 1)

            @block.vector
            def _(dve):
                V = nc.vector
                n = [0]

                def then(ins):
                    n[0] += 1
                    ins.then_inc(stat, 1)
                    dve.wait_ge(stat, n[0])

                dve.wait_ge(summed, 1)
                then(V.tensor_scalar(mean[:], PM[:, 0:D], 1.0 / N, None, ALU.mult))
                V.tensor_tensor(U[:], U[:], per_feature(mean[:]), ALU.subtract).then_inc(centred, 1)
                dve.wait_ge(loaded, 32)
                dve.wait_ge(summed, 2)
                then(V.tensor_scalar(scl[:], PV[:, 0:D], 1.0 / N, BN_EPS, ALU.mult, ALU.add))
                dve.wait_ge(root, 1)
                then(V.tensor_tensor(scl[:], scl[:], gam[:], ALU.mult))
                dve.wait_ge(squared, 1)
                then(V.tensor_tensor(U[:], U[:], per_feature(scl[:]), ALU.mult))
                then(V.tensor_tensor(U[:], U[:], per_feature(bet[:]), ALU.add))
                then(V.scalar_tensor_tensor(U[:], U[:], 0.0, H[:], ALU.max, ALU.add))
                then(V.tensor_tensor(g["X"][:], g["X"][:], U[:], ALU.add))
        sem.clear()


class Count:

    def __init__(self, eng, sem, before):
        self.eng, self.sem, self.n = eng, sem, before

    def then(self, ins):
        ins.then_inc(self.sem, 1)
        self.n = self.n + 1
        self.eng.wait_ge(self.sem, self.n)


def gather_group(nc, pool, g, idx, ready, table, out_of, gathered, k, stood):
    pool.tensor_copy(idx, g["src_idx"][:, bass.ds(k * GROUP, GROUP)]).then_inc(ready, 1)
    wait_alone(pool, ready, k + 1, stood)
    for s in range(GROUP):
        pool.indirect_dma_start(out=out_of(s), out_offset=None, in_=table,
                                in_offset=bass.IndirectOffsetOnAxis(ap=idx[:, s:s + 1], axis=0)).then_inc(gathered, 16)


def onehot_rows(nc, g, loc, k):
    return (g["iota_row"][:].unsqueeze(1).to_broadcast([P, GROUP, P]),
            loc[:, bass.ds(k * GROUP, GROUP)].unsqueeze(2).to_broadcast([P, GROUP, P]))


def softmax_pass(nc, g, name, heads, table, dst_part, dst_cols, ACC, att=None):
    hd = D // heads
    TC = table.shape[1]
    WC = D + heads
    AC = ACC.shape[2]
    PER = 3
    M = 1 if att is not None else 2
    with ExitStack() as ctx:
        def sb(n, shape, dt=F32):
            return ctx.enter_context(nc.sbuf_tensor(name + n, shape, dt))

        def ps(n, shape):
            return ctx.enter_context(nc.psum_tensor(name + n, shape, F32))

        sem = Semaphores(nc, ctx, name)

        idx = sb("idx", [P, 2, GROUP], I32)
        G = sb("G", [P, 2, GROUP, TC])
        LR = sb("LR", [P, 2, SLOTS], BF16)
        MS = sb("MS", [heads, 2, SLOTS], BF16)
        ME = sb("ME", [heads, 2, SLOTS], BF16)
        LF = sb("LF", [heads, 2])
        ST = sb("ST", [P, SLOTS])
        S = sb("S", [P, 2, GROUP, P])
        Z = sb("Z", [P, GROUP, dst_cols])
        SC = sb("SC", [P, GROUP, heads])
        FW = sb("FW", [heads, 2, SLOTS])
        CM = sb("CM", [heads, SLOTS])
        DIF = sb("DIF", [P, GROUP, heads])
        RH = sb("RH", [P, 2, GROUP, AC])
        cont = sb("cont", [heads, 1])
        drop = sb("drop", [heads, 1])
        fac = sb("fac", [heads, 1])
        OH = sb("OH", [heads, P])
        DG = sb("DG", [heads, heads + 1])
        rest = sb("rest", [P, 1])
        R = sb("R", [P, heads])
        ET = ps("ET", [heads, SLOTS])
        DP = ps("DP", [P, GROUP, dst_cols]) if att is not None else ps("DP", [P, 512])
        SB = ps("SB", [P, 512])
        OUT = ps("OUT", [P, 3, 512])
        dp_view = DP[:] if att is not None else DP[:, 0:GROUP * heads].rearrange("p (s h) -> p s h", h=heads)
        stab = SB[:, 0:GROUP * heads].rearrange("p (s h) -> p s h", h=heads)
        RP = SB[:, 256:256 + heads + 1]

        idx_ready = sem("idx_ready")
        gathered = g["gathered"]
        base = g["rows_gathered"][:]
        locrow_in = [sem(f"locrow_in{b}") for b in range(2)]
        masks_in = [sem(f"masks_in{b}") for b in range(2)]
        start = sem("start")
        stood = sem("stood")
        st_done = sem("st_done")
        s_done = sem("s_done")
        dp_done = sem("dp_done")
        score = sem("score")
        et_done = sem("et_done")
        cm_done = sem("cm_done")
        drop_done = sem("drop_done")
        fac_done = sem("fac_done")
        dg_done = sem("dg_done")
        stab_done = sem("stab_done")
        dif_done = sem("dif_done")
        p_done = sem("p_done")
        rh_done = sem("rh_done")
        r_done = sem("r_done")
        mm_done = sem("mm_done")
        acc_done = sem("acc_done")
        dve_step = sem("dve_step")

        with nc.Block() as block:
            @block.gpsimd
            def _(pool):
                def body(k, i, b):
                    wait_alone(pool, rh_done, k - 1, stood)
                    gather_group(nc, pool, g, idx[:, b, :], idx_ready, table[:, :], lambda s: G[:, b, s, :],
                                 gathered[b], k, stood)
                in_groups_of_two(pool, body)

            @block.sync
            def _(sp):
                def locrow(k, b):
                    sp.dma_start(LR[:, b, :], g["row_loc"][bass.ds(k * SLOTS, SLOTS)].partition_broadcast(P)).then_inc(locrow_in[b], 16)

                def body(k, i, b):
                    wait(sp, st_done, k - 1)
                    locrow(k, b)
                    wait(sp, rh_done, k - 1)
                    for t, row in ((MS, "row_start"), (ME, "row_end")):
                        sp.dma_start(t[:, b, :], g[row][bass.ds(k * SLOTS, SLOTS)].partition_broadcast(heads)).then_inc(masks_in[b], 16)
                in_groups_of_two(sp, body)
                sp.wait_ge(st_done, GROUPS - 1)
                locrow(GROUPS, 0)

            @block.scalar
            def _(act):
                def body(k, i, b):
                    wait_alone(act, drop_done, k + 1, stood)
                    nc.scalar.activation(fac[:], drop[:], ACT.Exp).then_inc(fac_done, 1)
                    wait_alone(act, dif_done, k + 1, stood)
                    nc.scalar.activation(RH[:, b, :, D:D + heads], DIF[:], ACT.Exp).then_inc(p_done, 1)
                in_groups_of_two(act, body)

            @block.vector
            def _(dve):
                V = nc.vector

                def st(k, b, use):
                    dve.wait_ge(locrow_in[b], 16 * use)
                    V.tensor_copy(LF[:, b:b + 1], LR[0:heads, b, 0:1])
                    V.tensor_scalar(ST[:], LR[:, b, :], g["iota_col"][:], None, ALU.is_equal).then_inc(st_done, 1)

                def add(k, first, tiles):
                    dve.wait_ge(mm_done, k + 1)
                    for s, t in enumerate(tiles):
                        dst = ACC[:, bass.ds(t, 1), :].rearrange("p o c -> p (o c)")
                        dve.wait_ge(acc_done, first + s)
                        V.tensor_tensor(dst, dst, OUT[:, s // PER, (s % PER) * AC:(s % PER + 1) * AC],
                                        ALU.add).then_inc(acc_done, 1)

                CHAIN = 9
                V.memset(ACC[:], 0.0).then_inc(acc_done, 1)
                V.memset(FW[:, 1, SLOTS - 1:SLOTS], -BIG).then_inc(start, 1)
                V.memset(DG[:, heads:heads + 1], 1.0 / heads).then_inc(start, 1)
                st(0, 0, 1)
                dve.wait_ge(start, 2)

                def body(k, i, b):
                    c = Count(dve, dve_step, k * CHAIN)
                    if isinstance(k, int) and k == 0:
                        tiles = load_tiles(nc, mybir.EngineType.DVE, g["tile_row"], 0, 1)
                    else:
                        tiles = load_tiles(nc, mybir.EngineType.DVE, g["tile_row"], (k - 1) * GROUP, GROUP + 1)
                    first = tiles[-1]
                    dve.wait_ge(gathered[b], base[b] + 16 * GROUP * (i + 1))
                    dve.wait_ge(dp_done, k + 1)
                    if att is not None:
                        c.then(V.tensor_tensor(Z[:], G[:, b], dp_view, ALU.add))
                        c.then(V.scalar_tensor_tensor(Z[:], Z[:], SLOPE, Z[:], ALU.mult, ALU.max))
                        c.then(V.tensor_tensor(Z[:], Z[:], per_feature(att[:], GROUP), ALU.mult))
                        V.tensor_reduce(SC[:, :, 0], Z[:], AX.X, ALU.add).then_inc(score, 1)
                    else:
                        c.then(V.tensor_tensor(Z[:], G[:, b, :, D:D + heads], dp_view, ALU.add))
                        V.scalar_tensor_tensor(SC[:], Z[:], SLOPE, Z[:], ALU.mult, ALU.max).then_inc(score, 1)
                    if b == 0:
                        st(k + 1, 1, i + 1)
                    else:
                        st(k + 1, 0, i + 2)
                    V.tensor_tensor(S[:, b], *onehot_rows(nc, g, g["loc"], k), ALU.is_equal).then_inc(s_done, 1)
                    dve.wait_ge(masks_in[b], 32 * (i + 1))
                    dve.wait_ge(et_done, k + 1)
                    c.then(V.tensor_tensor_scan(out=FW[:, b, :], data0=MS[:, b, :], data1=ET[:],
                                                initial=FW[:, 1 - b, SLOTS - 1:SLOTS], op0=ALU.add, op1=ALU.max))
                    V.tensor_tensor_scan(out=CM[:, ::-1], data0=ME[:, b, ::-1], data1=FW[:, b, ::-1],
                                         initial=-BIG, op0=ALU.add, op1=ALU.max).then_inc(cm_done, 1)
                    c.then(V.tensor_scalar(cont[:], MS[:, b, 0:1], -0.5, None, ALU.is_ge))
                    dve.wait_ge(cm_done, k + 1)
                    c.then(V.tensor_tensor(drop[:], FW[:, 1 - b, SLOTS - 1:SLOTS], CM[:, 0:1], ALU.subtract))
                    V.tensor_tensor(drop[:], drop[:], cont[:], ALU.mult).then_inc(drop_done, 1)
                    dve.wait_ge(st_done, k + 1)
                    c.then(V.tensor_scalar(OH[:], g["iota_row"][0:heads, :], LF[:, b:b + 1], None, ALU.is_equal))
                    if not (isinstance(k, int) and k == 0):
                        add(k - 1, (GROUP + M) * (k - 1) + M + 1, tiles[:GROUP])
                    dve.wait_ge(stab_done, k + 1)
                    V.tensor_tensor(DIF[:], SC[:], stab, ALU.subtract).then_inc(dif_done, 1)
                    if att is None:
                        c.then(V.tensor_scalar(RH[:, b, :, AC - 1:AC], g["loc_end"][:, bass.ds(k * GROUP, GROUP)].unsqueeze(2),
                                               0.0, None, ALU.is_ge))
                        c.then(V.tensor_tensor(RH[:, b, :, WC:WC + heads], stab,
                                               RH[:, b, :, AC - 1:AC].to_broadcast([P, GROUP, heads]), ALU.mult))
                    dve.wait_ge(fac_done, k + 1)
                    V.tensor_scalar(DG[:, 0:heads], g["eye"][0:heads, 0:heads], fac[:], None, ALU.mult).then_inc(dg_done, 1)
                    dve.wait_ge(p_done, k + 1)
                    V.tensor_tensor(RH[:, b, :, 0:D].rearrange("p s (h f) -> p s h f", h=heads),
                                    G[:, b, :, 0:D].rearrange("p s (h f) -> p s h f", h=heads),
                                    RH[:, b, :, D:D + heads].unsqueeze(3).to_broadcast([P, GROUP, heads, hd]),
                                    ALU.mult).then_inc(rh_done, 1)
                    dve.wait_ge(r_done, k + 1)
                    c.then(V.tensor_scalar(rest[:], RP[:, heads:heads + 1], -1.0, 1.0, ALU.mult, ALU.add))
                    c.then(V.tensor_scalar(R[:], RP[:, 0:heads], rest[:], None, ALU.add))
                    done = 1 if isinstance(k, int) and k == 0 else (GROUP + M) * k + 1
                    dve.wait_ge(acc_done, done)
                    if att is None:
                        rows = ACC[:, bass.ds(first, 1), 0:D].rearrange("p o (h f) -> p (o h) f", h=heads)
                        V.tensor_tensor(rows, rows, R[:].unsqueeze(2).to_broadcast([P, heads, hd]), ALU.mult).then_inc(acc_done, 1)
                        den = ACC[:, bass.ds(first, 1), D:WC].rearrange("p o h -> p (o h)")
                        V.tensor_tensor(den, den, R[:], ALU.mult).then_inc(acc_done, 1)
                    else:
                        rows = ACC[:, bass.ds(first, 1), 0:WC].rearrange("p o c -> p (o c)")
                        V.tensor_scalar(rows, rows, R[:], None, ALU.mult).then_inc(acc_done, 1)
                    if isinstance(k, int):
                        assert c.n == (k + 1) * CHAIN

                in_groups_of_two(dve, body)
                add(GROUPS - 1, (GROUP + M) * (GROUPS - 1) + M + 1,
                    load_tiles(nc, mybir.EngineType.DVE, g["tile_row"], (GROUPS - 1) * GROUP, GROUP))
                dve.wait_ge(acc_done, (GROUP + M) * GROUPS + 1)

            @block.tensor
            def _(pe):
                def destinations(k):
                    tiles = load_tiles(nc, mybir.EngineType.PE, g["tile_row"], k * GROUP, GROUP)
                    pe.wait_ge(st_done, k + 1)
                    for s, t in enumerate(tiles):
                        ins = nc.tensor.matmul(dp_view[:, s, :], ST[:, s * P:(s + 1) * P],
                                               dst_part[:, bass.ds(t, 1), :].rearrange("p o c -> p (o c)"), start=True, stop=True)
                    ins.then_inc(dp_done, 1)

                destinations(0)

                def body(k, i, b):
                    pe.wait_ge(score, k + 1)
                    for s in range(GROUP):
                        ins = nc.tensor.matmul(ET[:, s * P:(s + 1) * P], SC[:, s, :], g["eye"][:], start=True, stop=True)
                    ins.then_inc(et_done, 1)
                    destinations(k + 1)
                    pe.wait_ge(cm_done, k + 1)
                    for s in range(GROUP):
                        ins = nc.tensor.matmul(stab[:, s, :], CM[:, s * P:(s + 1) * P], g["eye"][0:heads, 0:heads],
                                               start=True, stop=True)
                    ins.then_inc(stab_done, 1)
                    pe.wait_ge(dg_done, k + 1)
                    nc.tensor.matmul(RP, OH[:], DG[:], start=True, stop=True).then_inc(r_done, 1)
                    pe.wait_ge(s_done, k + 1)
                    pe.wait_ge(rh_done, k + 1)
                    for s in range(GROUP):
                        ins = nc.tensor.matmul(OUT[:, s // PER, (s % PER) * AC:(s % PER + 1) * AC], S[:, b, s, :], RH[:, b, s, :],
                                               start=True, stop=True)
                    ins.then_inc(mm_done, 1)
                in_groups_of_two(pe, body)
        sem.clear()
        for b in range(2):
            g["rows_gathered"][b] += 16 * GROUP * (GROUPS // 2)




def sum_pass(nc, g, table, ACC):
    name = "s_"
    AC = D + 1
    PER = 3
    with ExitStack() as ctx:
        sem = Semaphores(nc, ctx, name)

        idx = ctx.enter_context(nc.sbuf_tensor(name + "idx", [P, 2, GROUP], I32))
        G = ctx.enter_context(nc.sbuf_tensor(name + "G", [P, 2, GROUP, AC], F32))
        S = ctx.enter_context(nc.sbuf_tensor(name + "S", [P, 2, GROUP, P], F32))
        OUT = ctx.enter_context(nc.psum_tensor(name + "OUT", [P, 2, 3, 512], F32))
        idx_ready = sem("idx_ready")
        gathered = g["gathered"]
        base = g["rows_gathered"][:]
        stood = sem("p_stood")
        start = sem("start")
        s_done = sem("s_done")
        mm_done = sem("mm_done")
        acc_done = sem("acc_done")

        with nc.Block() as block:
            @block.gpsimd
            def _(pool):
                def body(k, i, b):
                    wait_alone(pool, mm_done, k - 1, stood)
                    gather_group(nc, pool, g, idx[:, b, :], idx_ready, table[:, :], lambda s: G[:, b, s, 0:D],
                                 gathered[b], k, stood)
                in_groups_of_two(pool, body)

            @block.vector
            def _(dve):
                V = nc.vector

                def add(k, b):
                    tiles = load_tiles(nc, mybir.EngineType.DVE, g["tile_row"], k * GROUP, GROUP)
                    dve.wait_ge(mm_done, k + 1)
                    for s, t in enumerate(tiles):
                        dst = ACC[:, bass.ds(t, 1), :].rearrange("p o c -> p (o c)")
                        dve.wait_ge(acc_done, k * GROUP + 1 + s)
                        V.tensor_tensor(dst, dst, OUT[:, b, s // PER, (s % PER) * AC:(s % PER + 1) * AC],
                                        ALU.add).then_inc(acc_done, 1)

                V.memset(G[:, :, :, D:AC], 1.0).then_inc(start, 1)
                V.memset(ACC[:], 0.0).then_inc(acc_done, 1)

                def body(k, i, b):
                    wait(dve, mm_done, k - 1)
                    V.tensor_tensor(S[:, b], *onehot_rows(nc, g, g["loc"], k), ALU.is_equal).then_inc(s_done, 1)
                    if not (isinstance(k, int) and k == 0):
                        add(k - 1, 1 - b)
                in_groups_of_two(dve, body)
                add(GROUPS - 1, 1)
                dve.wait_ge(acc_done, GROUP * GROUPS + 1)

            @block.tensor
            def _(pe):
                pe.wait_ge(start, 1)

                def body(k, i, b):
                    wait(pe, acc_done, 1 + GROUP * (k - 1) if not isinstance(k, int) or k >= 2 else 0)
                    pe.wait_ge(s_done, k + 1)
                    pe.wait_ge(gathered[b], base[b] + 16 * GROUP * (i + 1))
                    for s in range(GROUP):
                        ins = nc.tensor.matmul(OUT[:, b, s // PER, (s % PER) * AC:(s % PER + 1) * AC], S[:, b, s, :], G[:, b, s, :],
                                               start=True, stop=True)
                    ins.then_inc(mm_done, 1)
                in_groups_of_two(pe, body)
        sem.clear()
        for b in range(2):
            g["rows_gathered"][b] += 16 * GROUP * (GROUPS // 2)


def moments_pass(nc, g, table, ACC):
    name = "m_"
    Q = 4
    with ExitStack() as ctx:
        def sb(n, shape, dt=F32):
            return ctx.enter_context(nc.sbuf_tensor(name + n, shape, dt))

        sem = Semaphores(nc, ctx, name)

        idx = sb("idx", [P, Q, GROUP], I32)
        G = sb("G", [P, Q, GROUP, D])
        SQ = sb("SQ", [P, GROUP, D])
        S = sb("S", [P, 2, GROUP, P])
        SE = sb("SE", [P, 2, GROUP, P])
        MS = sb("MS", [P, 2, SLOTS], BF16)
        MN = sb("MN", [P, SLOTS], BF16)
        XT = sb("XT", [P, 2, 2, SLOTS])
        XB = sb("XB", [P, 2, 2, 2, D])
        GT = ctx.enter_context(nc.psum_tensor(name + "GT", [P, SLOTS], F32))
        BK = ctx.enter_context(nc.psum_tensor(name + "BK", [P, 4, 512], F32))
        OUT = ctx.enter_context(nc.psum_tensor(name + "OUT", [P, 2, 512], F32))
        idx_ready = sem("idx_ready")
        gathered = g["gathered"]
        base = g["rows_gathered"][:]
        masks_in = [sem(f"masks_in{b}") for b in range(2)]
        stood = sem("p_stood")
        start = sem("start")
        gt_done = sem("gt_done")
        mn_done = sem("mn_done")
        scanned = sem("scanned")
        s_done = sem("s_done")
        sq_done = sem("sq_done")
        bk_done = sem("bk_done")
        xb_done = sem("xb_done")
        step_done = sem("step_done")
        acc_done = sem("acc_done")

        def in_groups_of_four(eng, body):
            for b in range(Q):
                body(b, 0, b)
            with eng.Fori(1, GROUPS // Q) as i:
                for b in range(Q):
                    body(Q * i + b, i, b)

        def is_first(k):
            return isinstance(k, int) and k == 0

        with nc.Block() as block:
            @block.gpsimd
            def _(pool):
                def body(k, i, b):
                    if not isinstance(k, int):
                        wait_alone(pool, step_done, (k - Q + 1) * GROUP, stood)
                    gather_group(nc, pool, g, idx[:, b, :], idx_ready, table[:, :], lambda s: G[:, b, s, :],
                                 gathered[b], k, stood)
                in_groups_of_four(pool, body)

            @block.sync
            def _(sp):
                def body(k, i, b):
                    wait(sp, scanned, 2 * (k - 1))
                    sp.dma_start(MS[:, b % 2, :], g["row_start"][bass.ds(k * SLOTS, SLOTS)].partition_broadcast(P)).then_inc(masks_in[b % 2], 16)
                in_groups_of_four(sp, body)

            @block.scalar
            def _(act):
                def back(k, i, b):
                    wait_alone(act, gathered[b], base[b] + 16 * GROUP * (i + 1), stood)
                    wait_alone(act, step_done, k * GROUP, stood)
                    nc.scalar.activation(SQ[:], G[:, b], ACT.Square).then_inc(sq_done, 1)
                    for q in range(4):
                        wait_alone(act, bk_done, 4 * k + q + 1, stood)
                        if q >= 2:
                            wait_alone(act, step_done, k * GROUP + 2 * (q - 1), stood)
                        nc.scalar.copy(XB[:, q % 2], BK[:, q, :].rearrange("p (s m d) -> p s m d", s=2, m=2)).then_inc(xb_done, 1)
                in_groups_of_four(act, back)

            @block.vector
            def _(dve):
                V = nc.vector

                def add(k, steps):
                    tiles = load_tiles(nc, mybir.EngineType.DVE, g["tile_row"], k * GROUP + steps[0], len(steps))
                    for s, t in zip(steps, tiles):
                        dst = ACC[:, bass.ds(t, 1), :].rearrange("p o c -> p (o c)")
                        dve.wait_ge(step_done, k * GROUP + s + 1)
                        dve.wait_ge(acc_done, k * GROUP + s + 1)
                        V.tensor_tensor(dst, dst, OUT[:, s % 2, :], ALU.add).then_inc(acc_done, 1)

                V.memset(ACC[:], 0.0).then_inc(acc_done, 1)
                V.memset(XT[:, 1, 0, SLOTS - 1:SLOTS], BIG).then_inc(start, 1)
                V.memset(XT[:, 1, 1, SLOTS - 1:SLOTS], -BIG).then_inc(start, 1)
                dve.wait_ge(start, 2)

                def body(k, i, b):
                    c = b % 2
                    dve.wait_ge(masks_in[c], 16 * ((k - c) // 2 + 1) if isinstance(k, int) else 16 * (2 * i + b // 2 + 1))
                    wait(dve, scanned, 2 * k)
                    V.tensor_scalar(MN[:], MS[:, c, :], -1.0, None, ALU.mult).then_inc(mn_done, 1)
                    V.tensor_tensor(S[:, c], *onehot_rows(nc, g, g["loc"], k), ALU.is_equal)
                    V.tensor_tensor(SE[:, c], *onehot_rows(nc, g, g["loc_end"], k), ALU.is_equal).then_inc(s_done, 1)
                    dve.wait_ge(gt_done, k + 1)
                    dve.wait_ge(mn_done, k + 1)
                    for m, (mask, op) in enumerate(((MN[:], ALU.min), (MS[:, c, :], ALU.max))):
                        wait(dve, scanned, 2 * k)
                        V.tensor_tensor_scan(out=XT[:, c, m, :], data0=mask, data1=GT[:],
                                             initial=XT[:, 1 - c, m, SLOTS - 1:SLOTS], op0=ALU.add, op1=op).then_inc(scanned, 1)
                        if not is_first(k):
                            add(k - 1, range(4 * m, 4 * m + 4))
                in_groups_of_four(dve, body)
                add(GROUPS - 1, range(GROUP))
                dve.wait_ge(acc_done, GROUP * GROUPS + 1)

            @block.tensor
            def _(pe):
                def turn(k, i, b):
                    wait(pe, scanned, 2 * k)
                    pe.wait_ge(gathered[b], base[b] + 16 * GROUP * (i + 1))
                    for s in range(GROUP):
                        ins = nc.tensor.transpose(GT[:, s * P:(s + 1) * P], G[:, b, s, :], g["eye"][:])
                    ins.then_inc(gt_done, 1)

                def sums(k, b):
                    c = b % 2
                    pe.wait_ge(scanned, 2 * (k + 1))
                    for q in range(4):
                        wait(pe, xb_done, 4 * (k - 1) + q + 1)
                        for s in (2 * q, 2 * q + 1):
                            for m in range(2):
                                ins = nc.tensor.transpose(BK[:, q, ((s % 2) * 2 + m) * D:((s % 2) * 2 + m + 1) * D],
                                                          XT[:, c, m, s * P:(s + 1) * P], g["eye"][:])
                        ins.then_inc(bk_done, 1)
                    pe.wait_ge(s_done, k + 1)
                    pe.wait_ge(sq_done, k + 1)
                    for s in range(GROUP):
                        pe.wait_ge(xb_done, 4 * k + s // 2 + 1)
                        wait(pe, acc_done, k * GROUP + s if not isinstance(k, int) or k * GROUP + s >= 2 else 0)
                        nc.tensor.matmul(OUT[:, s % 2, 0:D], S[:, c, s, :], G[:, b, s, :], start=True, stop=True)
                        nc.tensor.matmul(OUT[:, s % 2, D:3 * D], SE[:, c, s, :], XB[:, (s // 2) % 2, s % 2].rearrange("p m d -> p (m d)"), start=True, stop=True)
                        nc.tensor.matmul(OUT[:, s % 2, 3 * D:4 * D], S[:, c, s, :], SQ[:, s, :], start=True, stop=True).then_inc(step_done, 1)

                def body(k, i, b):
                    turn(k, i, b)
                    if not is_first(k):
                        sums(k - 1, (b - 1) % Q)
                in_groups_of_four(pe, body)
                sums(GROUPS - 1, Q - 1)
        sem.clear()
        for b in range(Q):
            g["rows_gathered"][b] += 16 * GROUP * (GROUPS // Q)


def layer_gat(nc, g, w):
    with ExitStack() as ctx:
        sem = Semaphores(nc, ctx, "")
        H = ctx.enter_context(nc.sbuf_tensor("H0", [P, TILES, D], F32))
        XPA = ctx.enter_context(nc.sbuf_tensor("XPA", [P, TILES, D + 2 * HEADS], F32))
        layer_norm_relu(nc, g, "ln0", H)
        with ExitStack() as c2:
            def sb(n, shape):
                return c2.enter_context(nc.sbuf_tensor("g0_" + n, shape, F32))
            W = sb("W", [D, D + 2 * HEADS])
            WT = sb("WT", [D, D])
            att = sb("att", [D, 2])
            first = sb("first", [P, HEADS])
            mask = sb("mask", [P, HEADS])
            AB = sb("AB", [P, 2 * HEADS])
            PW = c2.enter_context(nc.psum_tensor("g0_PW", [P, 2, 512], F32))
            loaded = sem("g0_loaded")
            turned = sem("g0_turned")
            ab_done = sem("g0_ab_done")
            with nc.Block() as block:
                @block.sync
                def _(sp):
                    sp.dma_start(W[:, 0:D], w["L0_gnn_W"]).then_inc(loaded, 16)
                    sp.dma_start(att[:, 0:1], w["L0_gnn_att_src"].rearrange("h (f o) -> (h f) o", o=1)).then_inc(loaded, 16)
                    sp.dma_start(att[:, 1:2], w["L0_gnn_att_dst"].rearrange("h (f o) -> (h f) o", o=1)).then_inc(loaded, 16)

                @block.tensor
                def _(pe):
                    pe.wait_ge(loaded, 48)
                    nc.tensor.transpose(PW[:, 0, 0:D], W[:, 0:D], g["eye"][:]).then_inc(turned, 1)
                    pe.wait_ge(ab_done, 5)
                    nc.tensor.matmul(PW[:, 1, 0:2 * HEADS], WT[:], AB[:], start=True, stop=True).then_inc(turned, 1)

                @block.vector
                def _(dve):
                    V = nc.vector
                    c = Count(dve, ab_done, 0)
                    dve.wait_ge(loaded, 48)
                    dve.wait_ge(turned, 1)
                    c.then(V.tensor_copy(WT[:], PW[:, 0, 0:D]))
                    c.then(V.tensor_scalar(first[:], g["iota_row"][:, 0:HEADS], -float(HF), g["iota_col"][:], ALU.mult, ALU.add))
                    c.then(V.tensor_scalar(mask[:], first[:], 0.0, None, ALU.is_ge))
                    c.then(V.scalar_tensor_tensor(mask[:], first[:], float(HF), mask[:], ALU.is_lt, ALU.mult))
                    V.tensor_scalar(AB[:, 0:HEADS], mask[:], att[:, 0:1], None, ALU.mult)
                    c.then(V.tensor_scalar(AB[:, HEADS:2 * HEADS], mask[:], att[:, 1:2], None, ALU.mult))
                    dve.wait_ge(turned, 2)
                    c.then(V.tensor_copy(W[:, D:D + 2 * HEADS], PW[:, 1, 0:2 * HEADS]))
            node_matmul(nc, g, "nm0", H, W[:], D + 2 * HEADS,
                        lambda dve, t, m, ps, i, k: nc.vector.tensor_copy(XPA[:, bass.ds(t, m), :], ps))
        store_table(nc, "st0", g["tab0"], XPA[:, :, 0:D + HEADS])
        ACC = ctx.enter_context(nc.sbuf_tensor("ACC0", [P, TILES, D + 2 * HEADS + 1], F32))
        softmax_pass(nc, g, "e0_", HEADS, g["tab0"], XPA[:, :, D + HEADS:D + 2 * HEADS], HEADS, ACC)
        U = ctx.enter_context(nc.sbuf_tensor("U0", [P, TILES, D], F32))
        with ExitStack() as c2:
            def sb(n, shape):
                return c2.enter_context(nc.sbuf_tensor("f0_" + n, shape, F32))
            bias = sb("bias", [P, D])
            none = sb("none", [P, TILES])
            es = sb("es", [P, TILES, HEADS])
            mx = sb("mx", [P, TILES, HEADS])
            r = sb("r", [P, TILES, HEADS])
            loaded = sem("f0_loaded")
            chain = sem("f0_chain")
            exps = sem("f0_exps")
            with nc.Block() as block:
                @block.sync
                def _(sp):
                    sp.dma_start(bias[:], w["L0_gnn_bias"].partition_broadcast(P)).then_inc(loaded, 16)

                @block.scalar
                def _(act):
                    act.wait_ge(chain, 8)
                    nc.scalar.activation(r[:], r[:], ACT.Exp).then_inc(exps, 1)
                    nc.scalar.activation(es[:], es[:], ACT.Exp).then_inc(exps, 1)

                @block.vector
                def _(dve):
                    V = nc.vector
                    c = Count(dve, chain, 0)
                    th = [P, TILES, HEADS]
                    den, big = ACC[:, :, D:D + HEADS], ACC[:, :, D + HEADS:D + 2 * HEADS]
                    c.then(V.tensor_scalar(none[:], ACC[:, :, D + 2 * HEADS], -1.0, BIG, ALU.add, ALU.mult))
                    c.then(V.tensor_tensor(r[:], big, none[:].unsqueeze(2).to_broadcast(th), ALU.add))
                    c.then(V.tensor_tensor(es[:], XPA[:, :, D:D + HEADS], XPA[:, :, D + HEADS:], ALU.add))
                    c.then(V.tensor_scalar(mx[:], es[:], SLOPE, None, ALU.mult))
                    c.then(V.tensor_tensor(es[:], es[:], mx[:], ALU.max))
                    c.then(V.tensor_tensor(mx[:], r[:], es[:], ALU.max))
                    c.then(V.tensor_tensor(r[:], r[:], mx[:], ALU.subtract))
                    c.then(V.tensor_tensor(es[:], es[:], mx[:], ALU.subtract))
                    dve.wait_ge(exps, 2)
                    c.then(V.tensor_tensor(mx[:], den, r[:], ALU.mult))
                    c.then(V.scalar_tensor_tensor(mx[:], mx[:], SOFTMAX_EPS, es[:], ALU.add, ALU.add))
                    c.then(V.reciprocal(mx[:], mx[:]))
                    c.then(V.tensor_tensor(r[:], r[:], mx[:], ALU.mult))
                    c.then(V.tensor_tensor(es[:], es[:], mx[:], ALU.mult))
                    for h in range(HEADS):
                        cols = slice(h * HF, (h + 1) * HF)
                        wide = [P, TILES, HF]
                        V.tensor_tensor(U[:, :, cols], ACC[:, :, cols], r[:, :, h:h + 1].to_broadcast(wide), ALU.mult)
                        ins = V.tensor_tensor(XPA[:, :, cols], XPA[:, :, cols], es[:, :, h:h + 1].to_broadcast(wide), ALU.mult)
                    c.then(ins)
                    c.then(V.tensor_tensor(U[:], U[:], XPA[:, :, 0:D], ALU.add))
                    dve.wait_ge(loaded, 16)
                    c.then(V.tensor_tensor(U[:], U[:], per_feature(bias[:]), ALU.add))
        batch_norm(nc, g, "bn0", U, H, w["L0_gnn_bn_gamma"], w["L0_gnn_bn_beta"])
        sem.clear()


def store_table(nc, name, table, rows):
    with ExitStack() as ctx:
        sem = Semaphores(nc, ctx, name)
        stored = sem("_stored")
        with nc.Block() as block:
            @block.sync
            def _(sp):
                sp.dma_start(table.rearrange("(t p) d -> p t d", p=P), rows).then_inc(stored, 16)
                sp.wait_ge(stored, 16)
        sem.clear()


def layer_gcn(nc, g, w):
    with ExitStack() as ctx:
        sem = Semaphores(nc, ctx, "")
        H = ctx.enter_context(nc.sbuf_tensor("H1", [P, TILES, D], F32))
        layer_norm_relu(nc, g, "ln1", H)
        with ExitStack() as c2:
            T = c2.enter_context(nc.sbuf_tensor("T1", [P, TILES, D], F32))
            scaled = sem("scaled1")
            with nc.Block() as block:
                @block.vector
                def _(dve):
                    nc.vector.tensor_tensor(T[:], H[:], per_tile(g["rs_out"][:]), ALU.mult).then_inc(scaled, 1)
                    dve.wait_ge(scaled, 1)
            store_table(nc, "st1", g["tab1"], T[:])
        ACC = ctx.enter_context(nc.sbuf_tensor("ACC1", [P, TILES, D + 1], F32))
        sum_pass(nc, g, g["tab1"], ACC)
        U = ctx.enter_context(nc.sbuf_tensor("U1", [P, TILES, D], F32))
        W = ctx.enter_context(nc.sbuf_tensor("W1", [D, D], F32))
        bias = ctx.enter_context(nc.sbuf_tensor("b1", [P, D], F32))
        rs_in = ctx.enter_context(nc.sbuf_tensor("rs_in", [P, TILES], F32))
        chain = sem("chain1")
        with nc.Block() as block:
            @block.gpsimd
            def _(pool):
                pool.wait_ge(chain, 2)
                pool.tensor_tensor(rs_in[:], rs_in[:], g["mhalf"][:, 0:TILES], ALU.pow).then_inc(chain, 1)

            @block.vector
            def _(dve):
                V = nc.vector
                c = Count(dve, chain, 0)
                c.then(V.tensor_copy(g["cnt"][:], ACC[:, :, D]))
                c.then(V.tensor_scalar(rs_in[:], ACC[:, :, D], 1.0, None, ALU.max))
                dve.wait_ge(chain, 3)
                c.n = 3
                c.then(V.tensor_tensor(ACC[:, :, 0:D], ACC[:, :, 0:D], per_tile(rs_in[:]), ALU.mult))
        node_matmul(nc, g, "nm1", ACC[:, :, 0:D], W[:], D,
                    lambda dve, t, m, ps, i, k: nc.vector.tensor_tensor(U[:, bass.ds(t, m), :], ps, per_feature(bias[:], m), ALU.add),
                    loads=((W[:], w["L1_gnn_W"]), (bias[:], w["L1_gnn_b"].partition_broadcast(P))))
        batch_norm(nc, g, "bn1", U, H, w["L1_gnn_gamma"], w["L1_gnn_beta"])
        sem.clear()


def layer_pna(nc, g, w):
    with ExitStack() as ctx:
        sem = Semaphores(nc, ctx, "")
        with ExitStack() as c2:
            H = c2.enter_context(nc.sbuf_tensor("H2", [P, TILES, D], F32))
            B = c2.enter_context(nc.sbuf_tensor("B2", [P, TILES, D], F32))
            W = c2.enter_context(nc.sbuf_tensor("W2s", [D, D], F32))
            layer_norm_relu(nc, g, "ln2", H)
            store_table(nc, "sth2", g["h2"], H[:])
            node_matmul(nc, g, "nm2", H, W[:], D,
                        lambda dve, t, m, ps, i, k: nc.vector.tensor_copy(B[:, bass.ds(t, m), :], ps),
                        loads=((W[:], w["L2_gnn_W_pre"][D:2 * D, :]),))
            store_table(nc, "st2", g["tab2"], B[:])
        ACC = ctx.enter_context(nc.sbuf_tensor("ACC2", [P, TILES, 4 * D], F32))
        moments_pass(nc, g, g["tab2"], ACC)
        mean, low, high, sq = (ACC[:, :, i * D:(i + 1) * D] for i in range(4))
        H = ctx.enter_context(nc.sbuf_tensor("H2b", [P, TILES, D], F32))
        s1 = ctx.enter_context(nc.sbuf_tensor("s1", [P, TILES], F32))
        s2 = ctx.enter_context(nc.sbuf_tensor("s2", [P, TILES], F32))
        has = ctx.enter_context(nc.sbuf_tensor("has", [P, TILES], F32))
        with ExitStack() as c2:
            T = c2.enter_context(nc.sbuf_tensor("T2", [P, TILES, D], F32))
            rd = c2.enter_context(nc.sbuf_tensor("rd", [P, TILES], F32))
            W = c2.enter_context(nc.sbuf_tensor("W2d", [D, D], F32))
            bias = c2.enter_context(nc.sbuf_tensor("b2", [P, D], F32))
            TAS = c2.enter_context(nc.sbuf_tensor("TA", [P, 2, 4, D], F32))
            chain = sem("chain2")
            logs = sem("logs2")
            h_in = sem("h_in2")
            evac = sem("evac2")
            with nc.Block() as block:
                @block.sync
                def _(sp):
                    sp.dma_start(H[:], g["h2"].rearrange("(t p) d -> p t d", p=P)).then_inc(h_in, 16)

                @block.scalar
                def _(act):
                    act.wait_ge(chain, 1)
                    nc.scalar.activation(s2[:], rd[:], ACT.Ln, bias=g["ones"][:, 0:1]).then_inc(logs, 1)
                    act.wait_ge(chain, 4)
                    nc.scalar.activation(T[:], mean, ACT.Square).then_inc(logs, 1)
                    act.wait_ge(chain, 9)
                    nc.scalar.activation(sq, sq, ACT.Sqrt).then_inc(logs, 1)
                    act.wait_ge(logs, 3)

                @block.vector
                def _(dve):
                    V = nc.vector
                    c = Count(dve, chain, 0)
                    c.then(V.tensor_scalar(rd[:], g["cnt"][:], 1.0, None, ALU.max))
                    c.then(V.tensor_scalar(has[:], g["cnt"][:], 0.0, None, ALU.is_gt))
                    dve.wait_ge(logs, 1)
                    c.then(V.reciprocal(rd[:], rd[:]))
                    c.then(V.tensor_tensor(mean, mean, per_tile(rd[:]), ALU.mult))
                    c.then(V.tensor_scalar(s1[:], s2[:], 1.0 / AVG_LOG, None, ALU.mult))
                    c.then(V.reciprocal(s2[:], s1[:]))
                    c.then(V.tensor_tensor(sq, sq, per_tile(rd[:]), ALU.mult))
                    dve.wait_ge(logs, 2)
                    c.then(V.tensor_tensor(sq, sq, T[:], ALU.subtract))
                    c.then(V.tensor_scalar(sq, sq, 0.0, STD_EPS, ALU.max, ALU.add))
                    dve.wait_ge(h_in, 16)

            def own_part(dve, t, m, ps, i, k):
                V = nc.vector
                TA = TAS[:, k]
                c = Count(dve, evac, 2 * (2 * i + k))
                c.then(V.tensor_tensor(TA[:, 0:m, :], ps, per_feature(bias[:], m), ALU.add))
                c.then(V.tensor_tensor(TA[:, 0:m, :], TA[:, 0:m, :], has[:, bass.ds(t, m)].unsqueeze(2).to_broadcast([P, m, D]), ALU.mult))
                for part in (mean, low, high):
                    dst = part[:, bass.ds(t, m), :]
                    ins = V.tensor_tensor(dst, dst, TA[:, 0:m, :], ALU.add)
                return ins

            node_matmul(nc, g, "nm2b", H, W[:], D, own_part,
                        loads=((W[:], w["L2_gnn_W_pre"][0:D, :]), (bias[:], w["L2_gnn_b_pre"].partition_broadcast(P))))
        post_matmul(nc, g, w, ACC, H, s1, s2, mean)
        batch_norm(nc, g, "bn2", mean, H, w["L2_gnn_gamma"], w["L2_gnn_beta"])
        sem.clear()


def post_matmul(nc, g, w, ACC, H, s1, s2, U):
    PARTS = 13
    with ExitStack() as ctx:
        def sb(n, shape):
            return ctx.enter_context(nc.sbuf_tensor("p_" + n, shape, F32))

        sem = Semaphores(nc, ctx, "")

        WF = sb("WF", [P, PARTS, D])
        BIAS = sb("BIAS", [P, D])
        with ExitStack() as c2:
            WP = c2.enter_context(nc.sbuf_tensor("p_WP", [P, PARTS, D], F32))
            WL = c2.enter_context(nc.sbuf_tensor("p_WL", [P, D], F32))
            WPT = c2.enter_context(nc.sbuf_tensor("p_WPT", [P, 2, P], F32))
            PT = c2.enter_context(nc.psum_tensor("p_PT", [P, 2, 512], F32))
            PF = c2.enter_context(nc.psum_tensor("p_PF", [P, 2, 512], F32))
            bp = c2.enter_context(nc.sbuf_tensor("p_bp", [P, 1], F32))
            bl = c2.enter_context(nc.sbuf_tensor("p_bl", [P, D], F32))
            bpr = c2.enter_context(nc.sbuf_tensor("p_bpr", [P, P], F32))
            loaded = sem("p_loaded")
            turned = sem("p_turned")
            turned_in = sem("p_turned_in")
            fused = sem("p_fused")
            fused_in = sem("p_fused_in")
            bias_rep = sem("p_bias_rep")
            with nc.Block() as block:
                @block.sync
                def _(sp):
                    sp.dma_start(WP[:], w["L2_gnn_W_post"].rearrange("(k p) d -> p k d", p=P)).then_inc(loaded, 16)
                    sp.dma_start(WL[:], w["L2_gnn_W_lin"]).then_inc(loaded, 16)
                    sp.dma_start(bp[:], w["L2_gnn_b_post"].unsqueeze(1)).then_inc(loaded, 16)
                    sp.dma_start(bl[:], w["L2_gnn_b_lin"].partition_broadcast(P)).then_inc(loaded, 16)

                @block.tensor
                def _(pe):
                    pe.wait_ge(loaded, 64)
                    for k in range(PARTS + 1):
                        if k < PARTS:
                            wait(pe, turned_in, k - 1)
                            nc.tensor.transpose(PT[:, k % 2, 0:P], WP[:, k, :], g["eye"][:]).then_inc(turned, 1)
                        if k >= 1:
                            pe.wait_ge(turned_in, k)
                            wait(pe, fused_in, k - 2)
                            nc.tensor.matmul(PF[:, (k - 1) % 2, 0:D], WPT[:, (k - 1) % 2, :], WL[:], start=True, stop=True).then_inc(fused, 1)
                    pe.wait_ge(bias_rep, 1)
                    pe.wait_ge(fused_in, PARTS)
                    nc.tensor.matmul(PF[:, 0, 0:D], bpr[:], WL[:], start=True, stop=True).then_inc(fused, 1)

                @block.scalar
                def _(act):
                    for k in range(PARTS):
                        act.wait_ge(turned, k + 1)
                        wait(act, fused, k - 1)
                        nc.scalar.copy(WPT[:, k % 2, :], PT[:, k % 2, 0:P]).then_inc(turned_in, 1)

                @block.vector
                def _(dve):
                    V = nc.vector
                    dve.wait_ge(loaded, 64)
                    V.tensor_scalar(bpr[:], g["ones"][:], bp[:], None, ALU.mult).then_inc(bias_rep, 1)
                    for k in range(PARTS):
                        dve.wait_ge(fused, k + 1)
                        V.tensor_copy(WF[:, k, :], PF[:, k % 2, 0:D]).then_inc(fused_in, 1)
                    dve.wait_ge(fused, PARTS + 1)
                    V.tensor_tensor(BIAS[:], PF[:, 0, 0:D], bl[:], ALU.add).then_inc(fused_in, 1)
                    dve.wait_ge(fused_in, PARTS + 1)
        SG = sb("SG", [P, 2, 5, D])
        HT = sb("HT", [P, 2, 5, P])
        T = sb("T", [P, 2, D])
        TP = ctx.enter_context(nc.psum_tensor("p_TP", [P, 2, 2, 512], F32))
        OP = ctx.enter_context(nc.psum_tensor("p_OP", [P, 2, 512], F32))
        staged = sem("p_staged")
        stood = sem("p_stood")
        turned = sem("p_turned2")
        ht_in = sem("p_ht_in")
        product = sem("p_product")
        chain = sem("p_chain")

        def in_pairs(eng, body):
            body(0, 0)
            body(1, 1)
            with eng.Fori(1, TILES // 2) as i:
                body(2 * i, 0)
                body(2 * i + 1, 1)
            body(TILES - 1, 0)

        with nc.Block() as block:
            @block.gpsimd
            def _(pool):
                def body(t, b):
                    wait_alone(pool, turned, t - 1, stood)
                    pool.tensor_copy(SG[:, b, 0:4, :], ACC[:, bass.ds(t, 1), :].rearrange("p o (a d) -> p (o a) d", a=4))
                    pool.tensor_copy(SG[:, b, 4:5, :], H[:, bass.ds(t, 1), :]).then_inc(staged, 1)
                in_pairs(pool, body)

            @block.tensor
            def _(pe):
                def turn(t, b):
                    pe.wait_ge(staged, t + 1)
                    wait(pe, ht_in, t - 1)
                    for a in range(5):
                        ins = nc.tensor.transpose(TP[:, b, a // 4, (a % 4) * P:(a % 4 + 1) * P], SG[:, b, a, :], g["eye"][:])
                    ins.then_inc(turned, 1)

                def multiply(t, b):
                    pe.wait_ge(ht_in, t + 1)
                    wait(pe, chain, 3 * (t - 1))
                    for a in range(4):
                        nc.tensor.matmul(OP[:, b, 0:3 * D].rearrange("p (r d) -> p r d", r=3), HT[:, b, a, :],
                                         WF[:, 1 + a:PARTS:4, :], start=(a == 0), stop=False)
                    nc.tensor.matmul(OP[:, b, 0:D], HT[:, b, 4, :], WF[:, 0, :], start=False, stop=True).then_inc(product, 1)

                def body(t, b):
                    turn(t, b)
                    if not (isinstance(t, int) and t == 0):
                        multiply(t - 1, 1 - b)
                in_pairs(pe, body)
                multiply(TILES - 1, 0)

            @block.scalar
            def _(act):
                def body(t, b):
                    wait_alone(act, turned, t + 1, stood)
                    wait_alone(act, product, t - 1, stood)
                    nc.scalar.copy(HT[:, b, 0:4, :], TP[:, b, 0, :].rearrange("p (a n) -> p a n", a=4))
                    nc.scalar.copy(HT[:, b, 4, :], TP[:, b, 1, 0:P]).then_inc(ht_in, 1)
                in_pairs(act, body)

            @block.vector
            def _(dve):
                V = nc.vector

                def body(t, b):
                    c = Count(dve, chain, 3 * t)
                    dve.wait_ge(product, t + 1)
                    c.then(V.tensor_tensor(T[:, b], OP[:, b, 0:D], BIAS[:], ALU.add))
                    c.then(V.scalar_tensor_tensor(T[:, b], OP[:, b, D:2 * D], s1[:, bass.ds(t, 1)], T[:, b], ALU.mult, ALU.add))
                    c.then(V.scalar_tensor_tensor(U[:, bass.ds(t, 1), :].rearrange("p o d -> p (o d)"), OP[:, b, 2 * D:3 * D],
                                                  s2[:, bass.ds(t, 1)], T[:, b], ALU.mult, ALU.add))
                in_pairs(dve, body)
        sem.clear()


def layer_gatv2(nc, g, w, out):
    with ExitStack() as ctx:
        sem = Semaphores(nc, ctx, "")
        XLR = ctx.enter_context(nc.sbuf_tensor("XLR", [P, TILES, 2 * D], F32))
        with ExitStack() as c2:
            H = c2.enter_context(nc.sbuf_tensor("H3", [P, TILES, D], F32))
            W = c2.enter_context(nc.sbuf_tensor("W3", [D, 2 * D], F32))
            bias = c2.enter_context(nc.sbuf_tensor("b3", [P, 2 * D], F32))
            layer_norm_relu(nc, g, "ln3", H)
            node_matmul(nc, g, "nm3", H, W[:], 2 * D,
                        lambda dve, t, m, ps, i, k: nc.vector.tensor_tensor(XLR[:, bass.ds(t, m), :], ps, per_feature(bias[:], m), ALU.add),
                        loads=((W[:, 0:D], w["L3_gnn_W_l"]), (W[:, D:2 * D], w["L3_gnn_W_r"]),
                               (bias[:, 0:D], w["L3_gnn_b_l"].partition_broadcast(P)),
                               (bias[:, D:2 * D], w["L3_gnn_b_r"].partition_broadcast(P))))
        att = ctx.enter_context(nc.sbuf_tensor("att3", [P, D], F32))
        bias = ctx.enter_context(nc.sbuf_tensor("bias3", [P, D], F32))
        loaded = sem("loaded3")
        with nc.Block() as block:
            @block.sync
            def _(sp):
                sp.dma_start(att[:], w["L3_gnn_att"].partition_broadcast(P)).then_inc(loaded, 16)
                sp.dma_start(bias[:], w["L3_gnn_bias"].partition_broadcast(P)).then_inc(loaded, 16)
                sp.wait_ge(loaded, 32)
        store_table(nc, "st3", g["tab3"], XLR[:, :, 0:D])
        ACC = ctx.enter_context(nc.sbuf_tensor("ACC3", [P, TILES, D + 1], F32))
        softmax_pass(nc, g, "e3_", 1, g["tab3"], XLR[:, :, D:2 * D], D, ACC, att=att)
        rd = ctx.enter_context(nc.sbuf_tensor("rd3", [P, TILES], F32))
        chain = sem("chain3")
        stored = sem("out_stored")
        with nc.Block() as block:
            @block.vector
            def _(dve):
                V = nc.vector
                c = Count(dve, chain, 0)
                rows = ACC[:, :, 0:D]
                c.then(V.tensor_scalar(rd[:], ACC[:, :, D], SOFTMAX_EPS, None, ALU.add))
                c.then(V.reciprocal(rd[:], rd[:]))
                c.then(V.tensor_tensor(rows, rows, per_tile(rd[:]), ALU.mult))
                c.then(V.tensor_tensor(rows, rows, per_feature(bias[:]), ALU.add))
                c.then(V.scalar_tensor_tensor(g["X"][:], rows, 0.0, g["X"][:], ALU.max, ALU.add))

            @block.sync
            def _(sp):
                sp.wait_ge(chain, 5)
                whole = (TILES - 1) * P
                sp.dma_start(out[0:whole, :].rearrange("(t p) d -> p t d", p=P), g["X"][:, 0:TILES - 1, :]).then_inc(stored, 16)
                sp.dma_start(out[whole:N, :], g["X"][0:LAST, TILES - 1, :]).then_inc(stored, 16)
                sp.wait_ge(stored, 32)


def gnn_kernel(nc, w, out):
    with ExitStack() as ctx:
        g = whole_program_tensors(nc, ctx)
        build_steps(nc, g, w["src"], w["dst"])
        with ExitStack() as c2:
            sem = Semaphores(nc, c2, "")
            x_in = sem("x_in")
            padded = sem("padded")
            with nc.Block() as block:
                @block.gpsimd
                def _(pool):
                    pool.memset(g["X"][:, TILES - 1, :], 0.0).then_inc(padded, 1)

                @block.sync
                def _(sp):
                    whole = (TILES - 1) * P
                    sp.dma_start(g["X"][:, 0:TILES - 1, :], w["x"][0:whole, :].rearrange("(t p) d -> p t d", p=P)).then_inc(x_in, 16)
                    sp.wait_ge(padded, 1)
                    sp.dma_start(g["X"][0:LAST, TILES - 1, :], w["x"][whole:N, :]).then_inc(x_in, 16)
                    sp.wait_ge(x_in, 32)
            sem.clear()
        layer_gat(nc, g, w)
        layer_gcn(nc, g, w)
        layer_pna(nc, g, w)
        layer_gatv2(nc, g, w, out)


_INS = ['x', 'src', 'dst', 'L0_gnn_W', 'L0_gnn_att_src', 'L0_gnn_att_dst', 'L0_gnn_bias', 'L0_gnn_bn_gamma',
        'L0_gnn_bn_beta', 'L1_gnn_W', 'L1_gnn_b', 'L1_gnn_gamma', 'L1_gnn_beta', 'L2_gnn_W_pre', 'L2_gnn_b_pre',
        'L2_gnn_W_post', 'L2_gnn_b_post', 'L2_gnn_W_lin', 'L2_gnn_b_lin', 'L2_gnn_gamma', 'L2_gnn_beta',
        'L3_gnn_W_l', 'L3_gnn_b_l', 'L3_gnn_W_r', 'L3_gnn_b_r', 'L3_gnn_att', 'L3_gnn_bias']


def kernel(**inputs):
    import numpy as _np
    import concourse.bacc as _bacc
    from concourse.bass_utils import run_bass_kernel_spmd as _run

    nc = _bacc.Bacc("TRN2", target_bir_lowering=False, num_devices=1)
    arrays, args = {}, {}
    for name in _INS:
        a = _np.ascontiguousarray(inputs[name])
        arrays[f"in_{name}_dram"] = a
        args[name] = nc.dram_tensor(f"in_{name}_dram", a.shape, mybir.dt.from_np(a.dtype), kind="ExternalInput").ap()
    out = nc.dram_tensor("out_dram", (N, D), F32, kind="ExternalOutput").ap()
    gnn_kernel(nc, args, out)
    r = _run(nc, [arrays], core_ids=[0])
    return r.results[0]["out_dram"]
```

```python
import concourse.bass as bass
from concourse import mybir
from contextlib import ExitStack
import math

F32, I32, BF16 = mybir.dt.float32, mybir.dt.int32, mybir.dt.bfloat16
ALU, ACT, AX = mybir.AluOpType, mybir.ActivationFunctionType, mybir.AxisListType

P = 128
D = 128
N = 6250
E = 100000
TILES = -(-N // P)
LAST = N - (TILES - 1) * P
CHUNKS = -(-E // P)
FULL = E // P
TAIL = E - FULL * P
GROUP = 8
GROUPS = -(-(CHUNKS + TILES - 1) // GROUP)
STEPS = GROUPS * GROUP
IT = -(-(STEPS + GROUP) // P)
SPAD = IT * P
SLOTS = GROUP * P
BIG = 1e38
HEADS, HF = 8, 16
LN_EPS = BN_EPS = STD_EPS = 1e-5
SOFTMAX_EPS = 1e-16
SLOPE = 0.2
AVG_LOG = math.log(17.0)
TG = 7
NG = TILES // TG


def whole_program_tensors(nc, ctx):
    g = {}

    def sb(name, shape, dt):
        g[name] = ctx.enter_context(nc.sbuf_tensor(name, shape, dt))

    g["gathered"] = [ctx.enter_context(nc.semaphore(f"gathered{b}")) for b in range(4)]
    g["rows_gathered"] = [16 * IT, 0, 0, 0]
    sb("eye", [P, P], F32)
    sb("iota_row", [P, P], F32)
    sb("iota_col", [P, 1], F32)
    sb("ones", [P, P], F32)
    sb("mhalf", [P, P], F32)
    sb("loc", [P, SPAD], F32)
    sb("loc_end", [P, SPAD], F32)
    sb("src_idx", [P, SPAD], I32)
    sb("tile_row", [1, SPAD], I32)
    sb("rs_out", [P, TILES], F32)
    sb("cnt", [P, TILES], F32)
    sb("X", [P, TILES, D], F32)
    for name, shape, dt in (
        ("step_rows", (CHUNKS + 2, 2 * P), I32),
        ("keys", (P + SPAD * P + P,), F32),
        ("row_loc", (SPAD * P,), BF16),
        ("row_start", (SPAD * P,), BF16),
        ("row_end", (SPAD * P,), BF16),
        ("tab0", (TILES * P, D + HEADS), F32),
        ("tab1", (TILES * P, D), F32),
        ("tab2", (TILES * P, D), F32),
        ("tab3", (TILES * P, D), F32),
        ("h2", (TILES * P, D), F32),
    ):
        g[name] = nc.dram_tensor("dr_" + name, shape, dt, kind="Internal").ap()
    return g


def wait(eng, sem, value):
    if isinstance(value, int) and value <= 0:
        return
    eng.wait_ge(sem, value)


def wait_alone(eng, sem, value, stood):
    if isinstance(value, int) and value <= 0:
        return
    eng.wait_ge(sem, value)
    if not isinstance(value, int):
        eng.sem_inc(stood, 1)


def in_groups_of_two(eng, body):
    body(0, 0, 0)
    body(1, 0, 1)
    with eng.Fori(1, GROUPS // 2) as i:
        body(2 * i, i, 0)
        body(2 * i + 1, i, 1)


def in_groups_of_four(eng, body):
    rounds = GROUPS // 4
    for b in range(4):
        body(b, 0, b)
    with eng.Fori(1, rounds - 1) as i:
        for b in range(4):
            body(4 * i + b, i, b)
    for b in range(4):
        body(4 * (rounds - 1) + b, rounds - 1, b)


def is_first(k):
    return isinstance(k, int) and k == 0


def is_last(k):
    return isinstance(k, int) and k == GROUPS - 1


def load_tiles(nc, engine, row, lo, n, top=TILES - 1):
    _, vals = nc.values_load_multi_w_load_instructions(
        row[0:1, bass.ds(lo, n)], engines=[engine], min_val=0, max_val=top,
        skip_runtime_bounds_check_because="the row is clamped to the last tile when it is built")
    return vals


class Semaphores:

    def __init__(self, nc, ctx, prefix):
        self.nc, self.ctx, self.prefix, self.all = nc, ctx, prefix, []

    def __call__(self, name):
        self.all.append(self.ctx.enter_context(self.nc.semaphore(self.prefix + name)))
        return self.all[-1]

    def clear(self):
        with self.nc.Block() as block:
            @block.sync
            def _(sp):
                for s in self.all:
                    sp.sem_clear(s)


def build_steps(nc, g, src, dst):
    with ExitStack() as ctx:
        def sb(name, shape, dt):
            return ctx.enter_context(nc.sbuf_tensor(name, shape, dt))

        sem = Semaphores(nc, ctx, "")

        last_dst = sb("last_dst", [P, IT], I32)
        tail = sb("tail", [3, 2 * P], I32)
        fin = sb("fin", [P, IT], F32)
        big = sb("big", [P, IT], F32)
        itmp = sb("itmp", [P, IT], I32)
        iota_p = sb("iota_p", [P, IT], F32)
        iota_s = sb("iota_s", [P, SPAD], F32)
        ints = sb("ints", [P, SPAD], I32)
        intp = sb("intp", [P, IT], I32)
        before = sb("before", [P, IT, SPAD], BF16)
        ones_bf = sb("ones_bf", [P, P], BF16)
        crep = sb("crep", [P, SPAD], F32)
        chunk_f = sb("chunk_f", [P, IT], F32)
        chunk_i = sb("chunk_i", [P, IT], I32)
        tile_c = sb("tile_c", [P, IT], F32)
        edges = sb("edges", [P, IT, 2 * P], I32)
        ef = sb("ef", [P, IT, 2 * P], F32)
        locp = sb("locp", [P, IT, P], F32)
        v = sb("v", [P, IT, P], F32)
        v2 = sb("v2", [P, IT, P], F32)
        key = sb("key", [P, IT, P], F32)
        kprev = sb("kprev", [P, IT, P], F32)
        knext = sb("knext", [P, IT, P], F32)
        padrow = sb("padrow", [1, P], F32)
        b_loc = sb("b_loc", [P, IT, P], BF16)
        b_start = sb("b_start", [P, IT, P], BF16)
        b_end = sb("b_end", [P, IT, P], BF16)
        lo_i = sb("lo_i", [P, SPAD], I32)
        hi_i = sb("hi_i", [P, SPAD], I32)
        lo_f = sb("lo_f", [P, SPAD], F32)
        hi_f = sb("hi_f", [P, SPAD], F32)
        eq_lo = sb("eq_lo", [P, 2, 16, P], BF16)
        eq_hi = sb("eq_hi", [P, 2, 16, TILES], BF16)
        deg = sb("deg", [P, TILES], F32)
        ps_c = ctx.enter_context(nc.psum_tensor("ps_c", [P, 2, 512], F32))
        ps_p = ctx.enter_context(nc.psum_tensor("ps_p", [P, 512], F32))
        ps_t = ctx.enter_context(nc.psum_tensor("ps_t", [P, 3, 512], F32))
        ps_h = ctx.enter_context(nc.psum_tensor("ps_h", [P, 2, 512], F32))
        HALF = SPAD // 2

        consts = sem("consts")
        setup = sem("setup")
        copied = sem("copied")
        tail_in = sem("tail_in")
        last_in = sem("last_in")
        v_done = sem("v_done")
        counted = sem("counted")
        gathered = g["gathered"][0]
        keys_out = sem("keys_out")
        near_in = sem("near_in")
        rows_out = sem("rows_out")
        turned = sem("turned")
        hist = sem("hist")
        added = sem("added")
        onehots = sem("onehots")

        with nc.Block() as block:
            @block.gpsimd
            def _(pool):
                pool.memset(g["eye"][:], 0.0).then_inc(setup, 1)
                pool.memset(g["ones"][:], 1.0).then_inc(setup, 1)
                pool.memset(ones_bf[:], 1.0).then_inc(setup, 1)
                pool.memset(g["mhalf"][:], -0.5).then_inc(setup, 1)
                pool.memset(tail[:, 0:P], 0).then_inc(setup, 1)
                pool.memset(tail[:, P:2 * P], -1).then_inc(setup, 1)
                pool.memset(last_dst[:], 0).then_inc(setup, 1)
                pool.memset(padrow[:], -1.0).then_inc(setup, 1)
                pool.iota(ints[:], pattern=[[1, SPAD]], base=0, channel_multiplier=0).then_inc(setup, 1)
                pool.iota(intp[:], pattern=[[P, IT]], base=0, channel_multiplier=1).then_inc(setup, 1)
                pool.wait_ge(setup, 10)
                pool.affine_select(out=g["eye"][:], in_=g["eye"][:], compare_op=ALU.not_equal, fill=1.0,
                                   base=0, pattern=[[-1, P]], channel_multiplier=1).then_inc(consts, 1)
                pool.wait_ge(copied, 16 * 3)
                pool.wait_ge(v_done, 7)
                for k in range(IT):
                    pool.indirect_dma_start(
                        out=edges[:, k, :], out_offset=None, in_=g["step_rows"][:, :],
                        in_offset=bass.IndirectOffsetOnAxis(ap=chunk_i[:, k:k + 1], axis=0)).then_inc(gathered, 16)

                pool.wait_ge(added, STEPS // 16 + 2)
                pool.tensor_tensor(g["rs_out"][:], deg[:], g["mhalf"][:, 0:TILES], ALU.pow).then_inc(added, 1)
                pool.wait_ge(added, STEPS // 16 + 3)

            @block.sync
            def _(sp):
                sp.dma_start(g["step_rows"][0:FULL, 0:P],
                             src[0:FULL * P].rearrange("(c e) -> c e", e=P)).then_inc(copied, 16)
                sp.dma_start(g["step_rows"][0:FULL, P:2 * P],
                             dst[0:FULL * P].rearrange("(c e) -> c e", e=P)).then_inc(copied, 16)
                sp.wait_ge(setup, 10)
                sp.dma_start(tail[0:1, 0:TAIL], src[FULL * P:E].unsqueeze(0)).then_inc(tail_in, 16)
                sp.dma_start(tail[0:1, P:P + TAIL], dst[FULL * P:E].unsqueeze(0)).then_inc(tail_in, 16)
                lasts = dst[0:FULL * P].rearrange("(c e) -> c e", e=P)[:, P - 1:P]
                whole = FULL // P
                sp.dma_start(last_dst[:, 0:whole],
                             lasts[0:whole * P, :].rearrange("(k p) o -> p (k o)", p=P),
                             allow_slow_non_contiguous=True).then_inc(last_in, 16)
                sp.dma_start(last_dst[0:FULL - whole * P, whole:whole + 1],
                             lasts[whole * P:FULL, :], allow_slow_non_contiguous=True).then_inc(last_in, 16)
                sp.dma_start(last_dst[FULL - whole * P:CHUNKS - whole * P, whole:whole + 1],
                             dst[E - 1:E].unsqueeze(0)).then_inc(last_in, 16)
                sp.wait_ge(tail_in, 32)
                sp.dma_start(g["step_rows"][FULL:FULL + 3, :], tail[:]).then_inc(copied, 16)
                body = g["keys"][P:P + SPAD * P].rearrange("(k p e) -> p k e", p=P, e=P)
                sp.wait_ge(v_done, 14)
                sp.dma_start(body, key[:]).then_inc(keys_out, 16)
                sp.dma_start(g["keys"][0:P].unsqueeze(0), padrow[:]).then_inc(keys_out, 16)
                sp.dma_start(g["keys"][P + SPAD * P:2 * P + SPAD * P].unsqueeze(0), padrow[:]).then_inc(keys_out, 16)
                sp.wait_ge(keys_out, 48)
                sp.dma_start(kprev[:], g["keys"][P - 1:P - 1 + SPAD * P].rearrange("(k p e) -> p k e", p=P, e=P)).then_inc(near_in, 16)
                sp.dma_start(knext[:], g["keys"][P + 1:P + 1 + SPAD * P].rearrange("(k p e) -> p k e", p=P, e=P)).then_inc(near_in, 16)
                sp.wait_ge(v_done, 20)
                for row, tile in (("row_loc", b_loc), ("row_start", b_start), ("row_end", b_end)):
                    sp.dma_start(g[row].rearrange("(k p e) -> p k e", p=P, e=P), tile[:]).then_inc(rows_out, 16)
                sp.wait_ge(rows_out, 48)

            @block.vector
            def _(dve):
                V = nc.vector
                n = [0]

                def step(ins):
                    n[0] += 1
                    ins.then_inc(v_done, 1)

                def then(ins):
                    step(ins)
                    dve.wait_ge(v_done, n[0])

                dve.wait_ge(setup, 10)
                V.tensor_copy(g["iota_row"][:], ints[:, 0:P]).then_inc(consts, 1)
                V.tensor_copy(iota_s[:], ints[:]).then_inc(consts, 1)
                V.tensor_copy(iota_p[:], intp[:]).then_inc(consts, 1)
                V.tensor_copy(g["iota_col"][:], intp[:, 0:1]).then_inc(consts, 1)
                dve.wait_ge(consts, 5)
                dve.wait_ge(last_in, 48)
                then(V.tensor_single_scalar(itmp[:], last_dst[:], 7, op=ALU.logical_shift_right))
                then(V.tensor_tensor(fin[:], itmp[:], iota_p[:], ALU.add))
                then(V.tensor_scalar(big[:], iota_p[:], float(CHUNKS), 1e6, ALU.is_ge, ALU.mult))
                then(V.tensor_tensor(fin[:], fin[:], big[:], ALU.max))
                for k in range(IT):
                    ins = V.tensor_scalar(before[:, k, :], iota_s[:], fin[:, k:k + 1], None, ALU.is_gt)
                step(ins)
                dve.wait_ge(counted, 1)
                then(V.tensor_copy(chunk_f[:], ps_p[:, 0:IT]))
                then(V.tensor_copy(chunk_i[:], chunk_f[:]))
                then(V.tensor_tensor(tile_c[:], iota_p[:], chunk_f[:], ALU.subtract))
                then(V.tensor_scalar(tile_c[:], tile_c[:], float(TILES - 1), float(P), ALU.min, ALU.mult))
                for h in range(2):
                    ins = V.tensor_copy(crep[:, h * HALF:(h + 1) * HALF], ps_c[:, h, 0:HALF])
                then(ins)
                then(V.tensor_tensor(crep[:], iota_s[:], crep[:], ALU.subtract))
                V.tensor_scalar(g["tile_row"][:], crep[0:1, :], float(TILES - 1), None, ALU.min).then_inc(consts, 1)
                dve.wait_ge(gathered, 16 * IT)
                then(V.tensor_copy(ef[:], edges[:]))
                V_tile = tile_c[:].unsqueeze(2).to_broadcast([P, IT, P])
                V.tensor_tensor(locp[:], ef[:, :, P:2 * P], V_tile, ALU.subtract).then_inc(turned, 1)
                dve.wait_ge(turned, 1)
                V.tensor_scalar(v[:], locp[:], 0.0, None, ALU.is_ge).then_inc(turned, 1)
                dve.wait_ge(turned, 2)
                V.scalar_tensor_tensor(v2[:], locp[:], float(P), v[:], ALU.is_lt, ALU.mult).then_inc(turned, 1)
                dve.wait_ge(turned, 3)
                then(V.scalar_tensor_tensor(locp[:], locp[:], 1.0, v2[:], ALU.add, ALU.mult))
                step(V.scalar_tensor_tensor(key[:], ef[:, :, P:2 * P], 1.0, v2[:], ALU.add, ALU.mult))
                step(V.tensor_scalar(b_loc[:], locp[:], -1.0, None, ALU.add))
                dve.wait_ge(near_in, 32)
                then(V.tensor_tensor(v[:], key[:], kprev[:], ALU.not_equal))
                step(V.tensor_scalar(b_start[:], v[:], -BIG, None, ALU.mult))
                then(V.tensor_tensor(v2[:], key[:], knext[:], ALU.not_equal))
                step(V.tensor_scalar(b_end[:], v2[:], -BIG, None, ALU.mult))
                then(V.tensor_tensor(key[:], locp[:], v2[:], ALU.mult))
                for k in range(IT):
                    dve.wait_ge(counted, 2 + k)
                    cols = slice(k * P, (k + 1) * P)
                    V.tensor_scalar(g["loc"][:, cols], ps_t[:, 0, 0:P], -1.0, None, ALU.add)
                    V.tensor_scalar(g["loc_end"][:, cols], ps_t[:, 1, 0:P], -1.0, None, ALU.add)
                    ins = V.tensor_copy(g["src_idx"][:, cols], ps_t[:, 2, 0:P])
                    then(ins)
                then(V.tensor_single_scalar(lo_i[:], g["src_idx"][:], P - 1, op=ALU.bitwise_and))
                then(V.tensor_single_scalar(hi_i[:], g["src_idx"][:], 7, op=ALU.logical_shift_right))
                then(V.tensor_copy(lo_f[:], lo_i[:]))
                then(V.tensor_copy(hi_f[:], hi_i[:]))
                then(V.tensor_scalar(crep[:], g["loc"][:], 0.0, None, ALU.is_ge))
                then(V.scalar_tensor_tensor(hi_f[:], hi_f[:], 1.0, crep[:], ALU.add, ALU.mult))
                then(V.tensor_scalar(hi_f[:], hi_f[:], -1.0, None, ALU.add))
                V.memset(deg[:], 0.0).then_inc(added, 1)

                def onehot(i, b):
                    a = iota_bc(16, P)
                    V.tensor_tensor(eq_lo[:, b], a, lo_f[:, bass.ds(i * 16, 16)].unsqueeze(2).to_broadcast([P, 16, P]),
                                    ALU.is_equal).then_inc(onehots, 1)
                    V.tensor_tensor(eq_hi[:, b], iota_bc(16, TILES),
                                    hi_f[:, bass.ds(i * 16, 16)].unsqueeze(2).to_broadcast([P, 16, TILES]),
                                    ALU.is_equal).then_inc(onehots, 1)

                def iota_bc(m, w):
                    return g["iota_row"][:, 0:w].unsqueeze(1).to_broadcast([P, m, w])

                onehot(0, 0)
                onehot(1, 1)
                with dve.Fori(1, STEPS // 32) as i:
                    for b in range(2):
                        dve.wait_ge(hist, 2 * i + b - 1)
                        dve.wait_ge(added, 2 * i + b - 1)
                        V.tensor_tensor(deg[:], deg[:], ps_h[:, b, 0:TILES], ALU.add).then_inc(added, 1)
                        onehot(2 * i + b, b)
                for b in range(2):
                    dve.wait_ge(hist, STEPS // 16 - 1 + b)
                    dve.wait_ge(added, STEPS // 16 - 1 + b)
                    V.tensor_tensor(deg[:], deg[:], ps_h[:, b, 0:TILES], ALU.add).then_inc(added, 1)
                dve.wait_ge(added, STEPS // 16 + 1)
                V.tensor_scalar(deg[:], deg[:], 1.0, None, ALU.max).then_inc(added, 1)

            @block.tensor
            def _(pe):
                pe.wait_ge(v_done, 5)
                for h in range(2):
                    for k in range(IT):
                        nc.tensor.matmul(ps_c[:, h, 0:HALF], ones_bf[:], before[:, k, h * HALF:(h + 1) * HALF],
                                         start=(k == 0), stop=(k == IT - 1))
                for s in range(IT):
                    for k in range(IT):
                        ins = nc.tensor.matmul(ps_p[:, s:s + 1], before[:, k, s * P:(s + 1) * P], ones_bf[:, 0:1],
                                               start=(k == 0), stop=(k == IT - 1))
                ins.then_inc(counted, 1)
                pe.wait_ge(consts, 1)
                pe.wait_ge(v_done, 20)
                for k in range(IT):
                    if k:
                        pe.wait_ge(v_done, 20 + k)
                    for j, m in enumerate((locp[:, k, :], key[:, k, :], ef[:, k, 0:P])):
                        ins = nc.tensor.transpose(ps_t[:, j, 0:P], m, g["eye"][:])
                    ins.then_inc(counted, 1)

                def count(i, b, waits):
                    pe.wait_ge(onehots, waits)
                    for s in range(16):
                        ins = nc.tensor.matmul(ps_h[:, b, 0:TILES], eq_lo[:, b, s, :], eq_hi[:, b, s, :],
                                               start=(s == 0), stop=(s == 15))
                    ins.then_inc(hist, 1)

                count(0, 0, 2)
                count(1, 1, 4)
                with pe.Fori(1, STEPS // 32) as i:
                    for b in range(2):
                        count(i, b, 2 * (2 * i + b + 1))
        sem.clear()


def per_tile(v):
    return v.unsqueeze(2).to_broadcast([P, TILES, D])


def per_feature(v, tiles=TILES):
    return v.unsqueeze(1).to_broadcast([P, tiles, v.shape[1]])


def layer_norm_relu(nc, g, name, H):
    with ExitStack() as ctx:
        sem = Semaphores(nc, ctx, name)
        SQ = ctx.enter_context(nc.sbuf_tensor(name + "_sq", [P, TILES, D], F32))
        mean = ctx.enter_context(nc.sbuf_tensor(name + "_mean", [P, TILES], F32))
        var = ctx.enter_context(nc.sbuf_tensor(name + "_var", [P, TILES], F32))
        centred = sem("_centred")
        squared = sem("_squared")
        stat = sem("_stat")
        with nc.Block() as block:
            @block.vector
            def _(dve):
                V = nc.vector
                V.tensor_reduce(mean[:], g["X"][:], AX.X, ALU.add).then_inc(stat, 1)
                dve.wait_ge(stat, 1)
                V.tensor_scalar(mean[:], mean[:], 1.0 / D, None, ALU.mult).then_inc(stat, 1)
                dve.wait_ge(stat, 2)
                V.tensor_tensor(H[:], g["X"][:], per_tile(mean[:]), ALU.subtract).then_inc(centred, 1)
                dve.wait_ge(squared, 1)
                V.tensor_reduce(var[:], SQ[:], AX.X, ALU.add).then_inc(stat, 1)
                dve.wait_ge(stat, 3)
                V.tensor_scalar(var[:], var[:], 1.0 / D, LN_EPS, ALU.mult, ALU.add).then_inc(stat, 1)
                dve.wait_ge(stat, 4)
                dve.wait_ge(stat, 5)
                dve.wait_ge(centred, 1)
                V.scalar_tensor_tensor(H[:], H[:], 0.0, per_tile(var[:]), ALU.max, ALU.mult).then_inc(stat, 1)
                dve.wait_ge(stat, 6)

            @block.scalar
            def _(act):
                act.wait_ge(centred, 1)
                nc.scalar.activation(SQ[:], H[:], ACT.Square).then_inc(squared, 1)

            @block.gpsimd
            def _(pool):
                pool.wait_ge(stat, 4)
                pool.tensor_tensor(var[:], var[:], g["mhalf"][:, 0:TILES], ALU.pow).then_inc(stat, 1)
        sem.clear()


def node_matmul(nc, g, name, SRC, W, NC, evacuate, loads=()):
    per = 512 // NC
    banks = [(u, min(per, TG - u)) for u in range(0, TG, per)]
    with ExitStack() as ctx:
        sem = Semaphores(nc, ctx, name)
        STG = ctx.enter_context(nc.sbuf_tensor(name + "_stage", [P, TG, D], F32))
        HT = ctx.enter_context(nc.sbuf_tensor(name + "_ht", [P, TG, P], F32))
        TP = ctx.enter_context(nc.psum_tensor(name + "_tp", [P, 2, 512], F32))
        OP = ctx.enter_context(nc.psum_tensor(name + "_op", [P, len(banks), 512], F32))
        loaded = sem("_loaded")
        staged = sem("_staged")
        stood = sem("_stood")
        turned = sem("_turned")
        ht_in = sem("_ht_in")
        product = sem("_product")
        taken = sem("_taken")

        def groups(eng, body):
            body(0)
            with eng.Fori(1, NG) as i:
                body(i)

        with nc.Block() as block:
            @block.sync
            def _(sp):
                for o, i in loads:
                    sp.dma_start(o, i).then_inc(loaded, 16)

            @block.gpsimd
            def _(pool):
                def body(i):
                    wait_alone(pool, turned, i, stood)
                    pool.tensor_copy(STG[:], SRC[:, bass.ds(i * TG, TG), :]).then_inc(staged, 1)
                groups(pool, body)

            @block.tensor
            def _(pe):
                if loads:
                    pe.wait_ge(loaded, 16 * len(loads))

                def body(i):
                    pe.wait_ge(staged, i + 1)
                    for u in range(TG):
                        ins = nc.tensor.transpose(TP[:, u // 4, (u % 4) * P:(u % 4 + 1) * P], STG[:, u, :], g["eye"][:])
                    ins.then_inc(turned, 1)
                    wait(pe, taken, i)
                    pe.wait_ge(ht_in, i + 1)
                    for u in range(TG):
                        ins = nc.tensor.matmul(OP[:, u // per, (u % per) * NC:(u % per + 1) * NC], HT[:, u, :], W,
                                               start=True, stop=True)
                    ins.then_inc(product, 1)
                groups(pe, body)

            @block.scalar
            def _(act):
                def body(i):
                    wait_alone(act, turned, i + 1, stood)
                    nc.scalar.copy(HT[:, 0:4, :], TP[:, 0, :].rearrange("p (u n) -> p u n", n=P))
                    nc.scalar.copy(HT[:, 4:TG, :], TP[:, 1, 0:(TG - 4) * P].rearrange("p (u n) -> p u n", n=P)).then_inc(ht_in, 1)
                groups(act, body)

            @block.vector
            def _(dve):
                if loads:
                    dve.wait_ge(loaded, 16 * len(loads))

                def body(i):
                    wait(dve, taken, i)
                    dve.wait_ge(product, i + 1)
                    for k, (u, m) in enumerate(banks):
                        ins = evacuate(dve, i * TG + u, m, OP[:, k, 0:m * NC].rearrange("p (u n) -> p u n", n=NC),
                                       i, k)
                    ins.then_inc(taken, 1)
                groups(dve, body)
                dve.wait_ge(taken, NG)
        sem.clear()


def batch_norm(nc, g, name, U, H, gamma, beta):
    with ExitStack() as ctx:
        sem = Semaphores(nc, ctx, name)
        SQ = ctx.enter_context(nc.sbuf_tensor(name + "_sq", [P, TILES, D], F32))
        gam = ctx.enter_context(nc.sbuf_tensor(name + "_gam", [P, D], F32))
        bet = ctx.enter_context(nc.sbuf_tensor(name + "_bet", [P, D], F32))
        mean = ctx.enter_context(nc.sbuf_tensor(name + "_mean", [P, D], F32))
        scl = ctx.enter_context(nc.sbuf_tensor(name + "_scl", [P, D], F32))
        PM = ctx.enter_context(nc.psum_tensor(name + "_pm", [P, 512], F32))
        PV = ctx.enter_context(nc.psum_tensor(name + "_pv", [P, 512], F32))
        loaded = sem("_loaded")
        summed = sem("_summed")
        centred = sem("_centred")
        squared = sem("_squared")
        stat = sem("_stat")
        root = sem("_root")

        with nc.Block() as block:
            @block.gpsimd
            def _(pool):
                pool.wait_ge(stat, 2)
                pool.tensor_tensor(scl[:], scl[:], g["mhalf"][:], ALU.pow).then_inc(root, 1)

            @block.sync
            def _(sp):
                sp.dma_start(gam[:], gamma.partition_broadcast(P)).then_inc(loaded, 16)
                sp.dma_start(bet[:], beta.partition_broadcast(P)).then_inc(loaded, 16)

            @block.tensor
            def _(pe):
                def column_sums(out, A):
                    nc.tensor.matmul(out, g["ones"][:], A[:, 0, :], start=True, stop=False)
                    with pe.Fori(1, TILES - 1) as t:
                        nc.tensor.matmul(out, g["ones"][:], A[:, bass.ds(t, 1), :].rearrange("p o d -> p (o d)"), start=False, stop=False)
                    nc.tensor.matmul(out, g["ones"][0:LAST, :], A[0:LAST, TILES - 1, :],
                                     start=False, stop=True).then_inc(summed, 1)
                column_sums(PM[:, 0:D], U)
                pe.wait_ge(squared, 1)
                column_sums(PV[:, 0:D], SQ)

            @block.scalar
            def _(act):
                act.wait_ge(centred, 1)
                nc.scalar.activation(SQ[:], U[:], ACT.Square).then_inc(squared, 1)

            @block.vector
            def _(dve):
                V = nc.vector
                n = [0]

                def then(ins):
                    n[0] += 1
                    ins.then_inc(stat, 1)
                    dve.wait_ge(stat, n[0])

                dve.wait_ge(summed, 1)
                then(V.tensor_scalar(mean[:], PM[:, 0:D], 1.0 / N, None, ALU.mult))
                V.tensor_tensor(U[:], U[:], per_feature(mean[:]), ALU.subtract).then_inc(centred, 1)
                dve.wait_ge(loaded, 32)
                dve.wait_ge(summed, 2)
                then(V.tensor_scalar(scl[:], PV[:, 0:D], 1.0 / N, BN_EPS, ALU.mult, ALU.add))
                dve.wait_ge(root, 1)
                then(V.tensor_tensor(scl[:], scl[:], gam[:], ALU.mult))
                dve.wait_ge(squared, 1)
                then(V.tensor_tensor(U[:], U[:], per_feature(scl[:]), ALU.mult))
                then(V.tensor_tensor(U[:], U[:], per_feature(bet[:]), ALU.add))
                then(V.scalar_tensor_tensor(U[:], U[:], 0.0, H[:], ALU.max, ALU.add))
                then(V.tensor_tensor(g["X"][:], g["X"][:], U[:], ALU.add))
        sem.clear()


class Count:

    def __init__(self, eng, sem, before):
        self.eng, self.sem, self.n = eng, sem, before

    def then(self, ins):
        ins.then_inc(self.sem, 1)
        self.n = self.n + 1
        self.eng.wait_ge(self.sem, self.n)


def gather_group(nc, pool, g, idx, ready, table, out_of, gathered, k, stood):
    pool.tensor_copy(idx, g["src_idx"][:, bass.ds(k * GROUP, GROUP)]).then_inc(ready, 1)
    wait_alone(pool, ready, k + 1, stood)
    for s in range(GROUP):
        pool.indirect_dma_start(out=out_of(s), out_offset=None, in_=table,
                                in_offset=bass.IndirectOffsetOnAxis(ap=idx[:, s:s + 1], axis=0)).then_inc(gathered, 16)


def onehot_rows(nc, g, loc, k):
    return (g["iota_row"][:].unsqueeze(1).to_broadcast([P, GROUP, P]),
            loc[:, bass.ds(k * GROUP, GROUP)].unsqueeze(2).to_broadcast([P, GROUP, P]))


class SoftmaxParts:

    def __init__(self, nc, g, ctx, name, heads, ACC, scaled, onehot_type=F32):
        self.nc, self.g, self.heads, self.ACC = nc, g, heads, ACC
        self.scaled = scaled
        self.changes = GROUP + len(scaled)

        def sb(n, shape, dt=F32):
            return ctx.enter_context(nc.sbuf_tensor(name + n, shape, dt))

        self.sem = sem = Semaphores(nc, ctx, name)
        self.idx = sb("idx", [P, 4, GROUP], I32)
        self.LR = sb("LR", [P, 2, SLOTS], BF16)
        self.MS = sb("MS", [heads, 2, SLOTS], BF16)
        self.ME = sb("ME", [heads, 2, SLOTS], BF16)
        self.LF = sb("LF", [heads, 2])
        self.ST = sb("ST", [P, 2, SLOTS], onehot_type)
        self.FW = sb("FW", [heads, 2, SLOTS])
        self.CM = sb("CM", [heads, SLOTS])
        self.cont = sb("cont", [heads, 1])
        self.drop = sb("drop", [heads, 1])
        self.fac = sb("fac", [heads, 1])
        self.OH = sb("OH", [heads, P])
        self.DG = sb("DG", [heads, heads + 1])
        self.rest = sb("rest", [P, 1])
        self.R = sb("R", [P, heads])
        self.ET = ctx.enter_context(nc.psum_tensor(name + "ET", [heads, SLOTS], F32))
        self.SB = ctx.enter_context(nc.psum_tensor(name + "SB", [P, 512], F32))
        self.OUT = ctx.enter_context(nc.psum_tensor(name + "OUT", [P, 3, 512], F32))
        self.RP = self.SB[:, 256:256 + heads + 1]
        self.idx_ready = sem("idx_ready")
        self.gathered = g["gathered"]
        self.base = g["rows_gathered"][:]
        self.locrow_in = [sem(f"locrow_in{b}") for b in range(2)]
        self.masks_in = [sem(f"masks_in{b}") for b in range(2)]
        self.start = sem("start")
        self.stood = sem("stood")
        self.st_done = sem("st_done")
        self.et_done = sem("et_done")
        self.cm_done = sem("cm_done")
        self.drop_done = sem("drop_done")
        self.fac_done = sem("fac_done")
        self.dg_done = sem("dg_done")
        self.scores, self.scores_done = self.ET, self.et_done
        self.r_done = sem("r_done")
        self.p_done = sem("p_done")
        self.mm_done = sem("mm_done")
        self.acc_done = sem("acc_done")
        self.maxima_step = sem("maxima_step")
        self.factor_step = sem("factor_step")

    def gathers(self, pool, table, G, rows, used):
        def body(k, i, b):
            wait_alone(pool, used, k - 3, self.stood)
            gather_group(self.nc, pool, self.g, self.idx[:, b, :], self.idx_ready, table[:, :],
                         lambda s: G[:, b, s, 0:rows], self.gathered[b], k, self.stood)
        in_groups_of_four(pool, body)

    def rows_in(self, sp):
        def locrow(k, c):
            sp.dma_start(self.LR[:, c, :], self.g["row_loc"][bass.ds(k * SLOTS, SLOTS)].partition_broadcast(P)).then_inc(self.locrow_in[c], 16)

        def body(k, i, b):
            c = b % 2
            wait(sp, self.st_done, k - 1)
            locrow(k, c)
            wait(sp, self.drop_done, k - 1)
            for t, row in ((self.MS, "row_start"), (self.ME, "row_end")):
                sp.dma_start(t[:, c, :], self.g[row][bass.ds(k * SLOTS, SLOTS)].partition_broadcast(self.heads)).then_inc(self.masks_in[c], 16)
        in_groups_of_four(sp, body)

    def prepare(self, dve):
        V = self.nc.vector
        V.memset(self.ACC[:], 0.0).then_inc(self.acc_done, 1)
        V.memset(self.FW[:, 1, SLOTS - 1:SLOTS], -BIG).then_inc(self.start, 1)
        V.memset(self.DG[:, self.heads:self.heads + 1], 1.0 / self.heads).then_inc(self.start, 1)
        self.node_slots(dve, 0, 0)
        self.node_slots(dve, 0, 1)
        dve.wait_ge(self.start, 2)

    def node_slots(self, dve, i, b):
        V, c = self.nc.vector, b % 2
        dve.wait_ge(self.locrow_in[c], 16 * (2 * i + b // 2 + 1))
        V.tensor_copy(self.LF[:, c:c + 1], self.LR[0:self.heads, c, 0:1])
        V.tensor_scalar(self.ST[:, c, :], self.LR[:, c, :], self.g["iota_col"][:], None, ALU.is_equal).then_inc(self.st_done, 1)

    def node_slots_ahead(self, dve, i, b):
        self.node_slots(dve, i + (b + 2) // 4, (b + 2) % 4)

    def running_maxima(self, dve, k, i, b):
        V, p = self.nc.vector, b % 2
        FW, CM, drop = self.FW, self.CM, self.drop
        dve.wait_ge(self.masks_in[p], 32 * (2 * i + b // 2 + 1))
        dve.wait_ge(self.scores_done, k + 1)
        V.tensor_tensor_scan(out=FW[:, p, :], data0=self.MS[:, p, :], data1=self.scores[:],
                             initial=FW[:, 1 - p, SLOTS - 1:SLOTS], op0=ALU.add, op1=ALU.max).then_inc(self.maxima_step, 1)
        dve.wait_ge(self.st_done, k + 1)
        V.tensor_scalar(self.OH[:], self.g["iota_row"][0:self.heads, :], self.LF[:, p:p + 1], None, ALU.is_equal)
        V.tensor_scalar(self.cont[:], self.MS[:, p, 0:1], -0.5, None, ALU.is_ge).then_inc(self.maxima_step, 1)
        dve.wait_ge(self.maxima_step, 3 * k + 2)
        V.tensor_tensor_scan(out=CM[:, ::-1], data0=self.ME[:, p, ::-1], data1=FW[:, p, ::-1],
                             initial=-BIG, op0=ALU.add, op1=ALU.max).then_inc(self.cm_done, 1)
        dve.wait_ge(self.cm_done, k + 1)
        V.tensor_tensor(drop[:], FW[:, 1 - p, SLOTS - 1:SLOTS], CM[:, 0:1], ALU.subtract).then_inc(self.maxima_step, 1)
        dve.wait_ge(self.maxima_step, 3 * k + 3)
        V.tensor_tensor(drop[:], drop[:], self.cont[:], ALU.mult).then_inc(self.drop_done, 1)

    def factor(self, act, k):
        wait_alone(act, self.drop_done, k + 1, self.stood)
        self.nc.scalar.activation(self.fac[:], self.drop[:], ACT.Exp).then_inc(self.fac_done, 1)

    def factor_diagonal(self, dve, k):
        dve.wait_ge(self.fac_done, k + 1)
        h = self.heads
        self.nc.vector.tensor_scalar(self.DG[:, 0:h], self.g["eye"][0:h, 0:h], self.fac[:], None, ALU.mult).then_inc(self.dg_done, 1)

    def factor_of_nodes(self, pe, k):
        pe.wait_ge(self.dg_done, k + 1)
        self.nc.tensor.matmul(self.RP, self.OH[:], self.DG[:], start=True, stop=True).then_inc(self.r_done, 1)

    def read_factors(self, dve, k):
        V, h = self.nc.vector, self.heads
        dve.wait_ge(self.r_done, k + 1)
        V.tensor_scalar(self.rest[:], self.RP[:, h:h + 1], -1.0, 1.0, ALU.mult, ALU.add).then_inc(self.factor_step, 1)
        dve.wait_ge(self.factor_step, 2 * k + 1)
        V.tensor_scalar(self.R[:], self.RP[:, 0:h], self.rest[:], None, ALU.add).then_inc(self.factor_step, 1)

    def tiles_of(self, dve, k):
        return load_tiles(self.nc, mybir.EngineType.DVE, self.g["tile_row"], k * GROUP, GROUP)

    def accumulate(self, dve, k, tiles, between=()):
        V, ACC, R, h = self.nc.vector, self.ACC, self.R, self.heads
        done = self.changes * k + 1
        dve.wait_ge(self.factor_step, 2 * k + 2)
        dve.wait_ge(self.acc_done, done)
        for cols in self.scaled:
            rows = ACC[:, bass.ds(tiles[0], 1), cols].rearrange("p o c -> p (o c)")
            if h == 1:
                ins = V.tensor_scalar(rows, rows, R[:], None, ALU.mult)
            else:
                rows = rows.rearrange("p (h f) -> p h f", h=h)
                ins = V.tensor_tensor(rows, rows, R[:].unsqueeze(2).to_broadcast([P, h, rows.shape[2]]), ALU.mult)
            ins.then_inc(self.acc_done, 1)
        dve.wait_ge(self.mm_done, k + 1)
        AC = ACC.shape[2]
        for s, t in enumerate(tiles):
            dst = ACC[:, bass.ds(t, 1), :].rearrange("p o c -> p (o c)")
            dve.wait_ge(self.acc_done, done + len(self.scaled) + s)
            V.tensor_tensor(dst, dst, self.OUT[:, s // 3, (s % 3) * AC:(s % 3 + 1) * AC], ALU.add).then_inc(self.acc_done, 1)
            for work in between[s * len(between) // GROUP:(s + 1) * len(between) // GROUP]:
                work()

    def close(self, dve):
        dve.wait_ge(self.acc_done, self.changes * GROUPS + 1)

    def finish(self):
        self.sem.clear()
        for b in range(4):
            self.g["rows_gathered"][b] += 16 * GROUP * (GROUPS // 4)


def gat_pass(nc, g, table, destination, ACC):
    heads, hd, AC = HEADS, HF, ACC.shape[2]
    WC = D + heads
    with ExitStack() as ctx:
        def sb(n, shape, dt=F32):
            return ctx.enter_context(nc.sbuf_tensor("e0_" + n, shape, dt))

        parts = SoftmaxParts(nc, g, ctx, "e0_", heads, ACC, (slice(0, D), slice(D, WC)), BF16)
        sem = parts.sem
        G = sb("G", [P, 4, GROUP, WC])
        S = sb("S", [P, 2, GROUP, P])
        Z = sb("Z", [P, GROUP, heads])
        exact = sb("exact", [P, TILES, heads])
        split = sb("split", [P, TILES, 3, heads], BF16)
        SC = sb("SC", [P, 2, GROUP, heads])
        DIF = sb("DIF", [P, GROUP, heads])
        RH = sb("RH", [P, 2, GROUP, AC])
        DP = ctx.enter_context(nc.psum_tensor("e0_DP", [P, 512], F32))
        dp_view = DP[:, 0:GROUP * 3 * heads].rearrange("p (s c h) -> p s c h", c=3, h=heads)
        stab = parts.SB[:, 0:GROUP * heads].rearrange("p (s h) -> p s h", h=heads)
        split_done = sem("split_done")
        dp_done = sem("dp_done")
        summed = sem("summed")
        score = sem("score")
        has_done = sem("has_done")
        s_done = sem("s_done")
        stab_done = sem("stab_done")
        dif_done = sem("dif_done")
        rh_done = sem("rh_done")

        with nc.Block() as block:
            @block.gpsimd
            def _(pool):
                parts.gathers(pool, table, G, WC, rh_done)

            @block.sync
            def _(sp):
                parts.rows_in(sp)

            @block.scalar
            def _(act):
                def weights(k, b):
                    wait_alone(act, dif_done, k + 1, parts.stood)
                    nc.scalar.activation(RH[:, b % 2, :, D:D + heads], DIF[:], ACT.Exp).then_inc(parts.p_done, 1)

                def body(k, i, b):
                    if not is_first(k):
                        weights(k - 1, b + 3)
                    parts.factor(act, k)
                in_groups_of_four(act, body)
                weights(GROUPS - 1, 3)

            @block.vector
            def _(dve):
                V = nc.vector
                c = Count(dve, split_done, 0)
                c.then(V.tensor_copy(split[:, :, 0, :], destination))
                c.then(V.tensor_tensor(exact[:], destination, split[:, :, 0, :], ALU.subtract))
                c.then(V.tensor_copy(split[:, :, 1, :], exact[:]))
                c.then(V.tensor_tensor(exact[:], exact[:], split[:, :, 1, :], ALU.subtract))
                c.then(V.tensor_copy(split[:, :, 2, :], exact[:]))
                parts.prepare(dve)

                def differences(k, b):
                    p = b % 2
                    dve.wait_ge(stab_done, k + 1)
                    V.tensor_tensor(DIF[:], SC[:, p], stab, ALU.subtract).then_inc(dif_done, 1)
                    V.tensor_scalar(RH[:, p, :, AC - 1:AC], g["loc_end"][:, bass.ds(k * GROUP, GROUP)].unsqueeze(2),
                                    0.0, None, ALU.is_ge).then_inc(has_done, 1)
                    dve.wait_ge(has_done, k + 1)
                    V.tensor_tensor(RH[:, p, :, WC:WC + heads], stab,
                                    RH[:, p, :, AC - 1:AC].to_broadcast([P, GROUP, heads]), ALU.mult)

                def weighted_rows(k, b):
                    dve.wait_ge(parts.p_done, k + 1)
                    V.tensor_tensor(RH[:, b % 2, :, 0:D].rearrange("p s (h f) -> p s h f", h=heads),
                                    G[:, b, :, 0:D].rearrange("p s (h f) -> p s h f", h=heads),
                                    RH[:, b % 2, :, D:D + heads].unsqueeze(3).to_broadcast([P, GROUP, heads, hd]),
                                    ALU.mult).then_inc(rh_done, 1)

                def score_sums(k, i, b, part):
                    if part == 0:
                        dve.wait_ge(parts.gathered[b], parts.base[b] + 16 * GROUP * (i + 1))
                        dve.wait_ge(dp_done, k + 1)
                    else:
                        dve.wait_ge(summed, 3 * k + part)
                    V.tensor_tensor(Z[:], Z[:] if part else G[:, b, :, D:D + heads], dp_view[:, :, part, :],
                                    ALU.add).then_inc(summed, 1)

                def scores(k, b):
                    dve.wait_ge(summed, 3 * k + 3)
                    V.scalar_tensor_tensor(SC[:, b % 2], Z[:], SLOPE, Z[:], ALU.mult, ALU.max).then_inc(score, 1)

                def onehots(k, b, part):
                    n = GROUP // 4
                    ins = V.tensor_tensor(S[:, b % 2, part * n:(part + 1) * n], g["iota_row"][:].unsqueeze(1).to_broadcast([P, n, P]),
                                          g["loc"][:, bass.ds(k * GROUP + part * n, n)].unsqueeze(2).to_broadcast([P, n, P]),
                                          ALU.is_equal)
                    if part == 3:
                        ins.then_inc(s_done, 1)

                def body(k, i, b):
                    last = (b + 3) % 4
                    if not is_first(k):
                        tiles = parts.tiles_of(dve, k - 1)
                        differences(k - 1, last)
                        parts.factor_diagonal(dve, k - 1)
                        weighted_rows(k - 1, last)
                        parts.read_factors(dve, k - 1)
                    parts.running_maxima(dve, k, i, b)
                    between = []
                    for part in range(4):
                        between.append(lambda part=part: onehots(k, b, part))
                        if not is_last(k):
                            nxt = (k + 1, i + (b + 1) // 4, (b + 1) % 4)
                            if part < 3:
                                between.append(lambda part=part: score_sums(*nxt, part))
                            else:
                                between.append(lambda: scores(k + 1, b + 1))
                    if not (isinstance(k, int) and k >= GROUPS - 2):
                        between.append(lambda: parts.node_slots_ahead(dve, i, b))
                    if is_first(k):
                        for work in between:
                            work()
                    else:
                        parts.accumulate(dve, k - 1, tiles, between)

                for part in range(3):
                    score_sums(0, 0, 0, part)
                scores(0, 0)
                in_groups_of_four(dve, body)
                tiles = parts.tiles_of(dve, GROUPS - 1)
                differences(GROUPS - 1, 3)
                parts.factor_diagonal(dve, GROUPS - 1)
                weighted_rows(GROUPS - 1, 3)
                parts.read_factors(dve, GROUPS - 1)
                parts.accumulate(dve, GROUPS - 1, tiles)
                parts.close(dve)

            @block.tensor
            def _(pe):
                def destinations(k, b, tiles):
                    pe.wait_ge(parts.st_done, k + 1)
                    for s, t in enumerate(tiles):
                        ins = nc.tensor.matmul(dp_view[:, s], parts.ST[:, b % 2, s * P:(s + 1) * P],
                                               split[:, bass.ds(t, 1)].rearrange("p o c h -> p (o c h)"), start=True, stop=True)
                    ins.then_inc(dp_done, 1)

                def tiles_of(k):
                    return load_tiles(nc, mybir.EngineType.PE, g["tile_row"], k * GROUP, GROUP)

                def sums(k, b):
                    pe.wait_ge(s_done, k + 1)
                    pe.wait_ge(rh_done, k + 1)
                    for s in range(GROUP):
                        ins = nc.tensor.matmul(parts.OUT[:, s // 3, (s % 3) * AC:(s % 3 + 1) * AC], S[:, b % 2, s, :],
                                               RH[:, b % 2, s, :], start=True, stop=True)
                    ins.then_inc(parts.mm_done, 1)

                tiles = tiles_of(0)
                pe.wait_ge(split_done, 5)
                destinations(0, 0, tiles)

                def body(k, i, b):
                    if not is_last(k):
                        tiles = tiles_of(k + 1)
                    pe.wait_ge(score, k + 1)
                    for s in range(GROUP):
                        ins = nc.tensor.transpose(parts.ET[:, s * P:(s + 1) * P], SC[:, b % 2, s, :], g["eye"][:])
                    ins.then_inc(parts.et_done, 1)
                    if not is_last(k):
                        destinations(k + 1, b + 1, tiles)
                    if not is_first(k):
                        parts.factor_of_nodes(pe, k - 1)
                        sums(k - 1, b + 3)
                    wait_alone(pe, parts.cm_done, k + 1, parts.stood)
                    for s in range(GROUP):
                        ins = nc.tensor.transpose(stab[:, s, :], parts.CM[:, s * P:(s + 1) * P], g["eye"][0:heads, 0:heads])
                    ins.then_inc(stab_done, 1)
                in_groups_of_four(pe, body)
                parts.factor_of_nodes(pe, GROUPS - 1)
                sums(GROUPS - 1, 3)
        parts.finish()


def gatv2_pass(nc, g, table, destination, ACC, att_col):
    AC = D + 1
    with ExitStack() as ctx:
        def sb(n, shape, dt=F32):
            return ctx.enter_context(nc.sbuf_tensor("e3_" + n, shape, dt))

        parts = SoftmaxParts(nc, g, ctx, "e3_", 1, ACC, (slice(0, AC),))
        sem = parts.sem
        G = sb("G", [P, 4, GROUP, AC])
        XR = sb("XR", [P, GROUP, D])
        LOC = sb("LOC", [P, 4, GROUP])
        LZ = sb("LZ", [P, 2, SLOTS])
        ER = sb("ER", [1, SLOTS])
        SC = sb("SC", [P, GROUP])
        DIF = sb("DIF", [P, GROUP])
        W = sb("W", [P, 2, GROUP])
        S = sb("S", [P, 2, GROUP, P])
        ZT = ctx.enter_context(nc.psum_tensor("e3_ZT", [P, SLOTS], F32))
        turned_scores, turned_maxima = parts.SB[:, 0:GROUP], parts.SB[:, GROUP:2 * GROUP]
        xr_done = sem("xr_done")
        zt_done = sem("zt_done")
        sloped_done = sem("sloped_done")
        lz_done = sem("lz_done")
        er_done = sem("er_done")
        parts.scores, parts.scores_done = ER, er_done
        turned = sem("turned")
        sc_done = sem("sc_done")
        dif_done = sem("dif_done")
        s_done = sem("s_done")

        with nc.Block() as block:
            @block.gpsimd
            def _(pool):
                pool.memset(G[:, :, :, D:AC], 1.0).then_inc(parts.start, 1)
                parts.gathers(pool, table, G, D, parts.mm_done)

            @block.sync
            def _(sp):
                parts.rows_in(sp)

            @block.scalar
            def _(act):
                def stage(k, b):
                    tiles = load_tiles(nc, mybir.EngineType.Activation, g["tile_row"], k * GROUP, GROUP)
                    wait_alone(act, zt_done, 2 * k, parts.stood)
                    nc.scalar.copy(LOC[:, b, :], g["loc"][:, bass.ds(k * GROUP, GROUP)])
                    for s, t in enumerate(tiles):
                        ins = nc.scalar.copy(XR[:, s, :], destination[:, bass.ds(t, 1), :].rearrange("p o c -> p (o c)"))
                    ins.then_inc(xr_done, 1)

                def weights(k, b):
                    wait_alone(act, dif_done, k + 1, parts.stood)
                    nc.scalar.activation(W[:, b % 2, :], DIF[:], ACT.Exp).then_inc(parts.p_done, 1)

                def score_row(k):
                    wait_alone(act, parts.et_done, k + 1, parts.stood)
                    nc.scalar.copy(ER[:], parts.ET[:]).then_inc(er_done, 1)

                def edge_scores(k):
                    wait_alone(act, turned, k + 1, parts.stood)
                    nc.scalar.copy(SC[:], turned_scores).then_inc(sc_done, 1)

                def sloped(k, b, half):
                    wait_alone(act, zt_done, 2 * k + half + 1, parts.stood)
                    cols = slice(half * SLOTS // 2, (half + 1) * SLOTS // 2)
                    nc.scalar.activation(LZ[:, b % 2, cols], ZT[:, cols], ACT.Copy, scale=SLOPE).then_inc(sloped_done, 1)

                stage(0, 0)
                sloped(0, 0, 0)
                sloped(0, 0, 1)
                stage(1, 1)

                def body(k, i, b):
                    if not is_first(k):
                        weights(k - 1, b + 3)
                    score_row(k)
                    if not is_last(k):
                        sloped(k + 1, b + 1, 0)
                        sloped(k + 1, b + 1, 1)
                    parts.factor(act, k)
                    edge_scores(k)
                    if not (isinstance(k, int) and k >= GROUPS - 2):
                        stage(k + 2, (b + 2) % 4)
                in_groups_of_four(act, body)
                weights(GROUPS - 1, 3)

            @block.vector
            def _(dve):
                V = nc.vector
                parts.prepare(dve)

                def differences(k):
                    dve.wait_ge(sc_done, k + 1)
                    V.tensor_tensor(DIF[:], SC[:], turned_maxima, ALU.subtract).then_inc(dif_done, 1)

                def weighted_onehots(k, b):
                    dve.wait_ge(parts.p_done, k + 1)
                    for s in range(GROUP):
                        ins = V.tensor_scalar(S[:, b % 2, s, :], g["iota_row"][:], LOC[:, b, s:s + 1], W[:, b % 2, s:s + 1],
                                              ALU.is_equal, ALU.mult)
                    ins.then_inc(s_done, 1)

                def leaky(k, b, part):
                    if part % 2 == 0:
                        dve.wait_ge(sloped_done, 2 * k + part // 2 + 1)
                    cols = slice(part * SLOTS // 4, (part + 1) * SLOTS // 4)
                    ins = V.tensor_tensor(LZ[:, b % 2, cols], ZT[:, cols], LZ[:, b % 2, cols], ALU.max)
                    if part == 3:
                        ins.then_inc(lz_done, 1)

                def body(k, i, b):
                    last = (b + 3) % 4
                    if not is_first(k):
                        tiles = parts.tiles_of(dve, k - 1)
                        differences(k - 1)
                        parts.factor_diagonal(dve, k - 1)
                        weighted_onehots(k - 1, last)
                        parts.read_factors(dve, k - 1)
                    parts.running_maxima(dve, k, i, b)
                    between = [lambda: None, lambda: None]
                    if not (isinstance(k, int) and k >= GROUPS - 2):
                        between[0] = lambda: parts.node_slots_ahead(dve, i, b)
                    if not is_last(k):
                        between += [lambda part=part: leaky(k + 1, b + 1, part) for part in range(4)]
                    if is_first(k):
                        for work in between:
                            work()
                    else:
                        parts.accumulate(dve, k - 1, tiles, between)

                for part in range(4):
                    leaky(0, 0, part)
                in_groups_of_four(dve, body)
                tiles = parts.tiles_of(dve, GROUPS - 1)
                differences(GROUPS - 1)
                parts.factor_diagonal(dve, GROUPS - 1)
                weighted_onehots(GROUPS - 1, 3)
                parts.read_factors(dve, GROUPS - 1)
                parts.accumulate(dve, GROUPS - 1, tiles)
                parts.close(dve)

            @block.tensor
            def _(pe):
                def rows(k, i, b, steps):
                    if steps[0] == 0:
                        pe.wait_ge(parts.st_done, k + 1)
                        pe.wait_ge(xr_done, k + 1)
                        pe.wait_ge(parts.gathered[b], parts.base[b] + 16 * GROUP * (i + 1))
                    for s in steps:
                        cols = slice(s * P, (s + 1) * P)
                        nc.tensor.matmul(ZT[:, cols], XR[:, s, :], parts.ST[:, b % 2, cols], start=True, stop=False)
                        ins = nc.tensor.matmul(ZT[:, cols], G[:, b, s, 0:D], g["eye"][:], start=False, stop=True)
                        if s % (GROUP // 2) == GROUP // 2 - 1:
                            ins.then_inc(zt_done, 1)

                def sums(k, b):
                    pe.wait_ge(s_done, k + 1)
                    for s in range(GROUP):
                        ins = nc.tensor.matmul(parts.OUT[:, s // 3, (s % 3) * AC:(s % 3 + 1) * AC], S[:, b % 2, s, :],
                                               G[:, b, s, :], start=True, stop=True)
                    ins.then_inc(parts.mm_done, 1)

                pe.wait_ge(parts.start, 3)
                rows(0, 0, 0, range(GROUP))

                def body(k, i, b):
                    pe.wait_ge(lz_done, k + 1)
                    for h in range(SLOTS // 512):
                        cols = slice(h * 512, (h + 1) * 512)
                        ins = nc.tensor.matmul(parts.ET[:, cols], att_col, LZ[:, b % 2, cols], start=True, stop=True)
                    ins.then_inc(parts.et_done, 1)
                    if not is_first(k):
                        parts.factor_of_nodes(pe, k - 1)
                    if not is_last(k):
                        rows(k + 1, i + (b + 1) // 4, (b + 1) % 4, range(0, GROUP // 2))
                    if not is_first(k):
                        sums(k - 1, (b + 3) % 4)
                    if not is_last(k):
                        rows(k + 1, i + (b + 1) // 4, (b + 1) % 4, range(GROUP // 2, GROUP))
                    wait_alone(pe, parts.cm_done, k + 1, parts.stood)
                    for s in range(GROUP):
                        cols = slice(s * P, (s + 1) * P)
                        nc.tensor.transpose(turned_scores[:, s:s + 1], ER[:, cols], g["eye"][0:1, 0:1])
                        ins = nc.tensor.transpose(turned_maxima[:, s:s + 1], parts.CM[:, cols], g["eye"][0:1, 0:1])
                    ins.then_inc(turned, 1)

                in_groups_of_four(pe, body)
                parts.factor_of_nodes(pe, GROUPS - 1)
                sums(GROUPS - 1, 3)
        parts.finish()




def sum_pass(nc, g, table, ACC):
    name = "s_"
    AC = D + 1
    PER = 3
    with ExitStack() as ctx:
        sem = Semaphores(nc, ctx, name)

        idx = ctx.enter_context(nc.sbuf_tensor(name + "idx", [P, 2, GROUP], I32))
        G = ctx.enter_context(nc.sbuf_tensor(name + "G", [P, 2, GROUP, AC], F32))
        S = ctx.enter_context(nc.sbuf_tensor(name + "S", [P, 2, GROUP, P], F32))
        OUT = ctx.enter_context(nc.psum_tensor(name + "OUT", [P, 2, 3, 512], F32))
        idx_ready = sem("idx_ready")
        gathered = g["gathered"]
        base = g["rows_gathered"][:]
        stood = sem("p_stood")
        start = sem("start")
        s_done = sem("s_done")
        mm_done = sem("mm_done")
        acc_done = sem("acc_done")

        with nc.Block() as block:
            @block.gpsimd
            def _(pool):
                def body(k, i, b):
                    wait_alone(pool, mm_done, k - 1, stood)
                    gather_group(nc, pool, g, idx[:, b, :], idx_ready, table[:, :], lambda s: G[:, b, s, 0:D],
                                 gathered[b], k, stood)
                in_groups_of_two(pool, body)

            @block.vector
            def _(dve):
                V = nc.vector

                def add(k, b):
                    tiles = load_tiles(nc, mybir.EngineType.DVE, g["tile_row"], k * GROUP, GROUP)
                    dve.wait_ge(mm_done, k + 1)
                    for s, t in enumerate(tiles):
                        dst = ACC[:, bass.ds(t, 1), :].rearrange("p o c -> p (o c)")
                        dve.wait_ge(acc_done, k * GROUP + 1 + s)
                        V.tensor_tensor(dst, dst, OUT[:, b, s // PER, (s % PER) * AC:(s % PER + 1) * AC],
                                        ALU.add).then_inc(acc_done, 1)

                V.memset(G[:, :, :, D:AC], 1.0).then_inc(start, 1)
                V.memset(ACC[:], 0.0).then_inc(acc_done, 1)

                def body(k, i, b):
                    wait(dve, mm_done, k - 1)
                    V.tensor_tensor(S[:, b], *onehot_rows(nc, g, g["loc"], k), ALU.is_equal).then_inc(s_done, 1)
                    if not (isinstance(k, int) and k == 0):
                        add(k - 1, 1 - b)
                in_groups_of_two(dve, body)
                add(GROUPS - 1, 1)
                dve.wait_ge(acc_done, GROUP * GROUPS + 1)

            @block.tensor
            def _(pe):
                pe.wait_ge(start, 1)

                def body(k, i, b):
                    wait(pe, acc_done, 1 + GROUP * (k - 1) if not isinstance(k, int) or k >= 2 else 0)
                    pe.wait_ge(s_done, k + 1)
                    pe.wait_ge(gathered[b], base[b] + 16 * GROUP * (i + 1))
                    for s in range(GROUP):
                        ins = nc.tensor.matmul(OUT[:, b, s // PER, (s % PER) * AC:(s % PER + 1) * AC], S[:, b, s, :], G[:, b, s, :],
                                               start=True, stop=True)
                    ins.then_inc(mm_done, 1)
                in_groups_of_two(pe, body)
        sem.clear()
        for b in range(2):
            g["rows_gathered"][b] += 16 * GROUP * (GROUPS // 2)


def moments_pass(nc, g, table, ACC):
    name = "m_"
    Q = 4
    with ExitStack() as ctx:
        def sb(n, shape, dt=F32):
            return ctx.enter_context(nc.sbuf_tensor(name + n, shape, dt))

        sem = Semaphores(nc, ctx, name)

        idx = sb("idx", [P, Q, GROUP], I32)
        G = sb("G", [P, Q, GROUP, D])
        SQ = sb("SQ", [P, GROUP, D])
        S = sb("S", [P, 2, GROUP, P])
        SE = sb("SE", [P, 2, GROUP, P])
        MS = sb("MS", [P, 2, SLOTS], BF16)
        MN = sb("MN", [P, SLOTS], BF16)
        XT = sb("XT", [P, 2, 2, SLOTS])
        XB = sb("XB", [P, 2, 2, 2, D])
        GT = ctx.enter_context(nc.psum_tensor(name + "GT", [P, SLOTS], F32))
        BK = ctx.enter_context(nc.psum_tensor(name + "BK", [P, 4, 512], F32))
        OUT = ctx.enter_context(nc.psum_tensor(name + "OUT", [P, 2, 512], F32))
        idx_ready = sem("idx_ready")
        gathered = g["gathered"]
        base = g["rows_gathered"][:]
        masks_in = [sem(f"masks_in{b}") for b in range(2)]
        stood = sem("p_stood")
        start = sem("start")
        gt_done = sem("gt_done")
        mn_done = sem("mn_done")
        scanned = sem("scanned")
        s_done = sem("s_done")
        sq_done = sem("sq_done")
        bk_done = sem("bk_done")
        xb_done = sem("xb_done")
        step_done = sem("step_done")
        acc_done = sem("acc_done")

        with nc.Block() as block:
            @block.gpsimd
            def _(pool):
                def body(k, i, b):
                    wait_alone(pool, step_done, (k - Q + 1) * GROUP, stood)
                    gather_group(nc, pool, g, idx[:, b, :], idx_ready, table[:, :], lambda s: G[:, b, s, :],
                                 gathered[b], k, stood)
                in_groups_of_four(pool, body)

            @block.sync
            def _(sp):
                def body(k, i, b):
                    wait(sp, scanned, 2 * (k - 1))
                    sp.dma_start(MS[:, b % 2, :], g["row_start"][bass.ds(k * SLOTS, SLOTS)].partition_broadcast(P)).then_inc(masks_in[b % 2], 16)
                in_groups_of_four(sp, body)

            @block.scalar
            def _(act):
                def back(k, i, b):
                    wait_alone(act, gathered[b], base[b] + 16 * GROUP * (i + 1), stood)
                    wait_alone(act, step_done, k * GROUP, stood)
                    nc.scalar.activation(SQ[:], G[:, b], ACT.Square).then_inc(sq_done, 1)
                    for q in range(4):
                        wait_alone(act, bk_done, 4 * k + q + 1, stood)
                        if q >= 2:
                            wait_alone(act, step_done, k * GROUP + 2 * (q - 1), stood)
                        nc.scalar.copy(XB[:, q % 2], BK[:, q, :].rearrange("p (s m d) -> p s m d", s=2, m=2)).then_inc(xb_done, 1)
                in_groups_of_four(act, back)

            @block.vector
            def _(dve):
                V = nc.vector

                def add(k, steps):
                    tiles = load_tiles(nc, mybir.EngineType.DVE, g["tile_row"], k * GROUP + steps[0], len(steps))
                    for s, t in zip(steps, tiles):
                        dst = ACC[:, bass.ds(t, 1), :].rearrange("p o c -> p (o c)")
                        dve.wait_ge(step_done, k * GROUP + s + 1)
                        dve.wait_ge(acc_done, k * GROUP + s + 1)
                        V.tensor_tensor(dst, dst, OUT[:, s % 2, :], ALU.add).then_inc(acc_done, 1)

                V.memset(ACC[:], 0.0).then_inc(acc_done, 1)
                V.memset(XT[:, 1, 0, SLOTS - 1:SLOTS], BIG).then_inc(start, 1)
                V.memset(XT[:, 1, 1, SLOTS - 1:SLOTS], -BIG).then_inc(start, 1)
                dve.wait_ge(start, 2)

                def body(k, i, b):
                    c = b % 2
                    dve.wait_ge(masks_in[c], 16 * ((k - c) // 2 + 1) if isinstance(k, int) else 16 * (2 * i + b // 2 + 1))
                    wait(dve, scanned, 2 * k)
                    V.tensor_scalar(MN[:], MS[:, c, :], -1.0, None, ALU.mult).then_inc(mn_done, 1)
                    V.tensor_tensor(S[:, c], *onehot_rows(nc, g, g["loc"], k), ALU.is_equal)
                    V.tensor_tensor(SE[:, c], *onehot_rows(nc, g, g["loc_end"], k), ALU.is_equal).then_inc(s_done, 1)
                    dve.wait_ge(gt_done, k + 1)
                    dve.wait_ge(mn_done, k + 1)
                    for m, (mask, op) in enumerate(((MN[:], ALU.min), (MS[:, c, :], ALU.max))):
                        wait(dve, scanned, 2 * k)
                        V.tensor_tensor_scan(out=XT[:, c, m, :], data0=mask, data1=GT[:],
                                             initial=XT[:, 1 - c, m, SLOTS - 1:SLOTS], op0=ALU.add, op1=op).then_inc(scanned, 1)
                        if not is_first(k):
                            add(k - 1, range(4 * m, 4 * m + 4))
                in_groups_of_four(dve, body)
                add(GROUPS - 1, range(GROUP))
                dve.wait_ge(acc_done, GROUP * GROUPS + 1)

            @block.tensor
            def _(pe):
                def turn(k, i, b):
                    wait(pe, scanned, 2 * k)
                    pe.wait_ge(gathered[b], base[b] + 16 * GROUP * (i + 1))
                    for s in range(GROUP):
                        ins = nc.tensor.transpose(GT[:, s * P:(s + 1) * P], G[:, b, s, :], g["eye"][:])
                    ins.then_inc(gt_done, 1)

                def sums(k, b):
                    c = b % 2
                    pe.wait_ge(scanned, 2 * (k + 1))
                    for q in range(4):
                        wait(pe, xb_done, 4 * (k - 1) + q + 1)
                        for s in (2 * q, 2 * q + 1):
                            for m in range(2):
                                ins = nc.tensor.transpose(BK[:, q, ((s % 2) * 2 + m) * D:((s % 2) * 2 + m + 1) * D],
                                                          XT[:, c, m, s * P:(s + 1) * P], g["eye"][:])
                        ins.then_inc(bk_done, 1)
                    pe.wait_ge(s_done, k + 1)
                    pe.wait_ge(sq_done, k + 1)
                    for s in range(GROUP):
                        pe.wait_ge(xb_done, 4 * k + s // 2 + 1)
                        wait(pe, acc_done, k * GROUP + s if not isinstance(k, int) or k * GROUP + s >= 2 else 0)
                        nc.tensor.matmul(OUT[:, s % 2, 0:D], S[:, c, s, :], G[:, b, s, :], start=True, stop=True)
                        nc.tensor.matmul(OUT[:, s % 2, D:3 * D], SE[:, c, s, :], XB[:, (s // 2) % 2, s % 2].rearrange("p m d -> p (m d)"), start=True, stop=True)
                        nc.tensor.matmul(OUT[:, s % 2, 3 * D:4 * D], S[:, c, s, :], SQ[:, s, :], start=True, stop=True).then_inc(step_done, 1)

                def body(k, i, b):
                    turn(k, i, b)
                    if not is_first(k):
                        sums(k - 1, (b - 1) % Q)
                in_groups_of_four(pe, body)
                sums(GROUPS - 1, Q - 1)
        sem.clear()
        for b in range(Q):
            g["rows_gathered"][b] += 16 * GROUP * (GROUPS // Q)


def layer_gat(nc, g, w):
    with ExitStack() as ctx:
        sem = Semaphores(nc, ctx, "")
        H = ctx.enter_context(nc.sbuf_tensor("H0", [P, TILES, D], F32))
        XPA = ctx.enter_context(nc.sbuf_tensor("XPA", [P, TILES, D + 2 * HEADS], F32))
        layer_norm_relu(nc, g, "ln0", H)
        with ExitStack() as c2:
            def sb(n, shape):
                return c2.enter_context(nc.sbuf_tensor("g0_" + n, shape, F32))
            W = sb("W", [D, D + 2 * HEADS])
            WT = sb("WT", [D, D])
            att = sb("att", [D, 2])
            first = sb("first", [P, HEADS])
            mask = sb("mask", [P, HEADS])
            AB = sb("AB", [P, 2 * HEADS])
            PW = c2.enter_context(nc.psum_tensor("g0_PW", [P, 2, 512], F32))
            loaded = sem("g0_loaded")
            turned = sem("g0_turned")
            ab_done = sem("g0_ab_done")
            with nc.Block() as block:
                @block.sync
                def _(sp):
                    sp.dma_start(W[:, 0:D], w["L0_gnn_W"]).then_inc(loaded, 16)
                    sp.dma_start(att[:, 0:1], w["L0_gnn_att_src"].rearrange("h (f o) -> (h f) o", o=1)).then_inc(loaded, 16)
                    sp.dma_start(att[:, 1:2], w["L0_gnn_att_dst"].rearrange("h (f o) -> (h f) o", o=1)).then_inc(loaded, 16)

                @block.tensor
                def _(pe):
                    pe.wait_ge(loaded, 48)
                    nc.tensor.transpose(PW[:, 0, 0:D], W[:, 0:D], g["eye"][:]).then_inc(turned, 1)
                    pe.wait_ge(ab_done, 5)
                    nc.tensor.matmul(PW[:, 1, 0:2 * HEADS], WT[:], AB[:], start=True, stop=True).then_inc(turned, 1)

                @block.vector
                def _(dve):
                    V = nc.vector
                    c = Count(dve, ab_done, 0)
                    dve.wait_ge(loaded, 48)
                    dve.wait_ge(turned, 1)
                    c.then(V.tensor_copy(WT[:], PW[:, 0, 0:D]))
                    c.then(V.tensor_scalar(first[:], g["iota_row"][:, 0:HEADS], -float(HF), g["iota_col"][:], ALU.mult, ALU.add))
                    c.then(V.tensor_scalar(mask[:], first[:], 0.0, None, ALU.is_ge))
                    c.then(V.scalar_tensor_tensor(mask[:], first[:], float(HF), mask[:], ALU.is_lt, ALU.mult))
                    V.tensor_scalar(AB[:, 0:HEADS], mask[:], att[:, 0:1], None, ALU.mult)
                    c.then(V.tensor_scalar(AB[:, HEADS:2 * HEADS], mask[:], att[:, 1:2], None, ALU.mult))
                    dve.wait_ge(turned, 2)
                    c.then(V.tensor_copy(W[:, D:D + 2 * HEADS], PW[:, 1, 0:2 * HEADS]))
            node_matmul(nc, g, "nm0", H, W[:], D + 2 * HEADS,
                        lambda dve, t, m, ps, i, k: nc.vector.tensor_copy(XPA[:, bass.ds(t, m), :], ps))
        store_table(nc, "st0", g["tab0"], XPA[:, :, 0:D + HEADS])
        ACC = ctx.enter_context(nc.sbuf_tensor("ACC0", [P, TILES, D + 2 * HEADS + 1], F32))
        gat_pass(nc, g, g["tab0"], XPA[:, :, D + HEADS:D + 2 * HEADS], ACC)
        U = ctx.enter_context(nc.sbuf_tensor("U0", [P, TILES, D], F32))
        with ExitStack() as c2:
            def sb(n, shape):
                return c2.enter_context(nc.sbuf_tensor("f0_" + n, shape, F32))
            bias = sb("bias", [P, D])
            none = sb("none", [P, TILES])
            es = sb("es", [P, TILES, HEADS])
            mx = sb("mx", [P, TILES, HEADS])
            r = sb("r", [P, TILES, HEADS])
            loaded = sem("f0_loaded")
            chain = sem("f0_chain")
            exps = sem("f0_exps")
            with nc.Block() as block:
                @block.sync
                def _(sp):
                    sp.dma_start(bias[:], w["L0_gnn_bias"].partition_broadcast(P)).then_inc(loaded, 16)

                @block.scalar
                def _(act):
                    act.wait_ge(chain, 8)
                    nc.scalar.activation(r[:], r[:], ACT.Exp).then_inc(exps, 1)
                    nc.scalar.activation(es[:], es[:], ACT.Exp).then_inc(exps, 1)

                @block.vector
                def _(dve):
                    V = nc.vector
                    c = Count(dve, chain, 0)
                    th = [P, TILES, HEADS]
                    den, big = ACC[:, :, D:D + HEADS], ACC[:, :, D + HEADS:D + 2 * HEADS]
                    c.then(V.tensor_scalar(none[:], ACC[:, :, D + 2 * HEADS], -1.0, BIG, ALU.add, ALU.mult))
                    c.then(V.tensor_tensor(r[:], big, none[:].unsqueeze(2).to_broadcast(th), ALU.add))
                    c.then(V.tensor_tensor(es[:], XPA[:, :, D:D + HEADS], XPA[:, :, D + HEADS:], ALU.add))
                    c.then(V.tensor_scalar(mx[:], es[:], SLOPE, None, ALU.mult))
                    c.then(V.tensor_tensor(es[:], es[:], mx[:], ALU.max))
                    c.then(V.tensor_tensor(mx[:], r[:], es[:], ALU.max))
                    c.then(V.tensor_tensor(r[:], r[:], mx[:], ALU.subtract))
                    c.then(V.tensor_tensor(es[:], es[:], mx[:], ALU.subtract))
                    dve.wait_ge(exps, 2)
                    c.then(V.tensor_tensor(mx[:], den, r[:], ALU.mult))
                    c.then(V.scalar_tensor_tensor(mx[:], mx[:], SOFTMAX_EPS, es[:], ALU.add, ALU.add))
                    c.then(V.reciprocal(mx[:], mx[:]))
                    c.then(V.tensor_tensor(r[:], r[:], mx[:], ALU.mult))
                    c.then(V.tensor_tensor(es[:], es[:], mx[:], ALU.mult))
                    for h in range(HEADS):
                        cols = slice(h * HF, (h + 1) * HF)
                        wide = [P, TILES, HF]
                        V.tensor_tensor(U[:, :, cols], ACC[:, :, cols], r[:, :, h:h + 1].to_broadcast(wide), ALU.mult)
                        ins = V.tensor_tensor(XPA[:, :, cols], XPA[:, :, cols], es[:, :, h:h + 1].to_broadcast(wide), ALU.mult)
                    c.then(ins)
                    c.then(V.tensor_tensor(U[:], U[:], XPA[:, :, 0:D], ALU.add))
                    dve.wait_ge(loaded, 16)
                    c.then(V.tensor_tensor(U[:], U[:], per_feature(bias[:]), ALU.add))
        batch_norm(nc, g, "bn0", U, H, w["L0_gnn_bn_gamma"], w["L0_gnn_bn_beta"])
        sem.clear()


def store_table(nc, name, table, rows):
    with ExitStack() as ctx:
        sem = Semaphores(nc, ctx, name)
        stored = sem("_stored")
        with nc.Block() as block:
            @block.sync
            def _(sp):
                sp.dma_start(table.rearrange("(t p) d -> p t d", p=P), rows).then_inc(stored, 16)
                sp.wait_ge(stored, 16)
        sem.clear()


def layer_gcn(nc, g, w):
    with ExitStack() as ctx:
        sem = Semaphores(nc, ctx, "")
        H = ctx.enter_context(nc.sbuf_tensor("H1", [P, TILES, D], F32))
        layer_norm_relu(nc, g, "ln1", H)
        with ExitStack() as c2:
            T = c2.enter_context(nc.sbuf_tensor("T1", [P, TILES, D], F32))
            scaled = sem("scaled1")
            with nc.Block() as block:
                @block.vector
                def _(dve):
                    nc.vector.tensor_tensor(T[:], H[:], per_tile(g["rs_out"][:]), ALU.mult).then_inc(scaled, 1)
                    dve.wait_ge(scaled, 1)
            store_table(nc, "st1", g["tab1"], T[:])
        ACC = ctx.enter_context(nc.sbuf_tensor("ACC1", [P, TILES, D + 1], F32))
        sum_pass(nc, g, g["tab1"], ACC)
        U = ctx.enter_context(nc.sbuf_tensor("U1", [P, TILES, D], F32))
        W = ctx.enter_context(nc.sbuf_tensor("W1", [D, D], F32))
        bias = ctx.enter_context(nc.sbuf_tensor("b1", [P, D], F32))
        rs_in = ctx.enter_context(nc.sbuf_tensor("rs_in", [P, TILES], F32))
        chain = sem("chain1")
        with nc.Block() as block:
            @block.gpsimd
            def _(pool):
                pool.wait_ge(chain, 2)
                pool.tensor_tensor(rs_in[:], rs_in[:], g["mhalf"][:, 0:TILES], ALU.pow).then_inc(chain, 1)

            @block.vector
            def _(dve):
                V = nc.vector
                c = Count(dve, chain, 0)
                c.then(V.tensor_copy(g["cnt"][:], ACC[:, :, D]))
                c.then(V.tensor_scalar(rs_in[:], ACC[:, :, D], 1.0, None, ALU.max))
                dve.wait_ge(chain, 3)
                c.n = 3
                c.then(V.tensor_tensor(ACC[:, :, 0:D], ACC[:, :, 0:D], per_tile(rs_in[:]), ALU.mult))
        node_matmul(nc, g, "nm1", ACC[:, :, 0:D], W[:], D,
                    lambda dve, t, m, ps, i, k: nc.vector.tensor_tensor(U[:, bass.ds(t, m), :], ps, per_feature(bias[:], m), ALU.add),
                    loads=((W[:], w["L1_gnn_W"]), (bias[:], w["L1_gnn_b"].partition_broadcast(P))))
        batch_norm(nc, g, "bn1", U, H, w["L1_gnn_gamma"], w["L1_gnn_beta"])
        sem.clear()


def layer_pna(nc, g, w):
    with ExitStack() as ctx:
        sem = Semaphores(nc, ctx, "")
        with ExitStack() as c2:
            H = c2.enter_context(nc.sbuf_tensor("H2", [P, TILES, D], F32))
            B = c2.enter_context(nc.sbuf_tensor("B2", [P, TILES, D], F32))
            W = c2.enter_context(nc.sbuf_tensor("W2s", [D, D], F32))
            layer_norm_relu(nc, g, "ln2", H)
            store_table(nc, "sth2", g["h2"], H[:])
            node_matmul(nc, g, "nm2", H, W[:], D,
                        lambda dve, t, m, ps, i, k: nc.vector.tensor_copy(B[:, bass.ds(t, m), :], ps),
                        loads=((W[:], w["L2_gnn_W_pre"][D:2 * D, :]),))
            store_table(nc, "st2", g["tab2"], B[:])
        ACC = ctx.enter_context(nc.sbuf_tensor("ACC2", [P, TILES, 4 * D], F32))
        moments_pass(nc, g, g["tab2"], ACC)
        mean, low, high, sq = (ACC[:, :, i * D:(i + 1) * D] for i in range(4))
        H = ctx.enter_context(nc.sbuf_tensor("H2b", [P, TILES, D], F32))
        s1 = ctx.enter_context(nc.sbuf_tensor("s1", [P, TILES], F32))
        s2 = ctx.enter_context(nc.sbuf_tensor("s2", [P, TILES], F32))
        has = ctx.enter_context(nc.sbuf_tensor("has", [P, TILES], F32))
        with ExitStack() as c2:
            T = c2.enter_context(nc.sbuf_tensor("T2", [P, TILES, D], F32))
            rd = c2.enter_context(nc.sbuf_tensor("rd", [P, TILES], F32))
            W = c2.enter_context(nc.sbuf_tensor("W2d", [D, D], F32))
            bias = c2.enter_context(nc.sbuf_tensor("b2", [P, D], F32))
            TAS = c2.enter_context(nc.sbuf_tensor("TA", [P, 2, 4, D], F32))
            chain = sem("chain2")
            logs = sem("logs2")
            h_in = sem("h_in2")
            evac = sem("evac2")
            with nc.Block() as block:
                @block.sync
                def _(sp):
                    sp.dma_start(H[:], g["h2"].rearrange("(t p) d -> p t d", p=P)).then_inc(h_in, 16)

                @block.scalar
                def _(act):
                    act.wait_ge(chain, 1)
                    nc.scalar.activation(s2[:], rd[:], ACT.Ln, bias=g["ones"][:, 0:1]).then_inc(logs, 1)
                    act.wait_ge(chain, 4)
                    nc.scalar.activation(T[:], mean, ACT.Square).then_inc(logs, 1)
                    act.wait_ge(chain, 9)
                    nc.scalar.activation(sq, sq, ACT.Sqrt).then_inc(logs, 1)
                    act.wait_ge(logs, 3)

                @block.vector
                def _(dve):
                    V = nc.vector
                    c = Count(dve, chain, 0)
                    c.then(V.tensor_scalar(rd[:], g["cnt"][:], 1.0, None, ALU.max))
                    c.then(V.tensor_scalar(has[:], g["cnt"][:], 0.0, None, ALU.is_gt))
                    dve.wait_ge(logs, 1)
                    c.then(V.reciprocal(rd[:], rd[:]))
                    c.then(V.tensor_tensor(mean, mean, per_tile(rd[:]), ALU.mult))
                    c.then(V.tensor_scalar(s1[:], s2[:], 1.0 / AVG_LOG, None, ALU.mult))
                    c.then(V.reciprocal(s2[:], s1[:]))
                    c.then(V.tensor_tensor(sq, sq, per_tile(rd[:]), ALU.mult))
                    dve.wait_ge(logs, 2)
                    c.then(V.tensor_tensor(sq, sq, T[:], ALU.subtract))
                    c.then(V.tensor_scalar(sq, sq, 0.0, STD_EPS, ALU.max, ALU.add))
                    dve.wait_ge(h_in, 16)

            def own_part(dve, t, m, ps, i, k):
                V = nc.vector
                TA = TAS[:, k]
                c = Count(dve, evac, 2 * (2 * i + k))
                c.then(V.tensor_tensor(TA[:, 0:m, :], ps, per_feature(bias[:], m), ALU.add))
                c.then(V.tensor_tensor(TA[:, 0:m, :], TA[:, 0:m, :], has[:, bass.ds(t, m)].unsqueeze(2).to_broadcast([P, m, D]), ALU.mult))
                for part in (mean, low, high):
                    dst = part[:, bass.ds(t, m), :]
                    ins = V.tensor_tensor(dst, dst, TA[:, 0:m, :], ALU.add)
                return ins

            node_matmul(nc, g, "nm2b", H, W[:], D, own_part,
                        loads=((W[:], w["L2_gnn_W_pre"][0:D, :]), (bias[:], w["L2_gnn_b_pre"].partition_broadcast(P))))
        post_matmul(nc, g, w, ACC, H, s1, s2, mean)
        batch_norm(nc, g, "bn2", mean, H, w["L2_gnn_gamma"], w["L2_gnn_beta"])
        sem.clear()


def post_matmul(nc, g, w, ACC, H, s1, s2, U):
    PARTS = 13
    with ExitStack() as ctx:
        def sb(n, shape):
            return ctx.enter_context(nc.sbuf_tensor("p_" + n, shape, F32))

        sem = Semaphores(nc, ctx, "")

        WF = sb("WF", [P, PARTS, D])
        BIAS = sb("BIAS", [P, D])
        with ExitStack() as c2:
            WP = c2.enter_context(nc.sbuf_tensor("p_WP", [P, PARTS, D], F32))
            WL = c2.enter_context(nc.sbuf_tensor("p_WL", [P, D], F32))
            WPT = c2.enter_context(nc.sbuf_tensor("p_WPT", [P, 2, P], F32))
            PT = c2.enter_context(nc.psum_tensor("p_PT", [P, 2, 512], F32))
            PF = c2.enter_context(nc.psum_tensor("p_PF", [P, 2, 512], F32))
            bp = c2.enter_context(nc.sbuf_tensor("p_bp", [P, 1], F32))
            bl = c2.enter_context(nc.sbuf_tensor("p_bl", [P, D], F32))
            bpr = c2.enter_context(nc.sbuf_tensor("p_bpr", [P, P], F32))
            loaded = sem("p_loaded")
            turned = sem("p_turned")
            turned_in = sem("p_turned_in")
            fused = sem("p_fused")
            fused_in = sem("p_fused_in")
            bias_rep = sem("p_bias_rep")
            with nc.Block() as block:
                @block.sync
                def _(sp):
                    sp.dma_start(WP[:], w["L2_gnn_W_post"].rearrange("(k p) d -> p k d", p=P)).then_inc(loaded, 16)
                    sp.dma_start(WL[:], w["L2_gnn_W_lin"]).then_inc(loaded, 16)
                    sp.dma_start(bp[:], w["L2_gnn_b_post"].unsqueeze(1)).then_inc(loaded, 16)
                    sp.dma_start(bl[:], w["L2_gnn_b_lin"].partition_broadcast(P)).then_inc(loaded, 16)

                @block.tensor
                def _(pe):
                    pe.wait_ge(loaded, 64)
                    for k in range(PARTS + 1):
                        if k < PARTS:
                            wait(pe, turned_in, k - 1)
                            nc.tensor.transpose(PT[:, k % 2, 0:P], WP[:, k, :], g["eye"][:]).then_inc(turned, 1)
                        if k >= 1:
                            pe.wait_ge(turned_in, k)
                            wait(pe, fused_in, k - 2)
                            nc.tensor.matmul(PF[:, (k - 1) % 2, 0:D], WPT[:, (k - 1) % 2, :], WL[:], start=True, stop=True).then_inc(fused, 1)
                    pe.wait_ge(bias_rep, 1)
                    pe.wait_ge(fused_in, PARTS)
                    nc.tensor.matmul(PF[:, 0, 0:D], bpr[:], WL[:], start=True, stop=True).then_inc(fused, 1)

                @block.scalar
                def _(act):
                    for k in range(PARTS):
                        act.wait_ge(turned, k + 1)
                        wait(act, fused, k - 1)
                        nc.scalar.copy(WPT[:, k % 2, :], PT[:, k % 2, 0:P]).then_inc(turned_in, 1)

                @block.vector
                def _(dve):
                    V = nc.vector
                    dve.wait_ge(loaded, 64)
                    V.tensor_scalar(bpr[:], g["ones"][:], bp[:], None, ALU.mult).then_inc(bias_rep, 1)
                    for k in range(PARTS):
                        dve.wait_ge(fused, k + 1)
                        V.tensor_copy(WF[:, k, :], PF[:, k % 2, 0:D]).then_inc(fused_in, 1)
                    dve.wait_ge(fused, PARTS + 1)
                    V.tensor_tensor(BIAS[:], PF[:, 0, 0:D], bl[:], ALU.add).then_inc(fused_in, 1)
                    dve.wait_ge(fused_in, PARTS + 1)
        SG = sb("SG", [P, 2, 5, D])
        HT = sb("HT", [P, 2, 5, P])
        T = sb("T", [P, 2, D])
        TP = ctx.enter_context(nc.psum_tensor("p_TP", [P, 2, 2, 512], F32))
        OP = ctx.enter_context(nc.psum_tensor("p_OP", [P, 2, 512], F32))
        staged = sem("p_staged")
        stood = sem("p_stood")
        turned = sem("p_turned2")
        ht_in = sem("p_ht_in")
        product = sem("p_product")
        chain = sem("p_chain")

        def in_pairs(eng, body):
            body(0, 0)
            body(1, 1)
            with eng.Fori(1, TILES // 2) as i:
                body(2 * i, 0)
                body(2 * i + 1, 1)
            body(TILES - 1, 0)

        with nc.Block() as block:
            @block.gpsimd
            def _(pool):
                def body(t, b):
                    wait_alone(pool, turned, t - 1, stood)
                    pool.tensor_copy(SG[:, b, 0:4, :], ACC[:, bass.ds(t, 1), :].rearrange("p o (a d) -> p (o a) d", a=4))
                    pool.tensor_copy(SG[:, b, 4:5, :], H[:, bass.ds(t, 1), :]).then_inc(staged, 1)
                in_pairs(pool, body)

            @block.tensor
            def _(pe):
                def turn(t, b):
                    pe.wait_ge(staged, t + 1)
                    wait(pe, ht_in, t - 1)
                    for a in range(5):
                        ins = nc.tensor.transpose(TP[:, b, a // 4, (a % 4) * P:(a % 4 + 1) * P], SG[:, b, a, :], g["eye"][:])
                    ins.then_inc(turned, 1)

                def multiply(t, b):
                    pe.wait_ge(ht_in, t + 1)
                    wait(pe, chain, 3 * (t - 1))
                    for a in range(4):
                        nc.tensor.matmul(OP[:, b, 0:3 * D].rearrange("p (r d) -> p r d", r=3), HT[:, b, a, :],
                                         WF[:, 1 + a:PARTS:4, :], start=(a == 0), stop=False)
                    nc.tensor.matmul(OP[:, b, 0:D], HT[:, b, 4, :], WF[:, 0, :], start=False, stop=True).then_inc(product, 1)

                def body(t, b):
                    turn(t, b)
                    if not (isinstance(t, int) and t == 0):
                        multiply(t - 1, 1 - b)
                in_pairs(pe, body)
                multiply(TILES - 1, 0)

            @block.scalar
            def _(act):
                def body(t, b):
                    wait_alone(act, turned, t + 1, stood)
                    wait_alone(act, product, t - 1, stood)
                    nc.scalar.copy(HT[:, b, 0:4, :], TP[:, b, 0, :].rearrange("p (a n) -> p a n", a=4))
                    nc.scalar.copy(HT[:, b, 4, :], TP[:, b, 1, 0:P]).then_inc(ht_in, 1)
                in_pairs(act, body)

            @block.vector
            def _(dve):
                V = nc.vector

                def body(t, b):
                    c = Count(dve, chain, 3 * t)
                    dve.wait_ge(product, t + 1)
                    c.then(V.tensor_tensor(T[:, b], OP[:, b, 0:D], BIAS[:], ALU.add))
                    c.then(V.scalar_tensor_tensor(T[:, b], OP[:, b, D:2 * D], s1[:, bass.ds(t, 1)], T[:, b], ALU.mult, ALU.add))
                    c.then(V.scalar_tensor_tensor(U[:, bass.ds(t, 1), :].rearrange("p o d -> p (o d)"), OP[:, b, 2 * D:3 * D],
                                                  s2[:, bass.ds(t, 1)], T[:, b], ALU.mult, ALU.add))
                in_pairs(dve, body)
        sem.clear()


def layer_gatv2(nc, g, w, out):
    with ExitStack() as ctx:
        sem = Semaphores(nc, ctx, "")
        XLR = ctx.enter_context(nc.sbuf_tensor("XLR", [P, TILES, 2 * D], F32))
        with ExitStack() as c2:
            H = c2.enter_context(nc.sbuf_tensor("H3", [P, TILES, D], F32))
            W = c2.enter_context(nc.sbuf_tensor("W3", [D, 2 * D], F32))
            bias = c2.enter_context(nc.sbuf_tensor("b3", [P, 2 * D], F32))
            layer_norm_relu(nc, g, "ln3", H)
            node_matmul(nc, g, "nm3", H, W[:], 2 * D,
                        lambda dve, t, m, ps, i, k: nc.vector.tensor_tensor(XLR[:, bass.ds(t, m), :], ps, per_feature(bias[:], m), ALU.add),
                        loads=((W[:, 0:D], w["L3_gnn_W_l"]), (W[:, D:2 * D], w["L3_gnn_W_r"]),
                               (bias[:, 0:D], w["L3_gnn_b_l"].partition_broadcast(P)),
                               (bias[:, D:2 * D], w["L3_gnn_b_r"].partition_broadcast(P))))
        att = ctx.enter_context(nc.sbuf_tensor("att3", [D, 1], F32))
        bias = ctx.enter_context(nc.sbuf_tensor("bias3", [P, D], F32))
        loaded = sem("loaded3")
        with nc.Block() as block:
            @block.sync
            def _(sp):
                sp.dma_start(att[:], w["L3_gnn_att"].unsqueeze(1)).then_inc(loaded, 16)
                sp.dma_start(bias[:], w["L3_gnn_bias"].partition_broadcast(P)).then_inc(loaded, 16)
                sp.wait_ge(loaded, 32)
        store_table(nc, "st3", g["tab3"], XLR[:, :, 0:D])
        ACC = ctx.enter_context(nc.sbuf_tensor("ACC3", [P, TILES, D + 1], F32))
        gatv2_pass(nc, g, g["tab3"], XLR[:, :, D:2 * D], ACC, att[:])
        rd = ctx.enter_context(nc.sbuf_tensor("rd3", [P, TILES], F32))
        chain = sem("chain3")
        stored = sem("out_stored")
        with nc.Block() as block:
            @block.vector
            def _(dve):
                V = nc.vector
                c = Count(dve, chain, 0)
                rows = ACC[:, :, 0:D]
                c.then(V.tensor_scalar(rd[:], ACC[:, :, D], SOFTMAX_EPS, None, ALU.add))
                c.then(V.reciprocal(rd[:], rd[:]))
                c.then(V.tensor_tensor(rows, rows, per_tile(rd[:]), ALU.mult))
                c.then(V.tensor_tensor(rows, rows, per_feature(bias[:]), ALU.add))
                c.then(V.scalar_tensor_tensor(g["X"][:], rows, 0.0, g["X"][:], ALU.max, ALU.add))

            @block.sync
            def _(sp):
                sp.wait_ge(chain, 5)
                whole = (TILES - 1) * P
                sp.dma_start(out[0:whole, :].rearrange("(t p) d -> p t d", p=P), g["X"][:, 0:TILES - 1, :]).then_inc(stored, 16)
                sp.dma_start(out[whole:N, :], g["X"][0:LAST, TILES - 1, :]).then_inc(stored, 16)
                sp.wait_ge(stored, 32)


def gnn_kernel(nc, w, out):
    with ExitStack() as ctx:
        g = whole_program_tensors(nc, ctx)
        build_steps(nc, g, w["src"], w["dst"])
        with ExitStack() as c2:
            sem = Semaphores(nc, c2, "")
            x_in = sem("x_in")
            padded = sem("padded")
            with nc.Block() as block:
                @block.gpsimd
                def _(pool):
                    pool.memset(g["X"][:, TILES - 1, :], 0.0).then_inc(padded, 1)

                @block.sync
                def _(sp):
                    whole = (TILES - 1) * P
                    sp.dma_start(g["X"][:, 0:TILES - 1, :], w["x"][0:whole, :].rearrange("(t p) d -> p t d", p=P)).then_inc(x_in, 16)
                    sp.wait_ge(padded, 1)
                    sp.dma_start(g["X"][0:LAST, TILES - 1, :], w["x"][whole:N, :]).then_inc(x_in, 16)
                    sp.wait_ge(x_in, 32)
            sem.clear()
        layer_gat(nc, g, w)
        layer_gcn(nc, g, w)
        layer_pna(nc, g, w)
        layer_gatv2(nc, g, w, out)


_INS = ['x', 'src', 'dst', 'L0_gnn_W', 'L0_gnn_att_src', 'L0_gnn_att_dst', 'L0_gnn_bias', 'L0_gnn_bn_gamma',
        'L0_gnn_bn_beta', 'L1_gnn_W', 'L1_gnn_b', 'L1_gnn_gamma', 'L1_gnn_beta', 'L2_gnn_W_pre', 'L2_gnn_b_pre',
        'L2_gnn_W_post', 'L2_gnn_b_post', 'L2_gnn_W_lin', 'L2_gnn_b_lin', 'L2_gnn_gamma', 'L2_gnn_beta',
        'L3_gnn_W_l', 'L3_gnn_b_l', 'L3_gnn_W_r', 'L3_gnn_b_r', 'L3_gnn_att', 'L3_gnn_bias']


def kernel(**inputs):
    import numpy as _np
    import concourse.bacc as _bacc
    from concourse.bass_utils import run_bass_kernel_spmd as _run

    nc = _bacc.Bacc("TRN2", target_bir_lowering=False, num_devices=1)
    arrays, args = {}, {}
    for name in _INS:
        a = _np.ascontiguousarray(inputs[name])
        arrays[f"in_{name}_dram"] = a
        args[name] = nc.dram_tensor(f"in_{name}_dram", a.shape, mybir.dt.from_np(a.dtype), kind="ExternalInput").ap()
    out = nc.dram_tensor("out_dram", (N, D), F32, kind="ExternalOutput").ap()
    gnn_kernel(nc, args, out)
    r = _run(nc, [arrays], core_ids=[0])
    return r.results[0]["out_dram"]
```

```python
import concourse.bass as bass
from concourse import mybir
from contextlib import ExitStack
import math

F32, I32, BF16 = mybir.dt.float32, mybir.dt.int32, mybir.dt.bfloat16
ALU, ACT, AX = mybir.AluOpType, mybir.ActivationFunctionType, mybir.AxisListType

P = 128
D = 128
N = 6250
E = 100000
TILES = -(-N // P)
LAST = N - (TILES - 1) * P
CHUNKS = -(-E // P)
FULL = E // P
TAIL = E - FULL * P
GROUP = 8
GROUPS = -(-(CHUNKS + TILES - 1) // GROUP)
STEPS = GROUPS * GROUP
IT = -(-(STEPS + GROUP) // P)
SPAD = IT * P
SLOTS = GROUP * P
BIG = 1e38
HEADS, HF = 8, 16
LN_EPS = BN_EPS = STD_EPS = 1e-5
SOFTMAX_EPS = 1e-16
SLOPE = 0.2
AVG_LOG = math.log(17.0)
TG = 7
NG = TILES // TG


def whole_program_tensors(nc, ctx):
    g = {}

    def sb(name, shape, dt):
        g[name] = ctx.enter_context(nc.sbuf_tensor(name, shape, dt))

    g["gathered"] = [ctx.enter_context(nc.semaphore(f"gathered{b}")) for b in range(4)]
    g["rows_gathered"] = [16 * IT, 0, 0, 0]
    sb("eye", [P, P], F32)
    sb("iota_row", [P, P], F32)
    sb("iota_col", [P, 1], F32)
    sb("ones", [P, P], F32)
    sb("mhalf", [P, P], F32)
    sb("loc", [P, SPAD], F32)
    sb("loc_end", [P, SPAD], F32)
    sb("src_idx", [P, SPAD], I32)
    sb("tile_row", [1, SPAD], I32)
    sb("rs_out", [P, TILES], F32)
    sb("cnt", [P, TILES], F32)
    sb("X", [P, TILES, D], F32)
    for name, shape, dt in (
        ("step_rows", (CHUNKS + 2, 2 * P), I32),
        ("keys", (P + SPAD * P + P,), F32),
        ("row_loc", (SPAD * P,), BF16),
        ("row_start", (SPAD * P,), BF16),
        ("row_end", (SPAD * P,), BF16),
        ("tab0", (TILES * P, D + HEADS), F32),
        ("tab1", (TILES * P, D), F32),
        ("tab2", (TILES * P, D), F32),
        ("tab3", (TILES * P, D), F32),
        ("h2", (TILES * P, D), F32),
    ):
        g[name] = nc.dram_tensor("dr_" + name, shape, dt, kind="Internal").ap()
    return g


def wait(eng, sem, value):
    if isinstance(value, int) and value <= 0:
        return
    eng.wait_ge(sem, value)


def wait_alone(eng, sem, value, stood):
    if isinstance(value, int) and value <= 0:
        return
    eng.wait_ge(sem, value)
    if not isinstance(value, int):
        eng.sem_inc(stood, 1)


def in_groups_of_two(eng, body):
    body(0, 0, 0)
    body(1, 0, 1)
    with eng.Fori(1, GROUPS // 2) as i:
        body(2 * i, i, 0)
        body(2 * i + 1, i, 1)


def in_groups_of_four(eng, body):
    rounds = GROUPS // 4
    for b in range(4):
        body(b, 0, b)
    with eng.Fori(1, rounds - 1) as i:
        for b in range(4):
            body(4 * i + b, i, b)
    for b in range(4):
        body(4 * (rounds - 1) + b, rounds - 1, b)


def is_first(k):
    return isinstance(k, int) and k == 0


def is_last(k):
    return isinstance(k, int) and k == GROUPS - 1


def load_tiles(nc, engine, row, lo, n, top=TILES - 1):
    _, vals = nc.values_load_multi_w_load_instructions(
        row[0:1, bass.ds(lo, n)], engines=[engine], min_val=0, max_val=top,
        skip_runtime_bounds_check_because="the row is clamped to the last tile when it is built")
    return vals


class Semaphores:

    def __init__(self, nc, ctx, prefix):
        self.nc, self.ctx, self.prefix, self.all = nc, ctx, prefix, []

    def __call__(self, name):
        self.all.append(self.ctx.enter_context(self.nc.semaphore(self.prefix + name)))
        return self.all[-1]

    def clear(self):
        with self.nc.Block() as block:
            @block.sync
            def _(sp):
                for s in self.all:
                    sp.sem_clear(s)


def build_steps(nc, g, src, dst):
    with ExitStack() as ctx:
        def sb(name, shape, dt):
            return ctx.enter_context(nc.sbuf_tensor(name, shape, dt))

        sem = Semaphores(nc, ctx, "")

        last_dst = sb("last_dst", [P, IT], I32)
        tail = sb("tail", [3, 2 * P], I32)
        fin = sb("fin", [P, IT], F32)
        big = sb("big", [P, IT], F32)
        itmp = sb("itmp", [P, IT], I32)
        iota_p = sb("iota_p", [P, IT], F32)
        iota_s = sb("iota_s", [P, SPAD], F32)
        ints = sb("ints", [P, SPAD], I32)
        intp = sb("intp", [P, IT], I32)
        before = sb("before", [P, IT, SPAD], BF16)
        ones_bf = sb("ones_bf", [P, P], BF16)
        crep = sb("crep", [P, SPAD], F32)
        chunk_f = sb("chunk_f", [P, IT], F32)
        chunk_i = sb("chunk_i", [P, IT], I32)
        tile_c = sb("tile_c", [P, IT], F32)
        edges = sb("edges", [P, IT, 2 * P], I32)
        ef = sb("ef", [P, IT, 2 * P], F32)
        locp = sb("locp", [P, IT, P], F32)
        v = sb("v", [P, IT, P], F32)
        v2 = sb("v2", [P, IT, P], F32)
        key = sb("key", [P, IT, P], F32)
        kprev = sb("kprev", [P, IT, P], F32)
        knext = sb("knext", [P, IT, P], F32)
        padrow = sb("padrow", [1, P], F32)
        b_loc = sb("b_loc", [P, IT, P], BF16)
        b_start = sb("b_start", [P, IT, P], BF16)
        b_end = sb("b_end", [P, IT, P], BF16)
        lo_i = sb("lo_i", [P, SPAD], I32)
        hi_i = sb("hi_i", [P, SPAD], I32)
        lo_f = sb("lo_f", [P, SPAD], BF16)
        hi_f = sb("hi_f", [P, SPAD], F32)
        iota_bf = sb("iota_bf", [P, P], BF16)
        apart = sb("apart", [P, 2, 16, TILES], F32)
        square = sb("square", [P, 16, TILES], F32)
        eq_lo = sb("eq_lo", [P, 2, 16, P], BF16)
        eq_hi = sb("eq_hi", [P, 2, 16, TILES], BF16)
        deg = sb("deg", [P, TILES], F32)
        ps_c = ctx.enter_context(nc.psum_tensor("ps_c", [P, 2, 512], F32))
        ps_p = ctx.enter_context(nc.psum_tensor("ps_p", [P, 512], F32))
        ps_t = ctx.enter_context(nc.psum_tensor("ps_t", [P, 3, 512], F32))
        ps_h = ctx.enter_context(nc.psum_tensor("ps_h", [P, 2, 512], F32))
        HALF = SPAD // 2

        consts = sem("consts")
        setup = sem("setup")
        copied = sem("copied")
        tail_in = sem("tail_in")
        last_in = sem("last_in")
        v_done = sem("v_done")
        counted = sem("counted")
        gathered = g["gathered"][0]
        keys_out = sem("keys_out")
        near_in = sem("near_in")
        rows_out = sem("rows_out")
        turned = sem("turned")
        hist = sem("hist")
        added = sem("added")
        onehots = sem("onehots")
        apart_done = sem("apart_done")
        squared = sem("squared")
        hi_onehots = sem("hi_onehots")
        stood = sem("stood")

        with nc.Block() as block:
            @block.gpsimd
            def _(pool):
                pool.memset(g["eye"][:], 0.0).then_inc(setup, 1)
                pool.memset(g["ones"][:], 1.0).then_inc(setup, 1)
                pool.memset(ones_bf[:], 1.0).then_inc(setup, 1)
                pool.memset(g["mhalf"][:], -0.5).then_inc(setup, 1)
                pool.memset(tail[:, 0:P], 0).then_inc(setup, 1)
                pool.memset(tail[:, P:2 * P], -1).then_inc(setup, 1)
                pool.memset(last_dst[:], 0).then_inc(setup, 1)
                pool.memset(padrow[:], -1.0).then_inc(setup, 1)
                pool.iota(ints[:], pattern=[[1, SPAD]], base=0, channel_multiplier=0).then_inc(setup, 1)
                pool.iota(intp[:], pattern=[[P, IT]], base=0, channel_multiplier=1).then_inc(setup, 1)
                pool.wait_ge(setup, 10)
                pool.affine_select(out=g["eye"][:], in_=g["eye"][:], compare_op=ALU.not_equal, fill=1.0,
                                   base=0, pattern=[[-1, P]], channel_multiplier=1).then_inc(consts, 1)
                pool.wait_ge(copied, 16 * 3)
                pool.wait_ge(v_done, 7)
                for k in range(IT):
                    pool.indirect_dma_start(
                        out=edges[:, k, :], out_offset=None, in_=g["step_rows"][:, :],
                        in_offset=bass.IndirectOffsetOnAxis(ap=chunk_i[:, k:k + 1], axis=0)).then_inc(gathered, 16)

                def tiles_apart(i, b):
                    pool.tensor_tensor(apart[:, b], g["iota_row"][:, 0:TILES].unsqueeze(1).to_broadcast([P, 16, TILES]),
                                       hi_f[:, bass.ds(i * 16, 16)].unsqueeze(2).to_broadcast([P, 16, TILES]),
                                       ALU.subtract).then_inc(apart_done, 1)

                pool.wait_ge(v_done, 34)
                tiles_apart(0, 0)
                tiles_apart(1, 1)
                with pool.Fori(1, STEPS // 32) as i:
                    for b in range(2):
                        wait_alone(pool, squared, 2 * i + b - 1, stood)
                        tiles_apart(2 * i + b, b)

                pool.wait_ge(added, STEPS // 16 + 3)
                pool.tensor_tensor(g["rs_out"][:], deg[:], g["mhalf"][:, 0:TILES], ALU.pow).then_inc(added, 1)
                pool.wait_ge(added, STEPS // 16 + 4)

            @block.sync
            def _(sp):
                sp.dma_start(g["step_rows"][0:FULL, 0:P],
                             src[0:FULL * P].rearrange("(c e) -> c e", e=P)).then_inc(copied, 16)
                sp.dma_start(g["step_rows"][0:FULL, P:2 * P],
                             dst[0:FULL * P].rearrange("(c e) -> c e", e=P)).then_inc(copied, 16)
                sp.wait_ge(setup, 10)
                sp.dma_start(tail[0:1, 0:TAIL], src[FULL * P:E].unsqueeze(0)).then_inc(tail_in, 16)
                sp.dma_start(tail[0:1, P:P + TAIL], dst[FULL * P:E].unsqueeze(0)).then_inc(tail_in, 16)
                lasts = dst[0:FULL * P].rearrange("(c e) -> c e", e=P)[:, P - 1:P]
                whole = FULL // P
                sp.dma_start(last_dst[:, 0:whole],
                             lasts[0:whole * P, :].rearrange("(k p) o -> p (k o)", p=P),
                             allow_slow_non_contiguous=True).then_inc(last_in, 16)
                sp.dma_start(last_dst[0:FULL - whole * P, whole:whole + 1],
                             lasts[whole * P:FULL, :], allow_slow_non_contiguous=True).then_inc(last_in, 16)
                sp.dma_start(last_dst[FULL - whole * P:CHUNKS - whole * P, whole:whole + 1],
                             dst[E - 1:E].unsqueeze(0)).then_inc(last_in, 16)
                sp.wait_ge(tail_in, 32)
                sp.dma_start(g["step_rows"][FULL:FULL + 3, :], tail[:]).then_inc(copied, 16)
                body = g["keys"][P:P + SPAD * P].rearrange("(k p e) -> p k e", p=P, e=P)
                sp.wait_ge(v_done, 14)
                sp.dma_start(body, key[:]).then_inc(keys_out, 16)
                sp.dma_start(g["keys"][0:P].unsqueeze(0), padrow[:]).then_inc(keys_out, 16)
                sp.dma_start(g["keys"][P + SPAD * P:2 * P + SPAD * P].unsqueeze(0), padrow[:]).then_inc(keys_out, 16)
                sp.wait_ge(keys_out, 48)
                sp.dma_start(kprev[:], g["keys"][P - 1:P - 1 + SPAD * P].rearrange("(k p e) -> p k e", p=P, e=P)).then_inc(near_in, 16)
                sp.dma_start(knext[:], g["keys"][P + 1:P + 1 + SPAD * P].rearrange("(k p e) -> p k e", p=P, e=P)).then_inc(near_in, 16)
                sp.wait_ge(v_done, 20)
                for row, tile in (("row_loc", b_loc), ("row_start", b_start), ("row_end", b_end)):
                    sp.dma_start(g[row].rearrange("(k p e) -> p k e", p=P, e=P), tile[:]).then_inc(rows_out, 16)
                sp.wait_ge(rows_out, 48)

            @block.scalar
            def _(act):
                def tiles_onehot(i, b):
                    wait_alone(act, apart_done, i + 1, stood)
                    wait_alone(act, hi_onehots, i, stood)
                    nc.scalar.activation(square[:], apart[:, b], ACT.Square).then_inc(squared, 1)
                    wait_alone(act, squared, i + 1, stood)
                    wait_alone(act, hist, i - 1, stood)
                    nc.scalar.activation(eq_hi[:, b], square[:], ACT.Relu, bias=g["ones"][:, 0:1], scale=-1.0).then_inc(hi_onehots, 1)

                act.wait_ge(setup, 10)
                tiles_onehot(0, 0)
                tiles_onehot(1, 1)
                with act.Fori(1, STEPS // 32) as i:
                    for b in range(2):
                        tiles_onehot(2 * i + b, b)

            @block.vector
            def _(dve):
                V = nc.vector
                n = [0]

                def step(ins):
                    n[0] += 1
                    ins.then_inc(v_done, 1)

                def then(ins):
                    step(ins)
                    dve.wait_ge(v_done, n[0])

                dve.wait_ge(setup, 10)
                V.tensor_copy(g["iota_row"][:], ints[:, 0:P]).then_inc(consts, 1)
                V.tensor_copy(iota_s[:], ints[:]).then_inc(consts, 1)
                V.tensor_copy(iota_p[:], intp[:]).then_inc(consts, 1)
                V.tensor_copy(g["iota_col"][:], intp[:, 0:1]).then_inc(consts, 1)
                dve.wait_ge(consts, 5)
                dve.wait_ge(last_in, 48)
                then(V.tensor_single_scalar(itmp[:], last_dst[:], 7, op=ALU.logical_shift_right))
                then(V.tensor_tensor(fin[:], itmp[:], iota_p[:], ALU.add))
                then(V.tensor_scalar(big[:], iota_p[:], float(CHUNKS), 1e6, ALU.is_ge, ALU.mult))
                then(V.tensor_tensor(fin[:], fin[:], big[:], ALU.max))
                for k in range(IT):
                    ins = V.tensor_scalar(before[:, k, :], iota_s[:], fin[:, k:k + 1], None, ALU.is_gt)
                step(ins)
                dve.wait_ge(counted, 1)
                then(V.tensor_copy(chunk_f[:], ps_p[:, 0:IT]))
                then(V.tensor_copy(chunk_i[:], chunk_f[:]))
                then(V.tensor_tensor(tile_c[:], iota_p[:], chunk_f[:], ALU.subtract))
                then(V.tensor_scalar(tile_c[:], tile_c[:], float(TILES - 1), float(P), ALU.min, ALU.mult))
                for h in range(2):
                    ins = V.tensor_copy(crep[:, h * HALF:(h + 1) * HALF], ps_c[:, h, 0:HALF])
                then(ins)
                then(V.tensor_tensor(crep[:], iota_s[:], crep[:], ALU.subtract))
                V.tensor_scalar(g["tile_row"][:], crep[0:1, :], float(TILES - 1), None, ALU.min).then_inc(consts, 1)
                dve.wait_ge(gathered, 16 * IT)
                then(V.tensor_copy(ef[:], edges[:]))
                V_tile = tile_c[:].unsqueeze(2).to_broadcast([P, IT, P])
                V.tensor_tensor(locp[:], ef[:, :, P:2 * P], V_tile, ALU.subtract).then_inc(turned, 1)
                dve.wait_ge(turned, 1)
                V.tensor_scalar(v[:], locp[:], 0.0, None, ALU.is_ge).then_inc(turned, 1)
                dve.wait_ge(turned, 2)
                V.scalar_tensor_tensor(v2[:], locp[:], float(P), v[:], ALU.is_lt, ALU.mult).then_inc(turned, 1)
                dve.wait_ge(turned, 3)
                then(V.scalar_tensor_tensor(locp[:], locp[:], 1.0, v2[:], ALU.add, ALU.mult))
                step(V.scalar_tensor_tensor(key[:], ef[:, :, P:2 * P], 1.0, v2[:], ALU.add, ALU.mult))
                step(V.tensor_scalar(b_loc[:], locp[:], -1.0, None, ALU.add))
                dve.wait_ge(near_in, 32)
                then(V.tensor_tensor(v[:], key[:], kprev[:], ALU.not_equal))
                step(V.tensor_scalar(b_start[:], v[:], -BIG, None, ALU.mult))
                then(V.tensor_tensor(v2[:], key[:], knext[:], ALU.not_equal))
                step(V.tensor_scalar(b_end[:], v2[:], -BIG, None, ALU.mult))
                then(V.tensor_tensor(key[:], locp[:], v2[:], ALU.mult))
                for k in range(IT):
                    dve.wait_ge(counted, 2 + k)
                    cols = slice(k * P, (k + 1) * P)
                    V.tensor_scalar(g["loc"][:, cols], ps_t[:, 0, 0:P], -1.0, None, ALU.add)
                    V.tensor_scalar(g["loc_end"][:, cols], ps_t[:, 1, 0:P], -1.0, None, ALU.add)
                    ins = V.tensor_copy(g["src_idx"][:, cols], ps_t[:, 2, 0:P])
                    then(ins)
                then(V.tensor_single_scalar(lo_i[:], g["src_idx"][:], P - 1, op=ALU.bitwise_and))
                then(V.tensor_single_scalar(hi_i[:], g["src_idx"][:], 7, op=ALU.logical_shift_right))
                then(V.tensor_copy(lo_f[:], lo_i[:]))
                then(V.tensor_copy(hi_f[:], hi_i[:]))
                then(V.tensor_scalar(crep[:], g["loc"][:], 0.0, None, ALU.is_ge))
                then(V.scalar_tensor_tensor(hi_f[:], hi_f[:], 1.0, crep[:], ALU.add, ALU.mult))
                then(V.tensor_scalar(hi_f[:], hi_f[:], -1.0, None, ALU.add))
                V.tensor_copy(iota_bf[:], g["iota_row"][:]).then_inc(added, 1)
                dve.wait_ge(added, 1)
                V.memset(deg[:], 0.0).then_inc(added, 1)

                def onehot(i, b):
                    V.tensor_tensor(eq_lo[:, b], iota_bf[:].unsqueeze(1).to_broadcast([P, 16, P]),
                                    lo_f[:, bass.ds(i * 16, 16)].unsqueeze(2).to_broadcast([P, 16, P]),
                                    ALU.is_equal).then_inc(onehots, 1)

                onehot(0, 0)
                onehot(1, 1)
                with dve.Fori(1, STEPS // 32) as i:
                    for b in range(2):
                        dve.wait_ge(hist, 2 * i + b - 1)
                        dve.wait_ge(added, 2 * i + b)
                        V.tensor_tensor(deg[:], deg[:], ps_h[:, b, 0:TILES], ALU.add).then_inc(added, 1)
                        onehot(2 * i + b, b)
                for b in range(2):
                    dve.wait_ge(hist, STEPS // 16 - 1 + b)
                    dve.wait_ge(added, STEPS // 16 + b)
                    V.tensor_tensor(deg[:], deg[:], ps_h[:, b, 0:TILES], ALU.add).then_inc(added, 1)
                dve.wait_ge(added, STEPS // 16 + 2)
                V.tensor_scalar(deg[:], deg[:], 1.0, None, ALU.max).then_inc(added, 1)

            @block.tensor
            def _(pe):
                pe.wait_ge(v_done, 5)
                for h in range(2):
                    for k in range(IT):
                        nc.tensor.matmul(ps_c[:, h, 0:HALF], ones_bf[:], before[:, k, h * HALF:(h + 1) * HALF],
                                         start=(k == 0), stop=(k == IT - 1))
                for s in range(IT):
                    for k in range(IT):
                        ins = nc.tensor.matmul(ps_p[:, s:s + 1], before[:, k, s * P:(s + 1) * P], ones_bf[:, 0:1],
                                               start=(k == 0), stop=(k == IT - 1))
                ins.then_inc(counted, 1)
                pe.wait_ge(consts, 1)
                pe.wait_ge(v_done, 20)
                for k in range(IT):
                    if k:
                        pe.wait_ge(v_done, 20 + k)
                    for j, m in enumerate((locp[:, k, :], key[:, k, :], ef[:, k, 0:P])):
                        ins = nc.tensor.transpose(ps_t[:, j, 0:P], m, g["eye"][:])
                    ins.then_inc(counted, 1)

                def count(i, b):
                    pe.wait_ge(onehots, i + 1)
                    pe.wait_ge(hi_onehots, i + 1)
                    for s in range(16):
                        ins = nc.tensor.matmul(ps_h[:, b, 0:TILES], eq_lo[:, b, s, :], eq_hi[:, b, s, :],
                                               start=(s == 0), stop=(s == 15))
                    ins.then_inc(hist, 1)

                count(0, 0)
                count(1, 1)
                with pe.Fori(1, STEPS // 32) as i:
                    for b in range(2):
                        count(2 * i + b, b)
        sem.clear()


def per_tile(v):
    return v.unsqueeze(2).to_broadcast([P, TILES, D])


def per_feature(v, tiles=TILES):
    return v.unsqueeze(1).to_broadcast([P, tiles, v.shape[1]])


def norm_matmul(nc, g, name, H, W, NC, evacuate, loads=(), stores=()):
    per = 512 // NC if W is not None else TG
    banks = [(u, min(per, TG - u)) for u in range(0, TG, per)]
    with ExitStack() as ctx:
        sem = Semaphores(nc, ctx, name)
        SQ = ctx.enter_context(nc.sbuf_tensor(name + "_sq", [P, 2, TG, D], F32))
        total = ctx.enter_context(nc.sbuf_tensor(name + "_total", [P, TILES], F32))
        var = ctx.enter_context(nc.sbuf_tensor(name + "_var", [P, TILES], F32))
        if W is not None:
            HT = ctx.enter_context(nc.sbuf_tensor(name + "_ht", [P, TG, P], F32))
            TP = ctx.enter_context(nc.psum_tensor(name + "_tp", [P, 2, 2, 512], F32))
            OP = ctx.enter_context(nc.psum_tensor(name + "_op", [P, len(banks), 512], F32))
        loaded = sem("_loaded")
        totalled = sem("_totalled")
        centred = sem("_centred")
        squared = sem("_squared")
        var_done = sem("_var_done")
        scaled = sem("_scaled")
        root = sem("_root")
        normed = sem("_normed")
        turned = sem("_turned")
        ht_in = sem("_ht_in")
        product = sem("_product")
        taken = sem("_taken")
        stored = sem("_stored")

        def tiles(i):
            return slice(i * TG, (i + 1) * TG)

        def rep_tiles(v, i):
            return v[:, tiles(i)].unsqueeze(2).to_broadcast([P, TG, D])

        with nc.Block() as block:
            @block.sync
            def _(sp):
                for o, i in loads:
                    sp.dma_start(o, i).then_inc(loaded, 16)
                for i in range(NG):
                    for table, rows, after_product in stores:
                        sp.wait_ge(taken if after_product else normed, i + 1)
                        sp.dma_start(table.rearrange("(t p) d -> p t d", p=P)[:, tiles(i), :], rows[:, tiles(i), :]).then_inc(stored, 16)
                if stores:
                    sp.wait_ge(stored, 16 * len(stores) * NG)

            @block.gpsimd
            def _(pool):
                for i in range(NG):
                    pool.wait_ge(var_done, i + 1)
                    pool.tensor_scalar(var[:, tiles(i)], var[:, tiles(i)], 1.0 / D, LN_EPS, ALU.mult, ALU.add).then_inc(scaled, 1)
                    pool.wait_ge(scaled, i + 1)
                    pool.tensor_tensor(var[:, tiles(i)], var[:, tiles(i)], g["mhalf"][:, 0:TG], ALU.pow).then_inc(root, 1)

            @block.tensor
            def _(pe):
                if W is None:
                    return
                if loads:
                    pe.wait_ge(loaded, 16 * len(loads))
                for i in range(NG + 1):
                    if i < NG:
                        pe.wait_ge(normed, i + 1)
                        for u in range(TG):
                            ins = nc.tensor.transpose(TP[:, i % 2, u // 4, (u % 4) * P:(u % 4 + 1) * P], H[:, i * TG + u, :], g["eye"][:])
                        ins.then_inc(turned, 1)
                    if i > 0:
                        wait(pe, taken, i - 1)
                        pe.wait_ge(ht_in, i)
                        for u in range(TG):
                            ins = nc.tensor.matmul(OP[:, u // per, (u % per) * NC:(u % per + 1) * NC], HT[:, u, :], W,
                                                   start=True, stop=True)
                        ins.then_inc(product, 1)

            @block.scalar
            def _(act):
                for j in range(NG + 3):
                    if j < NG:
                        act.wait_ge(centred, j + 1)
                        wait(act, var_done, j - 1)
                        nc.scalar.activation(SQ[:, j % 2], H[:, tiles(j), :], ACT.Square).then_inc(squared, 1)
                    i = j - 3
                    if i >= 0 and W is not None:
                        act.wait_ge(turned, i + 1)
                        wait(act, product, i)
                        nc.scalar.copy(HT[:, 0:4, :], TP[:, i % 2, 0, :].rearrange("p (u n) -> p u n", n=P))
                        nc.scalar.copy(HT[:, 4:TG, :], TP[:, i % 2, 1, 0:(TG - 4) * P].rearrange("p (u n) -> p u n", n=P)).then_inc(ht_in, 1)

            @block.vector
            def _(dve):
                V = nc.vector
                if loads:
                    dve.wait_ge(loaded, 16 * len(loads))
                for j in range(NG + 3):
                    if j < NG:
                        V.tensor_reduce(total[:, tiles(j)], g["X"][:, tiles(j), :], AX.X, ALU.add).then_inc(totalled, 1)
                        dve.wait_ge(totalled, j + 1)
                        V.scalar_tensor_tensor(H[:, tiles(j), :], rep_tiles(total, j), -1.0 / D, g["X"][:, tiles(j), :],
                                               ALU.mult, ALU.add).then_inc(centred, 1)
                    i = j - 1
                    if 0 <= i < NG:
                        dve.wait_ge(squared, i + 1)
                        V.tensor_reduce(var[:, tiles(i)], SQ[:, i % 2], AX.X, ALU.add).then_inc(var_done, 1)
                    i = j - 2
                    if 0 <= i < NG:
                        dve.wait_ge(root, i + 1)
                        V.scalar_tensor_tensor(H[:, tiles(i), :], H[:, tiles(i), :], 0.0, rep_tiles(var, i),
                                               ALU.max, ALU.mult).then_inc(normed, 1)
                    i = j - 3
                    if i >= 0:
                        if W is None:
                            dve.wait_ge(normed, i + 1)
                            ins = evacuate(i)
                        else:
                            dve.wait_ge(product, i + 1)
                            for k, (u, m) in enumerate(banks):
                                ins = evacuate(i, i * TG + u, m, OP[:, k, 0:m * NC].rearrange("p (u n) -> p u n", n=NC), k)
                        ins.then_inc(taken, 1)
                dve.wait_ge(taken, NG)
        sem.clear()


def node_matmul(nc, g, name, SRC, W, NC, evacuate, loads=()):
    per = 512 // NC
    banks = [(u, min(per, TG - u)) for u in range(0, TG, per)]
    with ExitStack() as ctx:
        sem = Semaphores(nc, ctx, name)
        STG = ctx.enter_context(nc.sbuf_tensor(name + "_stage", [P, TG, D], F32))
        HT = ctx.enter_context(nc.sbuf_tensor(name + "_ht", [P, TG, P], F32))
        TP = ctx.enter_context(nc.psum_tensor(name + "_tp", [P, 2, 512], F32))
        OP = ctx.enter_context(nc.psum_tensor(name + "_op", [P, len(banks), 512], F32))
        loaded = sem("_loaded")
        staged = sem("_staged")
        stood = sem("_stood")
        turned = sem("_turned")
        ht_in = sem("_ht_in")
        product = sem("_product")
        taken = sem("_taken")

        def groups(eng, body):
            body(0)
            with eng.Fori(1, NG) as i:
                body(i)

        with nc.Block() as block:
            @block.sync
            def _(sp):
                for o, i in loads:
                    sp.dma_start(o, i).then_inc(loaded, 16)

            @block.gpsimd
            def _(pool):
                def body(i):
                    wait_alone(pool, turned, i, stood)
                    pool.tensor_copy(STG[:], SRC[:, bass.ds(i * TG, TG), :]).then_inc(staged, 1)
                groups(pool, body)

            @block.tensor
            def _(pe):
                if loads:
                    pe.wait_ge(loaded, 16 * len(loads))

                def body(i):
                    pe.wait_ge(staged, i + 1)
                    for u in range(TG):
                        ins = nc.tensor.transpose(TP[:, u // 4, (u % 4) * P:(u % 4 + 1) * P], STG[:, u, :], g["eye"][:])
                    ins.then_inc(turned, 1)
                    wait(pe, taken, i)
                    pe.wait_ge(ht_in, i + 1)
                    for u in range(TG):
                        ins = nc.tensor.matmul(OP[:, u // per, (u % per) * NC:(u % per + 1) * NC], HT[:, u, :], W,
                                               start=True, stop=True)
                    ins.then_inc(product, 1)
                groups(pe, body)

            @block.scalar
            def _(act):
                def body(i):
                    wait_alone(act, turned, i + 1, stood)
                    nc.scalar.copy(HT[:, 0:4, :], TP[:, 0, :].rearrange("p (u n) -> p u n", n=P))
                    nc.scalar.copy(HT[:, 4:TG, :], TP[:, 1, 0:(TG - 4) * P].rearrange("p (u n) -> p u n", n=P)).then_inc(ht_in, 1)
                groups(act, body)

            @block.vector
            def _(dve):
                if loads:
                    dve.wait_ge(loaded, 16 * len(loads))

                def body(i):
                    wait(dve, taken, i)
                    dve.wait_ge(product, i + 1)
                    for k, (u, m) in enumerate(banks):
                        ins = evacuate(dve, i * TG + u, m, OP[:, k, 0:m * NC].rearrange("p (u n) -> p u n", n=NC),
                                       i, k)
                    ins.then_inc(taken, 1)
                groups(dve, body)
                dve.wait_ge(taken, NG)
        sem.clear()


def batch_norm(nc, g, name, U, H, gamma, beta):
    with ExitStack() as ctx:
        sem = Semaphores(nc, ctx, name)
        SQ = ctx.enter_context(nc.sbuf_tensor(name + "_sq", [P, TILES, D], F32))
        gam = ctx.enter_context(nc.sbuf_tensor(name + "_gam", [P, D], F32))
        bet = ctx.enter_context(nc.sbuf_tensor(name + "_bet", [P, D], F32))
        mean = ctx.enter_context(nc.sbuf_tensor(name + "_mean", [P, D], F32))
        scl = ctx.enter_context(nc.sbuf_tensor(name + "_scl", [P, D], F32))
        PM = ctx.enter_context(nc.psum_tensor(name + "_pm", [P, 512], F32))
        PV = ctx.enter_context(nc.psum_tensor(name + "_pv", [P, 512], F32))
        loaded = sem("_loaded")
        summed = sem("_summed")
        centred = sem("_centred")
        squared = sem("_squared")
        stat = sem("_stat")
        root = sem("_root")
        residual = sem("_residual")
        stood = sem("_stood")

        with nc.Block() as block:
            @block.gpsimd
            def _(pool):
                pool.tensor_tensor(g["X"][:], g["X"][:], H[:], ALU.add).then_inc(residual, 1)
                pool.wait_ge(stat, 2)
                pool.tensor_tensor(scl[:], scl[:], g["mhalf"][:], ALU.pow).then_inc(root, 1)

            @block.sync
            def _(sp):
                sp.dma_start(gam[:], gamma.partition_broadcast(P)).then_inc(loaded, 16)
                sp.dma_start(bet[:], beta.partition_broadcast(P)).then_inc(loaded, 16)

            @block.tensor
            def _(pe):
                def column_sums(out, A, ready=None):
                    def tile(t, start):
                        nc.tensor.matmul(out, g["ones"][:], A[:, bass.ds(t, 1), :].rearrange("p o d -> p (o d)"), start=start, stop=False)

                    if ready is not None:
                        pe.wait_ge(ready, 1)
                    for u in range(TG):
                        tile(u, u == 0)
                    with pe.Fori(1, NG - 1) as i:
                        if ready is not None:
                            pe.wait_ge(ready, i + 1)
                        for u in range(TG):
                            tile(i * TG + u, False)
                    if ready is not None:
                        pe.wait_ge(ready, NG)
                    for u in range(TG - 1):
                        tile((NG - 1) * TG + u, False)
                    nc.tensor.matmul(out, g["ones"][0:LAST, :], A[0:LAST, TILES - 1, :],
                                     start=False, stop=True).then_inc(summed, 1)
                column_sums(PM[:, 0:D], U)
                column_sums(PV[:, 0:D], SQ, squared)

            @block.scalar
            def _(act):
                def square(i):
                    wait_alone(act, centred, i + 1, stood)
                    nc.scalar.activation(SQ[:, bass.ds(i * TG, TG), :], U[:, bass.ds(i * TG, TG), :], ACT.Square).then_inc(squared, 1)
                with act.Fori(0, NG) as i:
                    square(i)

            @block.vector
            def _(dve):
                V = nc.vector
                n = [0]

                def then(ins):
                    n[0] += 1
                    ins.then_inc(stat, 1)
                    dve.wait_ge(stat, n[0])

                dve.wait_ge(summed, 1)
                then(V.tensor_scalar(mean[:], PM[:, 0:D], 1.0 / N, None, ALU.mult))
                with dve.Fori(0, NG) as i:
                    group = U[:, bass.ds(i * TG, TG), :]
                    V.tensor_tensor(group, group, per_feature(mean[:], TG), ALU.subtract).then_inc(centred, 1)
                dve.wait_ge(loaded, 32)
                dve.wait_ge(summed, 2)
                then(V.tensor_scalar(scl[:], PV[:, 0:D], 1.0 / N, BN_EPS, ALU.mult, ALU.add))
                dve.wait_ge(root, 1)
                then(V.tensor_tensor(scl[:], scl[:], gam[:], ALU.mult))
                dve.wait_ge(centred, NG)
                dve.wait_ge(squared, NG)
                then(V.tensor_tensor(U[:], U[:], per_feature(scl[:]), ALU.mult))
                then(V.tensor_tensor(U[:], U[:], per_feature(bet[:]), ALU.add))
                dve.wait_ge(residual, 1)
                then(V.scalar_tensor_tensor(g["X"][:], U[:], 0.0, g["X"][:], ALU.max, ALU.add))
        sem.clear()


class Count:

    def __init__(self, eng, sem, before):
        self.eng, self.sem, self.n = eng, sem, before

    def then(self, ins):
        ins.then_inc(self.sem, 1)
        self.n = self.n + 1
        self.eng.wait_ge(self.sem, self.n)


def gather_group(nc, pool, g, idx, ready, table, out_of, gathered, k, stood):
    pool.tensor_copy(idx, g["src_idx"][:, bass.ds(k * GROUP, GROUP)]).then_inc(ready, 1)
    wait_alone(pool, ready, k + 1, stood)
    for s in range(GROUP):
        pool.indirect_dma_start(out=out_of(s), out_offset=None, in_=table,
                                in_offset=bass.IndirectOffsetOnAxis(ap=idx[:, s:s + 1], axis=0)).then_inc(gathered, 16)


def onehot_rows(nc, g, loc, k):
    return (g["iota_row"][:].unsqueeze(1).to_broadcast([P, GROUP, P]),
            loc[:, bass.ds(k * GROUP, GROUP)].unsqueeze(2).to_broadcast([P, GROUP, P]))


class SoftmaxParts:

    def __init__(self, nc, g, ctx, name, heads, ACC, scaled, onehot_type=F32):
        self.nc, self.g, self.heads, self.ACC = nc, g, heads, ACC
        self.scaled = scaled
        self.changes = GROUP + len(scaled)

        def sb(n, shape, dt=F32):
            return ctx.enter_context(nc.sbuf_tensor(name + n, shape, dt))

        self.sem = sem = Semaphores(nc, ctx, name)
        self.idx = sb("idx", [P, 4, GROUP], I32)
        self.LR = sb("LR", [P, 2, SLOTS], BF16)
        self.MS = sb("MS", [heads, 2, SLOTS], BF16)
        self.ME = sb("ME", [heads, 2, SLOTS], BF16)
        self.LF = sb("LF", [heads, 2])
        self.ST = sb("ST", [P, 2, SLOTS], onehot_type)
        self.FW = sb("FW", [heads, 2, SLOTS])
        self.CM = sb("CM", [heads, SLOTS])
        self.cont = sb("cont", [heads, 1])
        self.drop = sb("drop", [heads, 1])
        self.fac = sb("fac", [heads, 1])
        self.OH = sb("OH", [heads, P])
        self.LOC = sb("LOC", [P, 4, GROUP])
        self.DG = sb("DG", [heads, heads + 1])
        self.rest = sb("rest", [P, 1])
        self.R = sb("R", [P, heads])
        self.ET = ctx.enter_context(nc.psum_tensor(name + "ET", [heads, SLOTS], F32))
        self.SB = ctx.enter_context(nc.psum_tensor(name + "SB", [P, 512], F32))
        self.OUT = ctx.enter_context(nc.psum_tensor(name + "OUT", [P, 3, 512], F32))
        self.RP = self.SB[:, 256:256 + heads + 1]
        self.idx_ready = sem("idx_ready")
        self.gathered = g["gathered"]
        self.base = g["rows_gathered"][:]
        self.locrow_in = [sem(f"locrow_in{b}") for b in range(2)]
        self.masks_in = [sem(f"masks_in{b}") for b in range(2)]
        self.start = sem("start")
        self.stood = sem("stood")
        self.st_done = sem("st_done")
        self.et_done = sem("et_done")
        self.cm_done = sem("cm_done")
        self.drop_done = sem("drop_done")
        self.fac_done = sem("fac_done")
        self.dg_done = sem("dg_done")
        self.scores, self.scores_done = self.ET, self.et_done
        self.r_done = sem("r_done")
        self.p_done = sem("p_done")
        self.mm_done = sem("mm_done")
        self.acc_done = sem("acc_done")
        self.maxima_step = sem("maxima_step")
        self.factor_step = sem("factor_step")
        self.loc_in = sem("loc_in")

    def gathers(self, pool, table, G, rows, used, per=1):
        def body(k, i, b):
            wait_alone(pool, used, per * (k - 3), self.stood)
            gather_group(self.nc, pool, self.g, self.idx[:, b, :], self.idx_ready, table[:, :],
                         lambda s: G[:, b, s, 0:rows], self.gathered[b], k, self.stood)
        in_groups_of_four(pool, body)

    def rows_in(self, sp):
        def locrow(k, c):
            sp.dma_start(self.LR[:, c, :], self.g["row_loc"][bass.ds(k * SLOTS, SLOTS)].partition_broadcast(P)).then_inc(self.locrow_in[c], 16)

        def body(k, i, b):
            c = b % 2
            wait(sp, self.st_done, k - 1)
            locrow(k, c)
            wait(sp, self.drop_done, k - 1)
            for t, row in ((self.MS, "row_start"), (self.ME, "row_end")):
                sp.dma_start(t[:, c, :], self.g[row][bass.ds(k * SLOTS, SLOTS)].partition_broadcast(self.heads)).then_inc(self.masks_in[c], 16)
        in_groups_of_four(sp, body)

    def prepare(self, dve):
        V = self.nc.vector
        V.memset(self.ACC[:], 0.0).then_inc(self.acc_done, 1)
        V.memset(self.FW[:, 1, SLOTS - 1:SLOTS], -BIG).then_inc(self.start, 1)
        V.memset(self.DG[:, self.heads:self.heads + 1], 1.0 / self.heads).then_inc(self.start, 1)
        self.node_slots(dve, 0, 0)
        self.node_slots(dve, 0, 1)
        dve.wait_ge(self.start, 2)

    def node_slots(self, dve, i, b):
        V, c = self.nc.vector, b % 2
        dve.wait_ge(self.locrow_in[c], 16 * (2 * i + b // 2 + 1))
        V.tensor_copy(self.LF[:, c:c + 1], self.LR[0:self.heads, c, 0:1])
        V.tensor_scalar(self.ST[:, c, :], self.LR[:, c, :], self.g["iota_col"][:], None, ALU.is_equal).then_inc(self.st_done, 1)

    def node_slots_ahead(self, dve, i, b):
        self.node_slots(dve, i + (b + 2) // 4, (b + 2) % 4)

    def running_maxima(self, dve, k, i, b):
        V, p = self.nc.vector, b % 2
        FW, CM, drop = self.FW, self.CM, self.drop
        dve.wait_ge(self.masks_in[p], 32 * (2 * i + b // 2 + 1))
        dve.wait_ge(self.scores_done, k + 1)
        V.tensor_tensor_scan(out=FW[:, p, :], data0=self.MS[:, p, :], data1=self.scores[:],
                             initial=FW[:, 1 - p, SLOTS - 1:SLOTS], op0=ALU.add, op1=ALU.max).then_inc(self.maxima_step, 1)
        dve.wait_ge(self.st_done, k + 1)
        V.tensor_scalar(self.OH[:], self.g["iota_row"][0:self.heads, :], self.LF[:, p:p + 1], None, ALU.is_equal)
        V.tensor_scalar(self.cont[:], self.MS[:, p, 0:1], -0.5, None, ALU.is_ge).then_inc(self.maxima_step, 1)
        dve.wait_ge(self.maxima_step, 3 * k + 2)
        V.tensor_tensor_scan(out=CM[:, ::-1], data0=self.ME[:, p, ::-1], data1=FW[:, p, ::-1],
                             initial=-BIG, op0=ALU.add, op1=ALU.max).then_inc(self.cm_done, 1)
        dve.wait_ge(self.cm_done, k + 1)
        V.tensor_tensor(drop[:], FW[:, 1 - p, SLOTS - 1:SLOTS], CM[:, 0:1], ALU.subtract).then_inc(self.maxima_step, 1)
        dve.wait_ge(self.maxima_step, 3 * k + 3)
        V.tensor_tensor(drop[:], drop[:], self.cont[:], ALU.mult).then_inc(self.drop_done, 1)

    def edge_nodes(self, k, b):
        self.nc.scalar.copy(self.LOC[:, b, :], self.g["loc"][:, bass.ds(k * GROUP, GROUP)]).then_inc(self.loc_in, 1)

    def factor(self, act, k):
        wait_alone(act, self.drop_done, k + 1, self.stood)
        self.nc.scalar.activation(self.fac[:], self.drop[:], ACT.Exp).then_inc(self.fac_done, 1)

    def factor_diagonal(self, dve, k):
        dve.wait_ge(self.fac_done, k + 1)
        h = self.heads
        self.nc.vector.tensor_scalar(self.DG[:, 0:h], self.g["eye"][0:h, 0:h], self.fac[:], None, ALU.mult).then_inc(self.dg_done, 1)

    def factor_of_nodes(self, pe, k):
        pe.wait_ge(self.dg_done, k + 1)
        self.nc.tensor.matmul(self.RP, self.OH[:], self.DG[:], start=True, stop=True).then_inc(self.r_done, 1)

    def read_factors(self, dve, k):
        V, h = self.nc.vector, self.heads
        dve.wait_ge(self.r_done, k + 1)
        V.tensor_scalar(self.rest[:], self.RP[:, h:h + 1], -1.0, 1.0, ALU.mult, ALU.add).then_inc(self.factor_step, 1)
        dve.wait_ge(self.factor_step, 2 * k + 1)
        V.tensor_scalar(self.R[:], self.RP[:, 0:h], self.rest[:], None, ALU.add).then_inc(self.factor_step, 1)

    def tiles_of(self, dve, k):
        if k is None:
            return None
        return load_tiles(self.nc, mybir.EngineType.DVE, self.g["tile_row"], k * GROUP, GROUP)

    def accumulate(self, dve, k, tiles, between=()):
        if k is None:
            for work in between:
                work()
        else:
            self.additions(dve, k, tiles, between)

    def additions(self, dve, k, tiles, between):
        V, ACC, R, h = self.nc.vector, self.ACC, self.R, self.heads
        done = self.changes * k + 1
        dve.wait_ge(self.factor_step, 2 * k + 2)
        dve.wait_ge(self.acc_done, done)
        for cols in self.scaled:
            rows = ACC[:, bass.ds(tiles[0], 1), cols].rearrange("p o c -> p (o c)")
            if h == 1:
                ins = V.tensor_scalar(rows, rows, R[:], None, ALU.mult)
            else:
                rows = rows.rearrange("p (h f) -> p h f", h=h)
                ins = V.tensor_tensor(rows, rows, R[:].unsqueeze(2).to_broadcast([P, h, rows.shape[2]]), ALU.mult)
            ins.then_inc(self.acc_done, 1)
        dve.wait_ge(self.mm_done, k + 1)
        AC = ACC.shape[2]
        for s, t in enumerate(tiles):
            dst = ACC[:, bass.ds(t, 1), :].rearrange("p o c -> p (o c)")
            dve.wait_ge(self.acc_done, done + len(self.scaled) + s)
            V.tensor_tensor(dst, dst, self.OUT[:, s // 3, (s % 3) * AC:(s % 3 + 1) * AC], ALU.add).then_inc(self.acc_done, 1)
            for work in between[s * len(between) // GROUP:(s + 1) * len(between) // GROUP]:
                work()

    def results_read(self, pe, k, last=GROUP - 1):
        wait(pe, self.acc_done, self.changes * k + 1 - (GROUP - 1 - last) if not is_first(k) else 0)

    def close(self, dve):
        dve.wait_ge(self.acc_done, self.changes * GROUPS + 1)

    def finish(self):
        self.sem.clear()
        for b in range(4):
            self.g["rows_gathered"][b] += 16 * GROUP * (GROUPS // 4)


def gat_pass(nc, g, table, destination, ACC):
    heads, hd, AC = HEADS, HF, ACC.shape[2]
    WC = D + heads
    with ExitStack() as ctx:
        def sb(n, shape, dt=F32):
            return ctx.enter_context(nc.sbuf_tensor("e0_" + n, shape, dt))

        parts = SoftmaxParts(nc, g, ctx, "e0_", heads, ACC, (slice(0, D), slice(D, WC)), BF16)
        sem = parts.sem
        G = sb("G", [P, 4, GROUP, WC])
        S = sb("S", [P, 2, GROUP, P])
        APART = sb("APART", [P, GROUP, P])
        Z = sb("Z", [P, GROUP, heads])
        exact = sb("exact", [P, TILES, heads])
        split = sb("split", [P, TILES, 3, heads], BF16)
        SC = sb("SC", [P, 2, GROUP, heads])
        DIF = sb("DIF", [P, GROUP, heads])
        RH = sb("RH", [P, 2, GROUP, AC])
        DP = ctx.enter_context(nc.psum_tensor("e0_DP", [P, 512], F32))
        dp_view = DP[:, 0:GROUP * 3 * heads].rearrange("p (s c h) -> p s c h", c=3, h=heads)
        stab = parts.SB[:, 0:GROUP * heads].rearrange("p (s h) -> p s h", h=heads)
        split_done = sem("split_done")
        dp_done = sem("dp_done")
        apart_done = sem("apart_done")
        summed = sem("summed")
        score = sem("score")
        has_done = sem("has_done")
        s_done = sem("s_done")
        stab_done = sem("stab_done")
        dif_done = sem("dif_done")
        rh_done = sem("rh_done")

        with nc.Block() as block:
            @block.gpsimd
            def _(pool):
                parts.gathers(pool, table, G, WC, rh_done, 4)

            @block.sync
            def _(sp):
                parts.rows_in(sp)

            @block.scalar
            def _(act):
                def weights(k, b):
                    wait_alone(act, dif_done, k + 1, parts.stood)
                    nc.scalar.activation(RH[:, b % 2, :, D:D + heads], DIF[:], ACT.Exp).then_inc(parts.p_done, 1)

                def onehots(k, b):
                    parts.edge_nodes(k, b)
                    wait_alone(act, parts.loc_in, k + 1, parts.stood)
                    wait_alone(act, s_done, k, parts.stood)
                    for s in range(GROUP):
                        ins = nc.scalar.activation(APART[:, s, :], g["iota_row"][:], ACT.Square,
                                                   bias=parts.LOC[:, b, s:s + 1], scale=-1.0)
                    ins.then_inc(apart_done, 1)
                    wait_alone(act, apart_done, k + 1, parts.stood)
                    wait_alone(act, parts.mm_done, k - 1, parts.stood)
                    nc.scalar.activation(S[:, b % 2], APART[:], ACT.Relu, bias=g["ones"][:, 0:1], scale=-1.0).then_inc(s_done, 1)

                def body(k, i, b):
                    if not is_first(k):
                        weights(k - 1, b + 3)
                    onehots(k, b)
                    parts.factor(act, k)
                in_groups_of_four(act, body)
                weights(GROUPS - 1, 3)

            @block.vector
            def _(dve):
                V = nc.vector
                c = Count(dve, split_done, 0)
                c.then(V.tensor_copy(split[:, :, 0, :], destination))
                c.then(V.tensor_tensor(exact[:], destination, split[:, :, 0, :], ALU.subtract))
                c.then(V.tensor_copy(split[:, :, 1, :], exact[:]))
                c.then(V.tensor_tensor(exact[:], exact[:], split[:, :, 1, :], ALU.subtract))
                c.then(V.tensor_copy(split[:, :, 2, :], exact[:]))
                parts.prepare(dve)

                def differences(k, b):
                    p = b % 2
                    dve.wait_ge(stab_done, k + 1)
                    V.tensor_tensor(DIF[:], SC[:, p], stab, ALU.subtract).then_inc(dif_done, 1)
                    V.tensor_scalar(RH[:, p, :, AC - 1:AC], g["loc_end"][:, bass.ds(k * GROUP, GROUP)].unsqueeze(2),
                                    0.0, None, ALU.is_ge).then_inc(has_done, 1)
                    dve.wait_ge(has_done, k + 1)
                    V.tensor_tensor(RH[:, p, :, WC:WC + heads], stab,
                                    RH[:, p, :, AC - 1:AC].to_broadcast([P, GROUP, heads]), ALU.mult)

                def weighted_rows(k, b, part):
                    if part == 0:
                        dve.wait_ge(parts.p_done, k + 1)
                    steps = slice(part * GROUP // 4, (part + 1) * GROUP // 4)
                    V.tensor_tensor(RH[:, b % 2, steps, 0:D].rearrange("p s (h f) -> p s h f", h=heads),
                                    G[:, b, steps, 0:D].rearrange("p s (h f) -> p s h f", h=heads),
                                    RH[:, b % 2, steps, D:D + heads].unsqueeze(3).to_broadcast([P, GROUP // 4, heads, hd]),
                                    ALU.mult).then_inc(rh_done, 1)

                def score_sums(k, i, b, part):
                    if part == 0:
                        dve.wait_ge(parts.gathered[b], parts.base[b] + 16 * GROUP * (i + 1))
                        dve.wait_ge(dp_done, k + 1)
                    else:
                        dve.wait_ge(summed, 3 * k + part)
                    V.tensor_tensor(Z[:], Z[:] if part else G[:, b, :, D:D + heads], dp_view[:, :, part, :],
                                    ALU.add).then_inc(summed, 1)

                def scores(k, b):
                    dve.wait_ge(summed, 3 * k + 3)
                    V.scalar_tensor_tensor(SC[:, b % 2], Z[:], SLOPE, Z[:], ALU.mult, ALU.max).then_inc(score, 1)

                def previous(k, b, between=()):
                    before = None if is_first(k) else k - 1
                    tiles = parts.tiles_of(dve, before)
                    differences(k, b)
                    parts.factor_diagonal(dve, k)
                    parts.accumulate(dve, before, tiles,
                                     [lambda part=part: weighted_rows(k, b, part) for part in range(4)] + list(between))
                    parts.read_factors(dve, k)

                def body(k, i, b):
                    between = []
                    if not is_last(k):
                        nxt = (k + 1, i + (b + 1) // 4, (b + 1) % 4)
                        between += [lambda part=part: score_sums(*nxt, part) for part in range(3)]
                        between.append(lambda: scores(k + 1, b + 1))
                    if is_first(k):
                        for work in between:
                            work()
                    else:
                        previous(k - 1, (b + 3) % 4, between)
                    parts.running_maxima(dve, k, i, b)
                    if not (isinstance(k, int) and k >= GROUPS - 2):
                        parts.node_slots_ahead(dve, i, b)

                for part in range(3):
                    score_sums(0, 0, 0, part)
                scores(0, 0)
                in_groups_of_four(dve, body)
                previous(GROUPS - 1, 3)
                parts.accumulate(dve, GROUPS - 1, parts.tiles_of(dve, GROUPS - 1))
                parts.close(dve)

            @block.tensor
            def _(pe):
                def destinations(k, b, tiles):
                    pe.wait_ge(parts.st_done, k + 1)
                    for s, t in enumerate(tiles):
                        ins = nc.tensor.matmul(dp_view[:, s], parts.ST[:, b % 2, s * P:(s + 1) * P],
                                               split[:, bass.ds(t, 1)].rearrange("p o c h -> p (o c h)"), start=True, stop=True)
                    ins.then_inc(dp_done, 1)

                def tiles_of(k):
                    return load_tiles(nc, mybir.EngineType.PE, g["tile_row"], k * GROUP, GROUP)

                def sums(k, b):
                    pe.wait_ge(s_done, k + 1)
                    for s in range(GROUP):
                        if s % 3 == 0:
                            last = min(s + 2, GROUP - 1)
                            pe.wait_ge(rh_done, 4 * k + last // 2 + 1)
                            parts.results_read(pe, k, last)
                        ins = nc.tensor.matmul(parts.OUT[:, s // 3, (s % 3) * AC:(s % 3 + 1) * AC], S[:, b % 2, s, :],
                                               RH[:, b % 2, s, :], start=True, stop=True)
                    ins.then_inc(parts.mm_done, 1)

                tiles = tiles_of(0)
                pe.wait_ge(split_done, 5)
                destinations(0, 0, tiles)

                def body(k, i, b):
                    if not is_last(k):
                        tiles = tiles_of(k + 1)
                    pe.wait_ge(score, k + 1)
                    for s in range(GROUP):
                        ins = nc.tensor.transpose(parts.ET[:, s * P:(s + 1) * P], SC[:, b % 2, s, :], g["eye"][:])
                    ins.then_inc(parts.et_done, 1)
                    if not is_last(k):
                        destinations(k + 1, b + 1, tiles)
                    if not is_first(k):
                        parts.factor_of_nodes(pe, k - 1)
                        sums(k - 1, b + 3)
                    wait_alone(pe, parts.cm_done, k + 1, parts.stood)
                    for s in range(GROUP):
                        ins = nc.tensor.transpose(stab[:, s, :], parts.CM[:, s * P:(s + 1) * P], g["eye"][0:heads, 0:heads])
                    ins.then_inc(stab_done, 1)
                in_groups_of_four(pe, body)
                parts.factor_of_nodes(pe, GROUPS - 1)
                sums(GROUPS - 1, 3)
        parts.finish()


def gatv2_pass(nc, g, table, destination, ACC, att_col):
    AC = D + 1
    with ExitStack() as ctx:
        def sb(n, shape, dt=F32):
            return ctx.enter_context(nc.sbuf_tensor("e3_" + n, shape, dt))

        parts = SoftmaxParts(nc, g, ctx, "e3_", 1, ACC, (slice(0, AC),))
        sem = parts.sem
        G = sb("G", [P, 4, GROUP, AC])
        XR = sb("XR", [P, GROUP, D])
        LZ = sb("LZ", [P, 2, SLOTS])
        ER = sb("ER", [1, SLOTS])
        SC = sb("SC", [P, GROUP])
        DIF = sb("DIF", [P, GROUP])
        W = sb("W", [P, 2, GROUP])
        S = sb("S", [P, 2, GROUP, P])
        ZT = ctx.enter_context(nc.psum_tensor("e3_ZT", [P, SLOTS], F32))
        turned_scores, turned_maxima = parts.SB[:, 0:GROUP], parts.SB[:, GROUP:2 * GROUP]
        xr_done = sem("xr_done")
        zt_done = sem("zt_done")
        sloped_done = sem("sloped_done")
        lz_done = sem("lz_done")
        er_done = sem("er_done")
        parts.scores, parts.scores_done = ER, er_done
        turned = sem("turned")
        sc_done = sem("sc_done")
        dif_done = sem("dif_done")
        s_done = sem("s_done")

        with nc.Block() as block:
            @block.gpsimd
            def _(pool):
                pool.memset(G[:, :, :, D:AC], 1.0).then_inc(parts.start, 1)
                parts.gathers(pool, table, G, D, parts.mm_done)

            @block.sync
            def _(sp):
                parts.rows_in(sp)

            @block.scalar
            def _(act):
                def stage(k, b):
                    tiles = load_tiles(nc, mybir.EngineType.Activation, g["tile_row"], k * GROUP, GROUP)
                    wait_alone(act, zt_done, 2 * k, parts.stood)
                    parts.edge_nodes(k, b)
                    for s, t in enumerate(tiles):
                        ins = nc.scalar.copy(XR[:, s, :], destination[:, bass.ds(t, 1), :].rearrange("p o c -> p (o c)"))
                    ins.then_inc(xr_done, 1)

                def weights(k, b):
                    wait_alone(act, dif_done, k + 1, parts.stood)
                    nc.scalar.activation(W[:, b % 2, :], DIF[:], ACT.Exp).then_inc(parts.p_done, 1)

                def score_row(k):
                    wait_alone(act, parts.et_done, k + 1, parts.stood)
                    nc.scalar.copy(ER[:], parts.ET[:]).then_inc(er_done, 1)

                def edge_scores(k):
                    wait_alone(act, turned, k + 1, parts.stood)
                    nc.scalar.copy(SC[:], turned_scores).then_inc(sc_done, 1)

                def sloped(k, b, half):
                    wait_alone(act, zt_done, 2 * k + half + 1, parts.stood)
                    cols = slice(half * SLOTS // 2, (half + 1) * SLOTS // 2)
                    nc.scalar.activation(LZ[:, b % 2, cols], ZT[:, cols], ACT.Copy, scale=SLOPE).then_inc(sloped_done, 1)

                stage(0, 0)
                sloped(0, 0, 0)
                sloped(0, 0, 1)

                def body(k, i, b):
                    if not is_first(k):
                        weights(k - 1, b + 3)
                    if not is_last(k):
                        stage(k + 1, (b + 1) % 4)
                    score_row(k)
                    if not is_last(k):
                        sloped(k + 1, b + 1, 0)
                        sloped(k + 1, b + 1, 1)
                    parts.factor(act, k)
                    edge_scores(k)
                in_groups_of_four(act, body)
                weights(GROUPS - 1, 3)

            @block.vector
            def _(dve):
                V = nc.vector
                parts.prepare(dve)

                def differences(k):
                    dve.wait_ge(sc_done, k + 1)
                    V.tensor_tensor(DIF[:], SC[:], turned_maxima, ALU.subtract).then_inc(dif_done, 1)

                def weighted_onehot(k, b, s):
                    if s == 0:
                        dve.wait_ge(parts.p_done, k + 1)
                    ins = V.tensor_scalar(S[:, b % 2, s, :], g["iota_row"][:], parts.LOC[:, b, s:s + 1], W[:, b % 2, s:s + 1],
                                          ALU.is_equal, ALU.mult)
                    if s == GROUP - 1:
                        ins.then_inc(s_done, 1)

                def leaky(k, b):
                    for half in range(2):
                        dve.wait_ge(sloped_done, 2 * k + half + 1)
                        cols = slice(half * SLOTS // 2, (half + 1) * SLOTS // 2)
                        ins = V.tensor_tensor(LZ[:, b % 2, cols], ZT[:, cols], LZ[:, b % 2, cols], ALU.max)
                    ins.then_inc(lz_done, 1)

                def previous(k, b):
                    before = None if is_first(k) else k - 1
                    tiles = parts.tiles_of(dve, before)
                    differences(k)
                    parts.factor_diagonal(dve, k)
                    parts.accumulate(dve, before, tiles, [lambda s=s: weighted_onehot(k, b, s) for s in range(GROUP)])
                    parts.read_factors(dve, k)

                def body(k, i, b):
                    if not is_first(k):
                        previous(k - 1, (b + 3) % 4)
                    parts.running_maxima(dve, k, i, b)
                    if not (isinstance(k, int) and k >= GROUPS - 2):
                        parts.node_slots_ahead(dve, i, b)
                    if not is_last(k):
                        leaky(k + 1, b + 1)

                leaky(0, 0)
                in_groups_of_four(dve, body)
                previous(GROUPS - 1, 3)
                parts.accumulate(dve, GROUPS - 1, parts.tiles_of(dve, GROUPS - 1))
                parts.close(dve)

            @block.tensor
            def _(pe):
                def rows(k, i, b, steps):
                    if steps[0] == 0:
                        pe.wait_ge(parts.st_done, k + 1)
                        pe.wait_ge(xr_done, k + 1)
                        pe.wait_ge(parts.gathered[b], parts.base[b] + 16 * GROUP * (i + 1))
                    for s in steps:
                        cols = slice(s * P, (s + 1) * P)
                        nc.tensor.matmul(ZT[:, cols], XR[:, s, :], parts.ST[:, b % 2, cols], start=True, stop=False)
                        ins = nc.tensor.matmul(ZT[:, cols], G[:, b, s, 0:D], g["eye"][:], start=False, stop=True)
                        if s % (GROUP // 2) == GROUP // 2 - 1:
                            ins.then_inc(zt_done, 1)

                def sums(k, b):
                    pe.wait_ge(s_done, k + 1)
                    parts.results_read(pe, k)
                    for s in range(GROUP):
                        ins = nc.tensor.matmul(parts.OUT[:, s // 3, (s % 3) * AC:(s % 3 + 1) * AC], S[:, b % 2, s, :],
                                               G[:, b, s, :], start=True, stop=True)
                    ins.then_inc(parts.mm_done, 1)

                pe.wait_ge(parts.start, 3)
                rows(0, 0, 0, range(GROUP))

                def body(k, i, b):
                    pe.wait_ge(lz_done, k + 1)
                    for h in range(SLOTS // 512):
                        cols = slice(h * 512, (h + 1) * 512)
                        ins = nc.tensor.matmul(parts.ET[:, cols], att_col, LZ[:, b % 2, cols], start=True, stop=True)
                    ins.then_inc(parts.et_done, 1)
                    if not is_first(k):
                        parts.factor_of_nodes(pe, k - 1)
                    if not is_last(k):
                        rows(k + 1, i + (b + 1) // 4, (b + 1) % 4, range(0, GROUP // 2))
                    if not is_first(k):
                        sums(k - 1, (b + 3) % 4)
                    if not is_last(k):
                        rows(k + 1, i + (b + 1) // 4, (b + 1) % 4, range(GROUP // 2, GROUP))
                    wait_alone(pe, parts.cm_done, k + 1, parts.stood)
                    for s in range(GROUP):
                        cols = slice(s * P, (s + 1) * P)
                        nc.tensor.transpose(turned_scores[:, s:s + 1], ER[:, cols], g["eye"][0:1, 0:1])
                        ins = nc.tensor.transpose(turned_maxima[:, s:s + 1], parts.CM[:, cols], g["eye"][0:1, 0:1])
                    ins.then_inc(turned, 1)

                in_groups_of_four(pe, body)
                parts.factor_of_nodes(pe, GROUPS - 1)
                sums(GROUPS - 1, 3)
        parts.finish()




def sum_pass(nc, g, table, ACC):
    name = "s_"
    AC = D + 1
    PER = 3
    with ExitStack() as ctx:
        sem = Semaphores(nc, ctx, name)

        idx = ctx.enter_context(nc.sbuf_tensor(name + "idx", [P, 2, GROUP], I32))
        G = ctx.enter_context(nc.sbuf_tensor(name + "G", [P, 2, GROUP, AC], F32))
        S = ctx.enter_context(nc.sbuf_tensor(name + "S", [P, 2, GROUP, P], F32))
        OUT = ctx.enter_context(nc.psum_tensor(name + "OUT", [P, 2, 3, 512], F32))
        idx_ready = sem("idx_ready")
        gathered = g["gathered"]
        base = g["rows_gathered"][:]
        stood = sem("p_stood")
        start = sem("start")
        s_done = sem("s_done")
        mm_done = sem("mm_done")
        acc_done = sem("acc_done")

        with nc.Block() as block:
            @block.gpsimd
            def _(pool):
                def body(k, i, b):
                    wait_alone(pool, mm_done, k - 1, stood)
                    gather_group(nc, pool, g, idx[:, b, :], idx_ready, table[:, :], lambda s: G[:, b, s, 0:D],
                                 gathered[b], k, stood)
                in_groups_of_two(pool, body)

            @block.vector
            def _(dve):
                V = nc.vector

                def add(k, b):
                    tiles = load_tiles(nc, mybir.EngineType.DVE, g["tile_row"], k * GROUP, GROUP)
                    dve.wait_ge(mm_done, k + 1)
                    for s, t in enumerate(tiles):
                        dst = ACC[:, bass.ds(t, 1), :].rearrange("p o c -> p (o c)")
                        dve.wait_ge(acc_done, k * GROUP + 1 + s)
                        V.tensor_tensor(dst, dst, OUT[:, b, s // PER, (s % PER) * AC:(s % PER + 1) * AC],
                                        ALU.add).then_inc(acc_done, 1)

                V.memset(G[:, :, :, D:AC], 1.0).then_inc(start, 1)
                V.memset(ACC[:], 0.0).then_inc(acc_done, 1)

                def body(k, i, b):
                    wait(dve, mm_done, k - 1)
                    V.tensor_tensor(S[:, b], *onehot_rows(nc, g, g["loc"], k), ALU.is_equal).then_inc(s_done, 1)
                    if not (isinstance(k, int) and k == 0):
                        add(k - 1, 1 - b)
                in_groups_of_two(dve, body)
                add(GROUPS - 1, 1)
                dve.wait_ge(acc_done, GROUP * GROUPS + 1)

            @block.tensor
            def _(pe):
                pe.wait_ge(start, 1)

                def body(k, i, b):
                    wait(pe, acc_done, 1 + GROUP * (k - 1) if not isinstance(k, int) or k >= 2 else 0)
                    pe.wait_ge(s_done, k + 1)
                    pe.wait_ge(gathered[b], base[b] + 16 * GROUP * (i + 1))
                    for s in range(GROUP):
                        ins = nc.tensor.matmul(OUT[:, b, s // PER, (s % PER) * AC:(s % PER + 1) * AC], S[:, b, s, :], G[:, b, s, :],
                                               start=True, stop=True)
                    ins.then_inc(mm_done, 1)
                in_groups_of_two(pe, body)
        sem.clear()
        for b in range(2):
            g["rows_gathered"][b] += 16 * GROUP * (GROUPS // 2)


def moments_pass(nc, g, table, ACC):
    name = "m_"
    Q = 4
    with ExitStack() as ctx:
        def sb(n, shape, dt=F32):
            return ctx.enter_context(nc.sbuf_tensor(name + n, shape, dt))

        sem = Semaphores(nc, ctx, name)

        idx = sb("idx", [P, Q, GROUP], I32)
        G = sb("G", [P, Q, GROUP, D])
        SQ = sb("SQ", [P, GROUP, D])
        S = sb("S", [P, 2, GROUP, P])
        SE = sb("SE", [P, 2, GROUP, P])
        MS = sb("MS", [P, 2, SLOTS], BF16)
        MN = sb("MN", [P, SLOTS], BF16)
        XT = sb("XT", [P, 2, 2, SLOTS])
        XB = sb("XB", [P, 2, 2, 2, D])
        GT = ctx.enter_context(nc.psum_tensor(name + "GT", [P, SLOTS], F32))
        BK = ctx.enter_context(nc.psum_tensor(name + "BK", [P, 2, 512], F32))
        OUT = ctx.enter_context(nc.psum_tensor(name + "OUT", [P, 4, 512], F32))
        idx_ready = sem("idx_ready")
        gathered = g["gathered"]
        base = g["rows_gathered"][:]
        masks_in = [sem(f"masks_in{b}") for b in range(2)]
        stood = sem("p_stood")
        start = sem("start")
        gt_done = sem("gt_done")
        mn_done = sem("mn_done")
        scanned = sem("scanned")
        s_done = sem("s_done")
        sq_done = sem("sq_done")
        bk_done = sem("bk_done")
        xb_done = sem("xb_done")
        step_done = sem("step_done")
        acc_done = sem("acc_done")

        with nc.Block() as block:
            @block.gpsimd
            def _(pool):
                def body(k, i, b):
                    wait_alone(pool, step_done, (k - Q + 1) * GROUP, stood)
                    gather_group(nc, pool, g, idx[:, b, :], idx_ready, table[:, :], lambda s: G[:, b, s, :],
                                 gathered[b], k, stood)
                in_groups_of_four(pool, body)

            @block.sync
            def _(sp):
                def body(k, i, b):
                    wait(sp, scanned, 2 * (k - 1))
                    sp.dma_start(MS[:, b % 2, :], g["row_start"][bass.ds(k * SLOTS, SLOTS)].partition_broadcast(P)).then_inc(masks_in[b % 2], 16)
                in_groups_of_four(sp, body)

            @block.scalar
            def _(act):
                def minus_masks(k, i, b):
                    wait_alone(act, masks_in[b % 2], 16 * (2 * i + b // 2 + 1), stood)
                    wait_alone(act, scanned, 2 * k - 1, stood)
                    nc.scalar.activation(MN[:], MS[:, b % 2, :], ACT.Copy, scale=-1.0).then_inc(mn_done, 1)

                def back(k, i, b):
                    wait_alone(act, gathered[b], base[b] + 16 * GROUP * (i + 1), stood)
                    wait_alone(act, step_done, k * GROUP, stood)
                    nc.scalar.activation(SQ[:], G[:, b], ACT.Square).then_inc(sq_done, 1)
                    for q in range(4):
                        wait_alone(act, bk_done, 4 * k + q + 1, stood)
                        if q >= 2:
                            wait_alone(act, step_done, k * GROUP + 2 * (q - 1), stood)
                        nc.scalar.copy(XB[:, q % 2], BK[:, q % 2, :].rearrange("p (s m d) -> p s m d", s=2, m=2)).then_inc(xb_done, 1)

                def body(k, i, b):
                    back(k, i, b)
                    if not (isinstance(k, int) and k >= GROUPS - 2):
                        minus_masks(k + 2, i + (b + 2) // 4, (b + 2) % 4)
                minus_masks(0, 0, 0)
                minus_masks(1, 0, 1)
                in_groups_of_four(act, body)

            @block.vector
            def _(dve):
                V = nc.vector

                def tiles_of(k):
                    return load_tiles(nc, mybir.EngineType.DVE, g["tile_row"], k * GROUP, GROUP)

                def add(k, tiles, between=()):
                    for s, t in enumerate(tiles):
                        dst = ACC[:, bass.ds(t, 1), :].rearrange("p o c -> p (o c)")
                        dve.wait_ge(step_done, k * GROUP + s + 1)
                        dve.wait_ge(acc_done, k * GROUP + s + 1)
                        V.tensor_tensor(dst, dst, OUT[:, s % 4, :], ALU.add).then_inc(acc_done, 1)
                        if s < len(between):
                            between[s]()

                def onehots(k, b, which, part):
                    n = GROUP // 4
                    out, loc = ((S, g["loc"]), (SE, g["loc_end"]))[which]
                    ins = V.tensor_tensor(out[:, b % 2, part * n:(part + 1) * n], g["iota_row"][:].unsqueeze(1).to_broadcast([P, n, P]),
                                          loc[:, bass.ds(k * GROUP + part * n, n)].unsqueeze(2).to_broadcast([P, n, P]),
                                          ALU.is_equal)
                    if which == 1 and part == 3:
                        ins.then_inc(s_done, 1)

                V.memset(ACC[:], 0.0).then_inc(acc_done, 1)
                V.memset(XT[:, 1, 0, SLOTS - 1:SLOTS], BIG).then_inc(start, 1)
                V.memset(XT[:, 1, 1, SLOTS - 1:SLOTS], -BIG).then_inc(start, 1)
                dve.wait_ge(start, 2)

                def body(k, i, b):
                    c = b % 2
                    if not is_first(k):
                        tiles = tiles_of(k - 1)
                    dve.wait_ge(masks_in[c], 16 * (2 * i + b // 2 + 1))
                    dve.wait_ge(gt_done, k + 1)
                    dve.wait_ge(mn_done, k + 1)
                    for m, (mask, op) in enumerate(((MN[:], ALU.min), (MS[:, c, :], ALU.max))):
                        wait(dve, scanned, 2 * k)
                        V.tensor_tensor_scan(out=XT[:, c, m, :], data0=mask, data1=GT[:],
                                             initial=XT[:, 1 - c, m, SLOTS - 1:SLOTS], op0=ALU.add, op1=op).then_inc(scanned, 1)
                    between = [lambda w=w, part=part: onehots(k, b, w, part) for part in range(4) for w in range(2)]
                    if is_first(k):
                        for work in between:
                            work()
                    else:
                        add(k - 1, tiles, between)
                in_groups_of_four(dve, body)
                add(GROUPS - 1, tiles_of(GROUPS - 1))
                dve.wait_ge(acc_done, GROUP * GROUPS + 1)

            @block.tensor
            def _(pe):
                def turn(k, i, b):
                    wait(pe, scanned, 2 * k)
                    pe.wait_ge(gathered[b], base[b] + 16 * GROUP * (i + 1))
                    for s in range(GROUP):
                        ins = nc.tensor.transpose(GT[:, s * P:(s + 1) * P], G[:, b, s, :], g["eye"][:])
                    ins.then_inc(gt_done, 1)

                def turn_back(k, c, q):
                    wait(pe, xb_done, 4 * k + q - 1)
                    for s in (2 * q, 2 * q + 1):
                        for m in range(2):
                            ins = nc.tensor.transpose(BK[:, q % 2, ((s % 2) * 2 + m) * D:((s % 2) * 2 + m + 1) * D],
                                                      XT[:, c, m, s * P:(s + 1) * P], g["eye"][:])
                    ins.then_inc(bk_done, 1)

                def sums(k, b):
                    c = b % 2
                    turn_back(k, c, 0)
                    turn_back(k, c, 1)
                    pe.wait_ge(s_done, k + 1)
                    pe.wait_ge(sq_done, k + 1)
                    for s in range(GROUP):
                        bank = s % 4
                        pe.wait_ge(xb_done, 4 * k + s // 2 + 1)
                        wait(pe, acc_done, k * GROUP + s - 2)
                        nc.tensor.matmul(OUT[:, bank, 0:D], S[:, c, s, :], G[:, b, s, :], start=True, stop=True)
                        nc.tensor.matmul(OUT[:, bank, D:3 * D], SE[:, c, s, :], XB[:, (s // 2) % 2, s % 2].rearrange("p m d -> p (m d)"), start=True, stop=True)
                        nc.tensor.matmul(OUT[:, bank, 3 * D:4 * D], S[:, c, s, :], SQ[:, s, :], start=True, stop=True).then_inc(step_done, 1)
                        if s in (1, 3):
                            turn_back(k, c, (s + 3) // 2)

                def body(k, i, b):
                    if not is_first(k):
                        sums(k - 1, (b - 1) % Q)
                    if not is_last(k):
                        turn(k + 1, i + (b + 1) // 4, (b + 1) % 4)
                turn(0, 0, 0)
                in_groups_of_four(pe, body)
                sums(GROUPS - 1, Q - 1)
        sem.clear()
        for b in range(Q):
            g["rows_gathered"][b] += 16 * GROUP * (GROUPS // Q)


def layer_gat(nc, g, w):
    with ExitStack() as ctx:
        sem = Semaphores(nc, ctx, "")
        H = ctx.enter_context(nc.sbuf_tensor("H0", [P, TILES, D], F32))
        XPA = ctx.enter_context(nc.sbuf_tensor("XPA", [P, TILES, D + 2 * HEADS], F32))
        with ExitStack() as c2:
            def sb(n, shape):
                return c2.enter_context(nc.sbuf_tensor("g0_" + n, shape, F32))
            W = sb("W", [D, D + 2 * HEADS])
            WT = sb("WT", [D, D])
            att = sb("att", [D, 2])
            first = sb("first", [P, HEADS])
            mask = sb("mask", [P, HEADS])
            AB = sb("AB", [P, 2 * HEADS])
            loaded = sem("g0_loaded")
            turned = sem("g0_turned")
            ab_done = sem("g0_ab_done")
            with nc.psum_tensor("g0_PW", [P, 2, 512], F32) as PW, nc.Block() as block:
                @block.sync
                def _(sp):
                    sp.dma_start(W[:, 0:D], w["L0_gnn_W"]).then_inc(loaded, 16)
                    sp.dma_start(att[:, 0:1], w["L0_gnn_att_src"].rearrange("h (f o) -> (h f) o", o=1)).then_inc(loaded, 16)
                    sp.dma_start(att[:, 1:2], w["L0_gnn_att_dst"].rearrange("h (f o) -> (h f) o", o=1)).then_inc(loaded, 16)

                @block.tensor
                def _(pe):
                    pe.wait_ge(loaded, 48)
                    nc.tensor.transpose(PW[:, 0, 0:D], W[:, 0:D], g["eye"][:]).then_inc(turned, 1)
                    pe.wait_ge(ab_done, 5)
                    nc.tensor.matmul(PW[:, 1, 0:2 * HEADS], WT[:], AB[:], start=True, stop=True).then_inc(turned, 1)

                @block.vector
                def _(dve):
                    V = nc.vector
                    c = Count(dve, ab_done, 0)
                    dve.wait_ge(loaded, 48)
                    dve.wait_ge(turned, 1)
                    c.then(V.tensor_copy(WT[:], PW[:, 0, 0:D]))
                    c.then(V.tensor_scalar(first[:], g["iota_row"][:, 0:HEADS], -float(HF), g["iota_col"][:], ALU.mult, ALU.add))
                    c.then(V.tensor_scalar(mask[:], first[:], 0.0, None, ALU.is_ge))
                    c.then(V.scalar_tensor_tensor(mask[:], first[:], float(HF), mask[:], ALU.is_lt, ALU.mult))
                    V.tensor_scalar(AB[:, 0:HEADS], mask[:], att[:, 0:1], None, ALU.mult)
                    c.then(V.tensor_scalar(AB[:, HEADS:2 * HEADS], mask[:], att[:, 1:2], None, ALU.mult))
                    dve.wait_ge(turned, 2)
                    c.then(V.tensor_copy(W[:, D:D + 2 * HEADS], PW[:, 1, 0:2 * HEADS]))
            norm_matmul(nc, g, "nm0", H, W[:], D + 2 * HEADS,
                        lambda i, t, m, ps, k: nc.vector.tensor_copy(XPA[:, t:t + m, :], ps),
                        stores=((g["tab0"], XPA[:, :, 0:D + HEADS], True),))
        ACC = ctx.enter_context(nc.sbuf_tensor("ACC0", [P, TILES, D + 2 * HEADS + 1], F32))
        gat_pass(nc, g, g["tab0"], XPA[:, :, D + HEADS:D + 2 * HEADS], ACC)
        U = ctx.enter_context(nc.sbuf_tensor("U0", [P, TILES, D], F32))
        with ExitStack() as c2:
            def sb(n, shape):
                return c2.enter_context(nc.sbuf_tensor("f0_" + n, shape, F32))
            bias = sb("bias", [P, D])
            none = sb("none", [P, TILES])
            es = sb("es", [P, TILES, HEADS])
            mx = sb("mx", [P, TILES, HEADS])
            r = sb("r", [P, TILES, HEADS])
            loaded = sem("f0_loaded")
            chain = sem("f0_chain")
            exps = sem("f0_exps")
            with nc.Block() as block:
                @block.sync
                def _(sp):
                    sp.dma_start(bias[:], w["L0_gnn_bias"].partition_broadcast(P)).then_inc(loaded, 16)

                @block.scalar
                def _(act):
                    act.wait_ge(chain, 8)
                    nc.scalar.activation(r[:], r[:], ACT.Exp).then_inc(exps, 1)
                    nc.scalar.activation(es[:], es[:], ACT.Exp).then_inc(exps, 1)

                @block.vector
                def _(dve):
                    V = nc.vector
                    c = Count(dve, chain, 0)
                    th = [P, TILES, HEADS]
                    den, big = ACC[:, :, D:D + HEADS], ACC[:, :, D + HEADS:D + 2 * HEADS]
                    c.then(V.tensor_scalar(none[:], ACC[:, :, D + 2 * HEADS], -1.0, BIG, ALU.add, ALU.mult))
                    c.then(V.tensor_tensor(r[:], big, none[:].unsqueeze(2).to_broadcast(th), ALU.add))
                    c.then(V.tensor_tensor(es[:], XPA[:, :, D:D + HEADS], XPA[:, :, D + HEADS:], ALU.add))
                    c.then(V.tensor_scalar(mx[:], es[:], SLOPE, None, ALU.mult))
                    c.then(V.tensor_tensor(es[:], es[:], mx[:], ALU.max))
                    c.then(V.tensor_tensor(mx[:], r[:], es[:], ALU.max))
                    c.then(V.tensor_tensor(r[:], r[:], mx[:], ALU.subtract))
                    c.then(V.tensor_tensor(es[:], es[:], mx[:], ALU.subtract))
                    dve.wait_ge(exps, 2)
                    c.then(V.tensor_tensor(mx[:], den, r[:], ALU.mult))
                    c.then(V.scalar_tensor_tensor(mx[:], mx[:], SOFTMAX_EPS, es[:], ALU.add, ALU.add))
                    c.then(V.reciprocal(mx[:], mx[:]))
                    c.then(V.tensor_tensor(r[:], r[:], mx[:], ALU.mult))
                    c.then(V.tensor_tensor(es[:], es[:], mx[:], ALU.mult))
                    for h in range(HEADS):
                        cols = slice(h * HF, (h + 1) * HF)
                        wide = [P, TILES, HF]
                        V.tensor_tensor(U[:, :, cols], ACC[:, :, cols], r[:, :, h:h + 1].to_broadcast(wide), ALU.mult)
                        ins = V.tensor_tensor(XPA[:, :, cols], XPA[:, :, cols], es[:, :, h:h + 1].to_broadcast(wide), ALU.mult)
                    c.then(ins)
                    c.then(V.tensor_tensor(U[:], U[:], XPA[:, :, 0:D], ALU.add))
                    dve.wait_ge(loaded, 16)
                    c.then(V.tensor_tensor(U[:], U[:], per_feature(bias[:]), ALU.add))
        batch_norm(nc, g, "bn0", U, H, w["L0_gnn_bn_gamma"], w["L0_gnn_bn_beta"])
        sem.clear()


def layer_gcn(nc, g, w):
    with ExitStack() as ctx:
        sem = Semaphores(nc, ctx, "")
        H = ctx.enter_context(nc.sbuf_tensor("H1", [P, TILES, D], F32))
        with ExitStack() as c2:
            T = c2.enter_context(nc.sbuf_tensor("T1", [P, TILES, D], F32))

            def by_out_degree(i):
                tiles = slice(i * TG, (i + 1) * TG)
                return nc.vector.tensor_tensor(T[:, tiles, :], H[:, tiles, :],
                                               g["rs_out"][:, tiles].unsqueeze(2).to_broadcast([P, TG, D]), ALU.mult)

            norm_matmul(nc, g, "ln1", H, None, D, by_out_degree, stores=((g["tab1"], T[:], True),))
        ACC = ctx.enter_context(nc.sbuf_tensor("ACC1", [P, TILES, D + 1], F32))
        sum_pass(nc, g, g["tab1"], ACC)
        U = ctx.enter_context(nc.sbuf_tensor("U1", [P, TILES, D], F32))
        W = ctx.enter_context(nc.sbuf_tensor("W1", [D, D], F32))
        bias = ctx.enter_context(nc.sbuf_tensor("b1", [P, D], F32))
        rs_in = ctx.enter_context(nc.sbuf_tensor("rs_in", [P, TILES], F32))
        chain = sem("chain1")
        with nc.Block() as block:
            @block.gpsimd
            def _(pool):
                pool.wait_ge(chain, 2)
                pool.tensor_tensor(rs_in[:], rs_in[:], g["mhalf"][:, 0:TILES], ALU.pow).then_inc(chain, 1)

            @block.vector
            def _(dve):
                V = nc.vector
                c = Count(dve, chain, 0)
                c.then(V.tensor_copy(g["cnt"][:], ACC[:, :, D]))
                c.then(V.tensor_scalar(rs_in[:], ACC[:, :, D], 1.0, None, ALU.max))
                dve.wait_ge(chain, 3)
                c.n = 3
                c.then(V.tensor_tensor(ACC[:, :, 0:D], ACC[:, :, 0:D], per_tile(rs_in[:]), ALU.mult))
        node_matmul(nc, g, "nm1", ACC[:, :, 0:D], W[:], D,
                    lambda dve, t, m, ps, i, k: nc.vector.tensor_tensor(U[:, bass.ds(t, m), :], ps, per_feature(bias[:], m), ALU.add),
                    loads=((W[:], w["L1_gnn_W"]), (bias[:], w["L1_gnn_b"].partition_broadcast(P))))
        batch_norm(nc, g, "bn1", U, H, w["L1_gnn_gamma"], w["L1_gnn_beta"])
        sem.clear()


def layer_pna(nc, g, w):
    with ExitStack() as ctx:
        sem = Semaphores(nc, ctx, "")
        with ExitStack() as c2:
            H = c2.enter_context(nc.sbuf_tensor("H2", [P, TILES, D], F32))
            B = c2.enter_context(nc.sbuf_tensor("B2", [P, TILES, D], F32))
            W = c2.enter_context(nc.sbuf_tensor("W2s", [D, D], F32))
            norm_matmul(nc, g, "nm2", H, W[:], D,
                        lambda i, t, m, ps, k: nc.vector.tensor_copy(B[:, t:t + m, :], ps),
                        loads=((W[:], w["L2_gnn_W_pre"][D:2 * D, :]),),
                        stores=((g["h2"], H[:], False), (g["tab2"], B[:], True)))
        ACC = ctx.enter_context(nc.sbuf_tensor("ACC2", [P, TILES, 4 * D], F32))
        moments_pass(nc, g, g["tab2"], ACC)
        mean, low, high, sq = (ACC[:, :, i * D:(i + 1) * D] for i in range(4))
        H = ctx.enter_context(nc.sbuf_tensor("H2b", [P, TILES, D], F32))
        s1 = ctx.enter_context(nc.sbuf_tensor("s1", [P, TILES], F32))
        s2 = ctx.enter_context(nc.sbuf_tensor("s2", [P, TILES], F32))
        has = ctx.enter_context(nc.sbuf_tensor("has", [P, TILES], F32))
        with ExitStack() as c2:
            T = c2.enter_context(nc.sbuf_tensor("T2", [P, TILES, D], F32))
            rd = c2.enter_context(nc.sbuf_tensor("rd", [P, TILES], F32))
            W = c2.enter_context(nc.sbuf_tensor("W2d", [D, D], F32))
            bias = c2.enter_context(nc.sbuf_tensor("b2", [P, D], F32))
            TAS = c2.enter_context(nc.sbuf_tensor("TA", [P, 2, 4, D], F32))
            chain = sem("chain2")
            logs = sem("logs2")
            h_in = sem("h_in2")
            evac = sem("evac2")
            with nc.Block() as block:
                @block.sync
                def _(sp):
                    sp.dma_start(H[:], g["h2"].rearrange("(t p) d -> p t d", p=P)).then_inc(h_in, 16)

                @block.scalar
                def _(act):
                    act.wait_ge(chain, 1)
                    nc.scalar.activation(s2[:], rd[:], ACT.Ln, bias=g["ones"][:, 0:1]).then_inc(logs, 1)
                    act.wait_ge(chain, 4)
                    nc.scalar.activation(T[:], mean, ACT.Square).then_inc(logs, 1)
                    act.wait_ge(chain, 9)
                    nc.scalar.activation(sq, sq, ACT.Sqrt).then_inc(logs, 1)
                    act.wait_ge(logs, 3)

                @block.vector
                def _(dve):
                    V = nc.vector
                    c = Count(dve, chain, 0)
                    c.then(V.tensor_scalar(rd[:], g["cnt"][:], 1.0, None, ALU.max))
                    c.then(V.tensor_scalar(has[:], g["cnt"][:], 0.0, None, ALU.is_gt))
                    dve.wait_ge(logs, 1)
                    c.then(V.reciprocal(rd[:], rd[:]))
                    c.then(V.tensor_tensor(mean, mean, per_tile(rd[:]), ALU.mult))
                    c.then(V.tensor_scalar(s1[:], s2[:], 1.0 / AVG_LOG, None, ALU.mult))
                    c.then(V.reciprocal(s2[:], s1[:]))
                    c.then(V.tensor_tensor(sq, sq, per_tile(rd[:]), ALU.mult))
                    dve.wait_ge(logs, 2)
                    c.then(V.tensor_tensor(sq, sq, T[:], ALU.subtract))
                    c.then(V.tensor_scalar(sq, sq, 0.0, STD_EPS, ALU.max, ALU.add))
                    dve.wait_ge(h_in, 16)

            def own_part(dve, t, m, ps, i, k):
                V = nc.vector
                TA = TAS[:, k]
                c = Count(dve, evac, 2 * (2 * i + k))
                c.then(V.tensor_tensor(TA[:, 0:m, :], ps, per_feature(bias[:], m), ALU.add))
                c.then(V.tensor_tensor(TA[:, 0:m, :], TA[:, 0:m, :], has[:, bass.ds(t, m)].unsqueeze(2).to_broadcast([P, m, D]), ALU.mult))
                for part in (mean, low, high):
                    dst = part[:, bass.ds(t, m), :]
                    ins = V.tensor_tensor(dst, dst, TA[:, 0:m, :], ALU.add)
                return ins

            node_matmul(nc, g, "nm2b", H, W[:], D, own_part,
                        loads=((W[:], w["L2_gnn_W_pre"][0:D, :]), (bias[:], w["L2_gnn_b_pre"].partition_broadcast(P))))
        post_matmul(nc, g, w, ACC, H, s1, s2, mean)
        batch_norm(nc, g, "bn2", mean, H, w["L2_gnn_gamma"], w["L2_gnn_beta"])
        sem.clear()


def post_matmul(nc, g, w, ACC, H, s1, s2, U):
    PARTS = 13
    with ExitStack() as ctx:
        def sb(n, shape):
            return ctx.enter_context(nc.sbuf_tensor("p_" + n, shape, F32))

        sem = Semaphores(nc, ctx, "")

        WF = sb("WF", [P, PARTS, D])
        BIAS = sb("BIAS", [P, D])
        with ExitStack() as c2:
            WP = c2.enter_context(nc.sbuf_tensor("p_WP", [P, PARTS, D], F32))
            WL = c2.enter_context(nc.sbuf_tensor("p_WL", [P, D], F32))
            WPT = c2.enter_context(nc.sbuf_tensor("p_WPT", [P, 2, P], F32))
            PT = c2.enter_context(nc.psum_tensor("p_PT", [P, 2, 512], F32))
            PF = c2.enter_context(nc.psum_tensor("p_PF", [P, 2, 512], F32))
            bp = c2.enter_context(nc.sbuf_tensor("p_bp", [P, 1], F32))
            bl = c2.enter_context(nc.sbuf_tensor("p_bl", [P, D], F32))
            bpr = c2.enter_context(nc.sbuf_tensor("p_bpr", [P, P], F32))
            loaded = sem("p_loaded")
            turned = sem("p_turned")
            turned_in = sem("p_turned_in")
            fused = sem("p_fused")
            fused_in = sem("p_fused_in")
            bias_rep = sem("p_bias_rep")
            with nc.Block() as block:
                @block.sync
                def _(sp):
                    sp.dma_start(WP[:], w["L2_gnn_W_post"].rearrange("(k p) d -> p k d", p=P)).then_inc(loaded, 16)
                    sp.dma_start(WL[:], w["L2_gnn_W_lin"]).then_inc(loaded, 16)
                    sp.dma_start(bp[:], w["L2_gnn_b_post"].unsqueeze(1)).then_inc(loaded, 16)
                    sp.dma_start(bl[:], w["L2_gnn_b_lin"].partition_broadcast(P)).then_inc(loaded, 16)

                @block.tensor
                def _(pe):
                    pe.wait_ge(loaded, 64)
                    for k in range(PARTS + 1):
                        if k < PARTS:
                            wait(pe, turned_in, k - 1)
                            nc.tensor.transpose(PT[:, k % 2, 0:P], WP[:, k, :], g["eye"][:]).then_inc(turned, 1)
                        if k >= 1:
                            pe.wait_ge(turned_in, k)
                            wait(pe, fused_in, k - 2)
                            nc.tensor.matmul(PF[:, (k - 1) % 2, 0:D], WPT[:, (k - 1) % 2, :], WL[:], start=True, stop=True).then_inc(fused, 1)
                    pe.wait_ge(bias_rep, 1)
                    pe.wait_ge(fused_in, PARTS)
                    nc.tensor.matmul(PF[:, 0, 0:D], bpr[:], WL[:], start=True, stop=True).then_inc(fused, 1)

                @block.scalar
                def _(act):
                    for k in range(PARTS):
                        act.wait_ge(turned, k + 1)
                        wait(act, fused, k - 1)
                        nc.scalar.copy(WPT[:, k % 2, :], PT[:, k % 2, 0:P]).then_inc(turned_in, 1)

                @block.vector
                def _(dve):
                    V = nc.vector
                    dve.wait_ge(loaded, 64)
                    V.tensor_scalar(bpr[:], g["ones"][:], bp[:], None, ALU.mult).then_inc(bias_rep, 1)
                    for k in range(PARTS):
                        dve.wait_ge(fused, k + 1)
                        V.tensor_copy(WF[:, k, :], PF[:, k % 2, 0:D]).then_inc(fused_in, 1)
                    dve.wait_ge(fused, PARTS + 1)
                    V.tensor_tensor(BIAS[:], PF[:, 0, 0:D], bl[:], ALU.add).then_inc(fused_in, 1)
                    dve.wait_ge(fused_in, PARTS + 1)
        SG = sb("SG", [P, 2, 5, D])
        HT = sb("HT", [P, 2, 5, P])
        T = sb("T", [P, 2, D])
        TP = ctx.enter_context(nc.psum_tensor("p_TP", [P, 2, 2, 512], F32))
        OP = ctx.enter_context(nc.psum_tensor("p_OP", [P, 2, 512], F32))
        staged = sem("p_staged")
        stood = sem("p_stood")
        turned = sem("p_turned2")
        ht_in = sem("p_ht_in")
        product = sem("p_product")
        chain = sem("p_chain")

        def in_pairs(eng, body):
            body(0, 0)
            body(1, 1)
            with eng.Fori(1, TILES // 2) as i:
                body(2 * i, 0)
                body(2 * i + 1, 1)
            body(TILES - 1, 0)

        with nc.Block() as block:
            @block.gpsimd
            def _(pool):
                def body(t, b):
                    wait_alone(pool, turned, t - 1, stood)
                    pool.tensor_copy(SG[:, b, 0:4, :], ACC[:, bass.ds(t, 1), :].rearrange("p o (a d) -> p (o a) d", a=4))
                    pool.tensor_copy(SG[:, b, 4:5, :], H[:, bass.ds(t, 1), :]).then_inc(staged, 1)
                in_pairs(pool, body)

            @block.tensor
            def _(pe):
                def turn(t, b):
                    pe.wait_ge(staged, t + 1)
                    wait(pe, ht_in, t - 1)
                    for a in range(5):
                        ins = nc.tensor.transpose(TP[:, b, a // 4, (a % 4) * P:(a % 4 + 1) * P], SG[:, b, a, :], g["eye"][:])
                    ins.then_inc(turned, 1)

                def multiply(t, b):
                    pe.wait_ge(ht_in, t + 1)
                    wait(pe, chain, 3 * (t - 1))
                    for a in range(4):
                        nc.tensor.matmul(OP[:, b, 0:3 * D].rearrange("p (r d) -> p r d", r=3), HT[:, b, a, :],
                                         WF[:, 1 + a:PARTS:4, :], start=(a == 0), stop=False)
                    nc.tensor.matmul(OP[:, b, 0:D], HT[:, b, 4, :], WF[:, 0, :], start=False, stop=True).then_inc(product, 1)

                def body(t, b):
                    turn(t, b)
                    if not (isinstance(t, int) and t == 0):
                        multiply(t - 1, 1 - b)
                in_pairs(pe, body)
                multiply(TILES - 1, 0)

            @block.scalar
            def _(act):
                def body(t, b):
                    wait_alone(act, turned, t + 1, stood)
                    wait_alone(act, product, t - 1, stood)
                    nc.scalar.copy(HT[:, b, 0:4, :], TP[:, b, 0, :].rearrange("p (a n) -> p a n", a=4))
                    nc.scalar.copy(HT[:, b, 4, :], TP[:, b, 1, 0:P]).then_inc(ht_in, 1)
                in_pairs(act, body)

            @block.vector
            def _(dve):
                V = nc.vector

                def body(t, b):
                    c = Count(dve, chain, 3 * t)
                    dve.wait_ge(product, t + 1)
                    c.then(V.tensor_tensor(T[:, b], OP[:, b, 0:D], BIAS[:], ALU.add))
                    c.then(V.scalar_tensor_tensor(T[:, b], OP[:, b, D:2 * D], s1[:, bass.ds(t, 1)], T[:, b], ALU.mult, ALU.add))
                    c.then(V.scalar_tensor_tensor(U[:, bass.ds(t, 1), :].rearrange("p o d -> p (o d)"), OP[:, b, 2 * D:3 * D],
                                                  s2[:, bass.ds(t, 1)], T[:, b], ALU.mult, ALU.add))
                in_pairs(dve, body)
        sem.clear()


def layer_gatv2(nc, g, w, out):
    with ExitStack() as ctx:
        sem = Semaphores(nc, ctx, "")
        XLR = ctx.enter_context(nc.sbuf_tensor("XLR", [P, TILES, 2 * D], F32))
        with ExitStack() as c2:
            H = c2.enter_context(nc.sbuf_tensor("H3", [P, TILES, D], F32))
            W = c2.enter_context(nc.sbuf_tensor("W3", [D, 2 * D], F32))
            bias = c2.enter_context(nc.sbuf_tensor("b3", [P, 2 * D], F32))
            norm_matmul(nc, g, "nm3", H, W[:], 2 * D,
                        lambda i, t, m, ps, k: nc.vector.tensor_tensor(XLR[:, t:t + m, :], ps, per_feature(bias[:], m), ALU.add),
                        stores=((g["tab3"], XLR[:, :, 0:D], True),),
                        loads=((W[:, 0:D], w["L3_gnn_W_l"]), (W[:, D:2 * D], w["L3_gnn_W_r"]),
                               (bias[:, 0:D], w["L3_gnn_b_l"].partition_broadcast(P)),
                               (bias[:, D:2 * D], w["L3_gnn_b_r"].partition_broadcast(P))))
        att = ctx.enter_context(nc.sbuf_tensor("att3", [D, 1], F32))
        bias = ctx.enter_context(nc.sbuf_tensor("bias3", [P, D], F32))
        loaded = sem("loaded3")
        with nc.Block() as block:
            @block.sync
            def _(sp):
                sp.dma_start(att[:], w["L3_gnn_att"].unsqueeze(1)).then_inc(loaded, 16)
                sp.dma_start(bias[:], w["L3_gnn_bias"].partition_broadcast(P)).then_inc(loaded, 16)
                sp.wait_ge(loaded, 32)
        ACC = ctx.enter_context(nc.sbuf_tensor("ACC3", [P, TILES, D + 1], F32))
        gatv2_pass(nc, g, g["tab3"], XLR[:, :, D:2 * D], ACC, att[:])
        rd = ctx.enter_context(nc.sbuf_tensor("rd3", [P, TILES], F32))
        chain = sem("chain3")
        stored = sem("out_stored")
        with nc.Block() as block:
            @block.vector
            def _(dve):
                V = nc.vector
                c = Count(dve, chain, 0)
                rows = ACC[:, :, 0:D]
                c.then(V.tensor_scalar(rd[:], ACC[:, :, D], SOFTMAX_EPS, None, ALU.add))
                c.then(V.reciprocal(rd[:], rd[:]))
                c.then(V.tensor_tensor(rows, rows, per_tile(rd[:]), ALU.mult))
                c.then(V.tensor_tensor(rows, rows, per_feature(bias[:]), ALU.add))
                c.then(V.scalar_tensor_tensor(g["X"][:], rows, 0.0, g["X"][:], ALU.max, ALU.add))

            @block.sync
            def _(sp):
                sp.wait_ge(chain, 5)
                whole = (TILES - 1) * P
                sp.dma_start(out[0:whole, :].rearrange("(t p) d -> p t d", p=P), g["X"][:, 0:TILES - 1, :]).then_inc(stored, 16)
                sp.dma_start(out[whole:N, :], g["X"][0:LAST, TILES - 1, :]).then_inc(stored, 16)
                sp.wait_ge(stored, 32)


def gnn_kernel(nc, w, out):
    with ExitStack() as ctx:
        g = whole_program_tensors(nc, ctx)
        build_steps(nc, g, w["src"], w["dst"])
        with ExitStack() as c2:
            sem = Semaphores(nc, c2, "")
            x_in = sem("x_in")
            padded = sem("padded")
            with nc.Block() as block:
                @block.gpsimd
                def _(pool):
                    pool.memset(g["X"][:, TILES - 1, :], 0.0).then_inc(padded, 1)

                @block.sync
                def _(sp):
                    whole = (TILES - 1) * P
                    sp.dma_start(g["X"][:, 0:TILES - 1, :], w["x"][0:whole, :].rearrange("(t p) d -> p t d", p=P)).then_inc(x_in, 16)
                    sp.wait_ge(padded, 1)
                    sp.dma_start(g["X"][0:LAST, TILES - 1, :], w["x"][whole:N, :]).then_inc(x_in, 16)
                    sp.wait_ge(x_in, 32)
            sem.clear()
        layer_gat(nc, g, w)
        layer_gcn(nc, g, w)
        layer_pna(nc, g, w)
        layer_gatv2(nc, g, w, out)


_INS = ['x', 'src', 'dst', 'L0_gnn_W', 'L0_gnn_att_src', 'L0_gnn_att_dst', 'L0_gnn_bias', 'L0_gnn_bn_gamma',
        'L0_gnn_bn_beta', 'L1_gnn_W', 'L1_gnn_b', 'L1_gnn_gamma', 'L1_gnn_beta', 'L2_gnn_W_pre', 'L2_gnn_b_pre',
        'L2_gnn_W_post', 'L2_gnn_b_post', 'L2_gnn_W_lin', 'L2_gnn_b_lin', 'L2_gnn_gamma', 'L2_gnn_beta',
        'L3_gnn_W_l', 'L3_gnn_b_l', 'L3_gnn_W_r', 'L3_gnn_b_r', 'L3_gnn_att', 'L3_gnn_bias']


def kernel(**inputs):
    import numpy as _np
    import concourse.bacc as _bacc
    from concourse.bass_utils import run_bass_kernel_spmd as _run

    nc = _bacc.Bacc("TRN2", target_bir_lowering=False, num_devices=1)
    arrays, args = {}, {}
    for name in _INS:
        a = _np.ascontiguousarray(inputs[name])
        arrays[f"in_{name}_dram"] = a
        args[name] = nc.dram_tensor(f"in_{name}_dram", a.shape, mybir.dt.from_np(a.dtype), kind="ExternalInput").ap()
    out = nc.dram_tensor("out_dram", (N, D), F32, kind="ExternalOutput").ap()
    gnn_kernel(nc, args, out)
    r = _run(nc, [arrays], core_ids=[0])
    return r.results[0]["out_dram"]
```
